# Optimizing a Trainium2 kernel written in Bass

```python
import numpy as np
import jax
import jax.numpy as jnp

def _softmax(x, axis=-1):
    return jax.nn.softmax(x, axis=axis)

def _gelu(x):
    return jax.nn.gelu(x, approximate=True)

def _silu(x):
    return jax.nn.silu(x)

def _sigmoid(x):
    return jax.nn.sigmoid(x)

def _layernorm(x, axis=-1, eps=1e-05):
    m = jnp.mean(x, axis=axis, keepdims=True)
    v = jnp.var(x, axis=axis, keepdims=True)
    return (x - m) / jnp.sqrt(v + eps)

def _scatter_add(tgt, idx, src, axis=0):
    return tgt.at[idx].add(src)

def _segment_sum(src, seg, n):
    return jax.ops.segment_sum(src, seg, n)
kernel_name = 'mk_pixart_seq_d2_seqx_r8_73e909'

def setup_inputs(seed: int=0):
    np.random.seed(seed)
    _w = jnp.asarray

    def _rec_inputs():
        import jax
        import jax.numpy as jnp
        _rk = jax.random.key(seed)
        x = -0.0002928 + 1 * jax.random.normal(jax.random.fold_in(_rk, 1), (2, 512, 128), jnp.float32)
        _lenS = 512 - jax.random.randint(jax.random.fold_in(_rk, 7), (2,), 0, max(1, 512 // 4) + 1, jnp.int32)
        _lenS2 = 77 - jax.random.randint(jax.random.fold_in(_rk, 8), (2,), 0, max(1, 77 // 4) + 1, jnp.int32)
        _ctx_1024P = jax.random.normal(jax.random.fold_in(_rk, 11), (2, 16, 128), jnp.float32)
        _ctx_1024c = jax.random.dirichlet(jax.random.fold_in(_rk, 511), 0.3 * jnp.ones((16,), jnp.float32), (2, 77))
        _ctx_1024t = jnp.einsum('bsk,bkd->bsd', _ctx_1024c, _ctx_1024P)
        _ctx_1024t = _ctx_1024t * jax.lax.rsqrt(jnp.mean(jnp.square(_ctx_1024t)) + 1e-12) * 0.953939
        ctx_1024 = -1.39393e-06 + 0.999914 * (_ctx_1024t + 0.3 * jax.random.normal(jax.random.fold_in(_rk, 611), (2, 77, 128), jnp.float32))
        cond_1024 = 0.00786388 + 1.0143 * jax.random.normal(jax.random.fold_in(_rk, 12), (2, 128), jnp.float32)
        return (x, ctx_1024, cond_1024)
    x, ctx_1024, cond_1024 = _rec_inputs()

    def _L0_xcond_setup():
        import jax, jax.numpy as jnp
        import numpy as np
        D = 128
        H = 16
        DH = D // H
        DFF = 512
        B = 2
        L = 256
        EPS = 1e-05

        def layer_norm(x, g, b):
            mu = jnp.mean(x, axis=-1, keepdims=True)
            var = jnp.mean(jnp.square(x - mu), axis=-1, keepdims=True)
            return (x - mu) * jax.lax.rsqrt(var + EPS) * g + b

        def ada_ln(x, t_emb, ln_g, ln_b, aff_w, aff_b):
            normed = layer_norm(x, ln_g, ln_b)
            affine = t_emb @ aff_w + aff_b
            gamma, beta = jnp.split(affine, 2, axis=-1)
            return gamma[:, None, :] * normed + beta[:, None, :]

        def mha(q_in, k_in, v_in, qw, qb, kw, kb, vw, vb, ow, ob):
            Bq, Lq, _ = q_in.shape
            Lk = k_in.shape[1]
            Q = (q_in @ qw + qb).reshape(Bq, Lq, H, DH)
            K = (k_in @ kw + kb).reshape(Bq, Lk, H, DH)
            V = (v_in @ vw + vb).reshape(Bq, Lk, H, DH)
            scores = jnp.einsum('bqhd,bkhd->bhqk', Q, K) / np.sqrt(DH).astype(np.float32)
            attn = jax.nn.softmax(scores, axis=-1)
            out = jnp.einsum('bhqk,bkhd->bqhd', attn, V).reshape(Bq, Lq, D)
            return out @ ow + ob
        key = jax.random.key(seed)
        ks = jax.random.split(key, 32)
        s = lambda k, shape, scale=0.02: jax.random.normal(k, shape, dtype=jnp.float32) * scale
        inp = {'x': jax.random.normal(ks[0], (B, L, D), dtype=jnp.float32), 'u': jax.random.normal(ks[1], (B, L, D), dtype=jnp.float32), 't_emb': jax.random.normal(ks[2], (B, D), dtype=jnp.float32), 'ln1_g': jnp.ones((D,), jnp.float32), 'ln1_b': jnp.zeros((D,), jnp.float32), 'aff1_w': s(ks[3], (D, 2 * D)), 'aff1_b': jnp.zeros((2 * D,), jnp.float32), 'ln2_g': jnp.ones((D,), jnp.float32), 'ln2_b': jnp.zeros((D,), jnp.float32), 'aff2_w': s(ks[4], (D, 2 * D)), 'aff2_b': jnp.zeros((2 * D,), jnp.float32), 'sa_qw': s(ks[5], (D, D)), 'sa_qb': jnp.zeros((D,), jnp.float32), 'sa_kw': s(ks[6], (D, D)), 'sa_kb': jnp.zeros((D,), jnp.float32), 'sa_vw': s(ks[7], (D, D)), 'sa_vb': jnp.zeros((D,), jnp.float32), 'sa_ow': s(ks[8], (D, D)), 'sa_ob': jnp.zeros((D,), jnp.float32), 'ca_qw': s(ks[9], (D, D)), 'ca_qb': jnp.zeros((D,), jnp.float32), 'ca_kw': s(ks[10], (D, D)), 'ca_kb': jnp.zeros((D,), jnp.float32), 'ca_vw': s(ks[11], (D, D)), 'ca_vb': jnp.zeros((D,), jnp.float32), 'ca_ow': s(ks[12], (D, D)), 'ca_ob': jnp.zeros((D,), jnp.float32), 'ffn_w1': s(ks[13], (D, DFF)), 'ffn_b1': jnp.zeros((DFF,), jnp.float32), 'ffn_w2': s(ks[14], (DFF, D)), 'ffn_b2': jnp.zeros((D,), jnp.float32)}
        return inp
    _L0_xcond_all = _L0_xcond_setup()
    _L0_xcond_in = {k: v for k, v in _L0_xcond_all.items() if k in ('ln1_g', 'ln1_b', 'aff1_w', 'aff1_b', 'ln2_g', 'ln2_b', 'aff2_w', 'aff2_b', 'sa_qw', 'sa_qb', 'sa_kw', 'sa_kb', 'sa_vw', 'sa_vb', 'sa_ow', 'sa_ob', 'ca_qw', 'ca_qb', 'ca_kw', 'ca_kb', 'ca_vw', 'ca_vb', 'ca_ow', 'ca_ob', 'ffn_w1', 'ffn_b1', 'ffn_w2', 'ffn_b2')}
    del _L0_xcond_all

    def _L1_xcond_setup():
        import jax, jax.numpy as jnp
        import numpy as np
        H = 128
        RH = 2 * H
        E = 3
        B, T, P = (8, 256, 64)
        LN_EPS = 1e-05

        def _layer_norm(x, gamma, beta):
            mu = jnp.mean(x, axis=-1, keepdims=True)
            var = jnp.mean(jnp.square(x - mu), axis=-1, keepdims=True)
            return (x - mu) * jax.lax.rsqrt(var + LN_EPS) * gamma + beta
        key = jax.random.key(seed)
        ks = jax.random.split(key, 24)
        s = lambda fan_in: 1.0 / np.sqrt(fan_in)
        inp = {'mix_hidden_states': jax.random.normal(ks[0], (B, T, H), jnp.float32), 'global_anchor': jax.random.normal(ks[1], (B, H), jnp.float32), 'prototype_bank': jax.random.normal(ks[2], (B, P, H), jnp.float32), 'ln_gamma': jnp.ones((H,), jnp.float32), 'ln_beta': jnp.zeros((H,), jnp.float32), 'Wq': jax.random.normal(ks[3], (H, H), jnp.float32) * s(H), 'Wk': jax.random.normal(ks[4], (H, H), jnp.float32) * s(H), 'Wv': jax.random.normal(ks[5], (H, H), jnp.float32) * s(H), 'router_W': jax.random.normal(ks[6], (3 * H, E), jnp.float32) * s(3 * H), 'router_b': jnp.zeros((E,), jnp.float32), 'e_w1': jax.random.normal(ks[7], (E, 3 * H, RH), jnp.float32) * s(3 * H), 'e_b1': jnp.zeros((E, RH), jnp.float32), 'e_w2': jax.random.normal(ks[8], (E, RH, H), jnp.float32) * s(RH), 'e_b2': jnp.zeros((E, H), jnp.float32), 'gate_w1': jax.random.normal(ks[9], (3 * H, H), jnp.float32) * s(3 * H), 'gate_b1': jnp.zeros((H,), jnp.float32), 'gate_w2': jax.random.normal(ks[10], (H, H), jnp.float32) * s(H), 'gate_b2': jnp.zeros((H,), jnp.float32), 'out_w': jax.random.normal(ks[11], (H, H), jnp.float32) * s(H), 'out_b': jnp.zeros((H,), jnp.float32)}
        return inp
    _L1_xcond_all = _L1_xcond_setup()
    _L1_xcond_in = {k: v for k, v in _L1_xcond_all.items() if k in ('ln_gamma', 'ln_beta', 'Wq', 'Wk', 'Wv', 'router_W', 'router_b', 'e_w1', 'e_b1', 'e_w2', 'e_b2', 'gate_w1', 'gate_b1', 'gate_w2', 'gate_b2', 'out_w', 'out_b')}
    del _L1_xcond_all
    return {'x': x, 'ctx_1024': ctx_1024, 'cond_1024': cond_1024, 'L0_xcond_ln1_g': _L0_xcond_in['ln1_g'], 'L0_xcond_ln1_b': _L0_xcond_in['ln1_b'], 'L0_xcond_aff1_w': _L0_xcond_in['aff1_w'], 'L0_xcond_aff1_b': _L0_xcond_in['aff1_b'], 'L0_xcond_ln2_g': _L0_xcond_in['ln2_g'], 'L0_xcond_ln2_b': _L0_xcond_in['ln2_b'], 'L0_xcond_aff2_w': _L0_xcond_in['aff2_w'], 'L0_xcond_aff2_b': _L0_xcond_in['aff2_b'], 'L0_xcond_sa_qw': _L0_xcond_in['sa_qw'], 'L0_xcond_sa_qb': _L0_xcond_in['sa_qb'], 'L0_xcond_sa_kw': _L0_xcond_in['sa_kw'], 'L0_xcond_sa_kb': _L0_xcond_in['sa_kb'], 'L0_xcond_sa_vw': _L0_xcond_in['sa_vw'], 'L0_xcond_sa_vb': _L0_xcond_in['sa_vb'], 'L0_xcond_sa_ow': _L0_xcond_in['sa_ow'], 'L0_xcond_sa_ob': _L0_xcond_in['sa_ob'], 'L0_xcond_ca_qw': _L0_xcond_in['ca_qw'], 'L0_xcond_ca_qb': _L0_xcond_in['ca_qb'], 'L0_xcond_ca_kw': _L0_xcond_in['ca_kw'], 'L0_xcond_ca_kb': _L0_xcond_in['ca_kb'], 'L0_xcond_ca_vw': _L0_xcond_in['ca_vw'], 'L0_xcond_ca_vb': _L0_xcond_in['ca_vb'], 'L0_xcond_ca_ow': _L0_xcond_in['ca_ow'], 'L0_xcond_ca_ob': _L0_xcond_in['ca_ob'], 'L0_xcond_ffn_w1': _L0_xcond_in['ffn_w1'], 'L0_xcond_ffn_b1': _L0_xcond_in['ffn_b1'], 'L0_xcond_ffn_w2': _L0_xcond_in['ffn_w2'], 'L0_xcond_ffn_b2': _L0_xcond_in['ffn_b2'], 'L1_xcond_ln_gamma': _L1_xcond_in['ln_gamma'], 'L1_xcond_ln_beta': _L1_xcond_in['ln_beta'], 'L1_xcond_Wq': _L1_xcond_in['Wq'], 'L1_xcond_Wk': _L1_xcond_in['Wk'], 'L1_xcond_Wv': _L1_xcond_in['Wv'], 'L1_xcond_router_W': _L1_xcond_in['router_W'], 'L1_xcond_router_b': _L1_xcond_in['router_b'], 'L1_xcond_e_w1': _L1_xcond_in['e_w1'], 'L1_xcond_e_b1': _L1_xcond_in['e_b1'], 'L1_xcond_e_w2': _L1_xcond_in['e_w2'], 'L1_xcond_e_b2': _L1_xcond_in['e_b2'], 'L1_xcond_gate_w1': _L1_xcond_in['gate_w1'], 'L1_xcond_gate_b1': _L1_xcond_in['gate_b1'], 'L1_xcond_gate_w2': _L1_xcond_in['gate_w2'], 'L1_xcond_gate_b2': _L1_xcond_in['gate_b2'], 'L1_xcond_out_w': _L1_xcond_in['out_w'], 'L1_xcond_out_b': _L1_xcond_in['out_b']}

def reference(x, ctx_1024, cond_1024, L0_xcond_ln1_g, L0_xcond_ln1_b, L0_xcond_aff1_w, L0_xcond_aff1_b, L0_xcond_ln2_g, L0_xcond_ln2_b, L0_xcond_aff2_w, L0_xcond_aff2_b, L0_xcond_sa_qw, L0_xcond_sa_qb, L0_xcond_sa_kw, L0_xcond_sa_kb, L0_xcond_sa_vw, L0_xcond_sa_vb, L0_xcond_sa_ow, L0_xcond_sa_ob, L0_xcond_ca_qw, L0_xcond_ca_qb, L0_xcond_ca_kw, L0_xcond_ca_kb, L0_xcond_ca_vw, L0_xcond_ca_vb, L0_xcond_ca_ow, L0_xcond_ca_ob, L0_xcond_ffn_w1, L0_xcond_ffn_b1, L0_xcond_ffn_w2, L0_xcond_ffn_b2, L1_xcond_ln_gamma, L1_xcond_ln_beta, L1_xcond_Wq, L1_xcond_Wk, L1_xcond_Wv, L1_xcond_router_W, L1_xcond_router_b, L1_xcond_e_w1, L1_xcond_e_b1, L1_xcond_e_w2, L1_xcond_e_b2, L1_xcond_gate_w1, L1_xcond_gate_b1, L1_xcond_gate_w2, L1_xcond_gate_b2, L1_xcond_out_w, L1_xcond_out_b):
    import jax
    import jax.numpy as jnp

    def _L0_xcond_ref(x, u, t_emb, ln1_g, ln1_b, aff1_w, aff1_b, ln2_g, ln2_b, aff2_w, aff2_b, sa_qw, sa_qb, sa_kw, sa_kb, sa_vw, sa_vb, sa_ow, sa_ob, ca_qw, ca_qb, ca_kw, ca_kb, ca_vw, ca_vb, ca_ow, ca_ob, ffn_w1, ffn_b1, ffn_w2, ffn_b2):
        import jax, jax.numpy as jnp
        import numpy as np
        D = 128
        H = 16
        DH = D // H
        DFF = 512
        B = 2
        L = 256
        EPS = 1e-05

        def layer_norm(x, g, b):
            mu = jnp.mean(x, axis=-1, keepdims=True)
            var = jnp.mean(jnp.square(x - mu), axis=-1, keepdims=True)
            return (x - mu) * jax.lax.rsqrt(var + EPS) * g + b

        def ada_ln(x, t_emb, ln_g, ln_b, aff_w, aff_b):
            normed = layer_norm(x, ln_g, ln_b)
            affine = t_emb @ aff_w + aff_b
            gamma, beta = jnp.split(affine, 2, axis=-1)
            return gamma[:, None, :] * normed + beta[:, None, :]

        def mha(q_in, k_in, v_in, qw, qb, kw, kb, vw, vb, ow, ob):
            Bq, Lq, _ = q_in.shape
            Lk = k_in.shape[1]
            Q = (q_in @ qw + qb).reshape(Bq, Lq, H, DH)
            K = (k_in @ kw + kb).reshape(Bq, Lk, H, DH)
            V = (v_in @ vw + vb).reshape(Bq, Lk, H, DH)
            scores = jnp.einsum('bqhd,bkhd->bhqk', Q, K) / np.sqrt(DH).astype(np.float32)
            attn = jax.nn.softmax(scores, axis=-1)
            out = jnp.einsum('bhqk,bkhd->bqhd', attn, V).reshape(Bq, Lq, D)
            return out @ ow + ob
        xn = ada_ln(x, t_emb, ln1_g, ln1_b, aff1_w, aff1_b)
        x = x + mha(xn, xn, xn, sa_qw, sa_qb, sa_kw, sa_kb, sa_vw, sa_vb, sa_ow, sa_ob)
        x = x + mha(x, u, u, ca_qw, ca_qb, ca_kw, ca_kb, ca_vw, ca_vb, ca_ow, ca_ob)
        xn = ada_ln(x, t_emb, ln2_g, ln2_b, aff2_w, aff2_b)
        h = jax.nn.gelu(xn @ ffn_w1 + ffn_b1, approximate=False)
        x = x + (h @ ffn_w2 + ffn_b2)
        return x

    def _L1_xcond_ref(mix_hidden_states, global_anchor, prototype_bank, ln_gamma, ln_beta, Wq, Wk, Wv, router_W, router_b, e_w1, e_b1, e_w2, e_b2, gate_w1, gate_b1, gate_w2, gate_b2, out_w, out_b):
        import jax, jax.numpy as jnp
        import numpy as np
        H = 128
        RH = 2 * H
        E = 3
        B, T, P = (8, 256, 64)
        LN_EPS = 1e-05

        def _layer_norm(x, gamma, beta):
            mu = jnp.mean(x, axis=-1, keepdims=True)
            var = jnp.mean(jnp.square(x - mu), axis=-1, keepdims=True)
            return (x - mu) * jax.lax.rsqrt(var + LN_EPS) * gamma + beta
        x = mix_hidden_states
        nx = _layer_norm(x, ln_gamma, ln_beta)
        q = nx @ Wq
        k = prototype_bank @ Wk
        v = prototype_bank @ Wv
        scores = jnp.einsum('bth,bph->btp', q, k) * H ** (-0.5)
        weights = jax.nn.softmax(scores, axis=-1)
        evidence = jnp.einsum('btp,bph->bth', weights, v)
        anchor = jnp.broadcast_to(global_anchor[:, None, :], nx.shape)
        combined = jnp.concatenate([nx, evidence, anchor], axis=-1)
        router_logits = combined @ router_W + router_b
        router_probs = jax.nn.softmax(router_logits, axis=-1)
        h = jax.nn.silu(jnp.einsum('btc,ecr->bter', combined, e_w1) + e_b1)
        expert_out = jnp.einsum('bter,erh->bteh', h, e_w2) + e_b2
        routed = jnp.sum(expert_out * router_probs[..., None], axis=-2)
        g = jax.nn.sigmoid(jax.nn.silu(combined @ gate_w1 + gate_b1) @ gate_w2 + gate_b2)
        refined_delta = g * (routed @ out_w + out_b)
        return x + refined_delta
    x = _L0_xcond_ref(x, ctx_1024, cond_1024, L0_xcond_ln1_g, L0_xcond_ln1_b, L0_xcond_aff1_w, L0_xcond_aff1_b, L0_xcond_ln2_g, L0_xcond_ln2_b, L0_xcond_aff2_w, L0_xcond_aff2_b, L0_xcond_sa_qw, L0_xcond_sa_qb, L0_xcond_sa_kw, L0_xcond_sa_kb, L0_xcond_sa_vw, L0_xcond_sa_vb, L0_xcond_sa_ow, L0_xcond_sa_ob, L0_xcond_ca_qw, L0_xcond_ca_qb, L0_xcond_ca_kw, L0_xcond_ca_kb, L0_xcond_ca_vw, L0_xcond_ca_vb, L0_xcond_ca_ow, L0_xcond_ca_ob, L0_xcond_ffn_w1, L0_xcond_ffn_b1, L0_xcond_ffn_w2, L0_xcond_ffn_b2)
    x = _L1_xcond_ref(x, cond_1024, ctx_1024, L1_xcond_ln_gamma, L1_xcond_ln_beta, L1_xcond_Wq, L1_xcond_Wk, L1_xcond_Wv, L1_xcond_router_W, L1_xcond_router_b, L1_xcond_e_w1, L1_xcond_e_b1, L1_xcond_e_w2, L1_xcond_e_b2, L1_xcond_gate_w1, L1_xcond_gate_b1, L1_xcond_gate_w2, L1_xcond_gate_b2, L1_xcond_out_w, L1_xcond_out_b)
    return x

_drawn_inputs = setup_inputs


def setup_inputs(seed=0):
    import zlib

    import numpy as np

    out = dict(_drawn_inputs(seed))
    spreads = {'L0_xcond_ln1_g': (1.0, 0.6),
     'L0_xcond_ln1_b': (0.0, 0.8),
     'L0_xcond_aff1_b': (0.0, 0.8),
     'L0_xcond_ln2_g': (1.0, 0.6),
     'L0_xcond_ln2_b': (0.0, 0.8),
     'L0_xcond_aff2_b': (0.0, 0.8),
     'L0_xcond_sa_qb': (0.0, 0.8),
     'L0_xcond_sa_kb': (0.0, 2.0),
     'L0_xcond_sa_vb': (0.0, 0.4),
     'L0_xcond_sa_ob': (0.0, 0.1),
     'L0_xcond_ca_qb': (0.0, 2.0),
     'L0_xcond_ca_kb': (0.0, 2.0),
     'L0_xcond_ca_vb': (0.0, 0.344),
     'L0_xcond_ca_ob': (0.0, 0.1),
     'L0_xcond_ffn_b1': (0.0, 0.345),
     'L0_xcond_ffn_b2': (0.0, 0.1),
     'L1_xcond_ln_gamma': (1.0, 0.572),
     'L1_xcond_ln_beta': (0.0, 0.55),
     'L1_xcond_router_b': (0.0, 0.375),
     'L1_xcond_e_b1': (0.0, 0.389),
     'L1_xcond_e_b2': (0.0, 0.1),
     'L1_xcond_gate_b1': (0.0, 0.8),
     'L1_xcond_gate_b2': (0.0, 0.8),
     'L1_xcond_out_b': (0.0, 0.1)}
    factors = {'L0_xcond_aff1_w': 4.688,
     'L0_xcond_aff2_w': 3.365,
     'L0_xcond_sa_qw': 8.0,
     'L0_xcond_sa_kw': 8.0,
     'L0_xcond_sa_vw': 4.496,
     'L0_xcond_ca_qw': 8.0,
     'L0_xcond_ca_kw': 8.0,
     'L0_xcond_ffn_w1': 3.038}
    for name, (base, spread) in spreads.items():
        noise = np.random.default_rng([zlib.crc32(name.encode()), seed]).standard_normal(out[name].shape)
        drawn = base * np.exp(spread * noise) if base else spread * noise
        out[name] = jnp.asarray(drawn.astype(out[name].dtype))
    for name, factor in factors.items():
        out[name] = (out[name] * factor).astype(out[name].dtype)
    return out
```

```python
from contextlib import ExitStack

import concourse.bass as bass
from concourse import mybir

F32 = mybir.dt.float32
BF16 = mybir.dt.bfloat16
ALU = mybir.AluOpType
ACT = mybir.ActivationFunctionType
AX = mybir.AxisListType

B, L, D = 2, 512, 128
H, DH = 16, 8
LC = 77
DFF = 512
P = 128
QT = L // P
E, RH = 3, 256
RC = RH // P
EPS = 1e-5
SCALE = 1.0 / (DH ** 0.5)
SCALE1 = D ** -0.5
HEADS = 4
GROUPS = H // HEADS
PARTS = 3
STACK = 6 * DH
STRIP = 64

VECTORS = [("ln1_g", 1), ("ln1_b", 1), ("aff1_b", 2), ("ln2_g", 1), ("ln2_b", 1), ("aff2_b", 2),
           ("sa_qb", 1), ("sa_kb", 1), ("sa_vb", 1), ("sa_ob", 1), ("ca_qb", 1), ("ca_kb", 1),
           ("ca_vb", 1), ("ca_ob", 1), ("ffn_b1", DFF // P), ("ffn_b2", 1), ("ln_gamma", 1),
           ("ln_beta", 1), ("e_b1", E * RC), ("gate_b1", 1), ("gate_b2", 1), ("out_b", 1),
           ("cond", B)]
EARLY = [("vec", sum(n for _, n in VECTORS)), ("aff1_w", 2 * D), ("sa_qw", D), ("sa_kw", D),
         ("sa_vw", D)]
LATE = [("ctxT", B * LC), ("ca_kw", D), ("ca_vw", D), ("Wk", D), ("WqT", D), ("Wv", D),
        ("sa_ow", D), ("ca_qw", D), ("ca_ow", D), ("aff2_w", 2 * D), ("ffn_w1", DFF),
        ("ffn_w2", DFF), ("router_W", 3 * E), ("e_w1", 3 * E * RH), ("e_w2", E * RC * D),
        ("gate_w1", 3 * D), ("gate_w2", D), ("out_w", D)]


def places(fields):
    at, out = 0, {}
    for name, n in fields:
        out[name] = at
        at += n
    return out, at


VEC_AT, _ = places(VECTORS)
EARLY_AT, EARLY_N = places(EARLY)
LATE_AT, LATE_N = places(LATE)

SELF, CROSS = 0, 1
TWO_ONES = 1 + 0x3F80 / 2 ** 23
RING = GROUPS


def maxima_chunks():
    chunks = [(SELF, b, g, qt) for b in range(B) for g in range(GROUPS) for qt in range(QT)]
    cross = [[(CROSS, b, g, half) for g in range(GROUPS) for half in range(2)] for b in range(B)]
    return chunks, cross


def plan():
    chunks, cross = maxima_chunks()
    steps = []

    def maxima(c):
        steps.append(("maxima", c))
        kind, b, g, i = c
        if i == (QT if kind == SELF else 2) - 1:
            steps.append(("split", kind, b, g))

    units = [(SELF, b, g) for b in range(B) for g in range(GROUPS)]
    ahead = 6
    for c in chunks[:QT]:
        maxima(c)
    todo = chunks[QT:]
    steps.append(("mrows",) + units[0])
    steps.append(("prepare_rest",))
    for _ in range(ahead - QT):
        maxima(todo.pop(0))
    rounds = [(u, kt) for u in units for kt in range(QT)]
    later = {}
    for n, (unit, kt) in enumerate(rounds):
        kind, b, g = unit
        steps.append(("scores", unit, kt, n))
        if n:
            steps.append(("values", rounds[n - 1][0], rounds[n - 1][1], n - 1))
            for s in later.pop(n - 1, []):
                steps.append(s)
        steps.append(("exps", unit, kt, n))
        if todo:
            maxima(todo.pop(0))
        elif cross[0] and n < len(rounds) - 1:
            maxima(cross[0].pop(0))
            maxima(cross[0].pop(0))
        if kt == 2 and n // QT + 1 < len(units):
            steps.append(("mrows",) + units[n // QT + 1])
        if kt == QT - 1 and g % 2 == 1:
            r = g // 2
            later.setdefault(n, []).append(("gather", kind, b, r))
            later.setdefault(n + 1, []).append(("natural", kind, b, r))
            if r == 1:
                later.setdefault(n + 2, []).append(("turn", kind, b))
                later.setdefault(n + 4, []).append(("project", kind, b))
                later.setdefault(n + 5, []).append(("queries", b))
    n = len(rounds)
    steps.append(("values", rounds[-1][0], rounds[-1][1], n - 1))
    for m in sorted(later):
        steps += later[m]
    for b in range(B):
        for c in cross[b]:
            maxima(c)
        for g in range(GROUPS):
            steps.append(("mrows", CROSS, b, g))
        for g in range(GROUPS):
            unit = (CROSS, b, g)
            steps.append(("scores", unit, 0, n))
            steps.append(("exps", unit, 0, n))
            steps.append(("values", unit, 0, n))
            if g % 2 == 1:
                steps.append(("gather", CROSS, b, g // 2))
                steps.append(("natural", CROSS, b, g // 2))
            n += 1
        steps.append(("turn", CROSS, b))
        steps.append(("project", CROSS, b))
    return steps


def counts(steps):
    seen, out = {}, []
    for s in steps:
        k = s[0]
        out.append(seen.get(k, 0))
        seen[k] = out[-1] + 1
    return out


def block_program(nc, x_nat, x_T, early, late, router_b, e_b2, out_T):
    steps = plan()
    nth = counts(steps)
    TURNS = {"mrows": "mT_out", "natural": "o_out", "turn": "oT_out", "project": "x_out",
             "queries": "rest_qx"}
    bank_reader, before = [], None
    for st, n in zip(steps, nth):
        bank_reader.append(before)
        if st[0] in TURNS:
            before = (TURNS[st[0]], n + 1)
    event_at, ev = {}, 0
    for s in steps:
        if s[0] == "maxima":
            event_at[s[1]] = ev
            ev += 4 if s[1][0] == SELF else 2
    split_nth = {s[1:]: nth[i] for i, s in enumerate(steps) if s[0] == "split"}
    mrows_nth = {s[1:]: nth[i] for i, s in enumerate(steps) if s[0] == "mrows"}
    queries_nth = {s[1]: nth[i] for i, s in enumerate(steps) if s[0] == "queries"}

    with ExitStack() as ctx:
        def sb(name, shape, dt=F32):
            return ctx.enter_context(nc.sbuf_tensor(name, shape, dt))

        def psum(name, shape, dt=F32):
            return ctx.enter_context(nc.psum_tensor(name, shape, dt))

        def sem(name):
            return ctx.enter_context(nc.semaphore(name))

        xn = sb("xn", [P, B * QT, D])
        xT = sb("xT", [P, B, L])
        w_early = sb("w_early", [P, EARLY_N])
        w_late = sb("w_late", [P, LATE_N])
        rb_row = sb("rb_row", [1, E])
        b2_rows = sb("b2_rows", [E, D])
        ident = sb("ident", [P, P])
        ident16 = sb("ident16", [P, P], BF16)
        ones_row = sb("ones_row", [1, P])
        pick = sb("pick", [E, E, P])
        half = sb("half", [P, B * QT])
        stats = sb("stats", [P, B * QT, 6])
        mv = sb("mv", [P, B * QT, 2])
        rstd = sb("rstd", [P, B * QT])
        aff = sb("aff", [P, 2, 2, B])
        lnA = sb("lnA", [P, 2, B])
        lnB = sb("lnB", [P, 2, B])
        normed = sb("normed", [P, B * QT, D])
        xnT = sb("xnT", [P, B, L])
        QS = sb("QS", [P, H // 2, B * L], BF16)
        KS = sb("KS", [P, H // 2, B * L], BF16)
        QX = sb("QX", [P, H // 2, B * L], BF16)
        KX = sb("KX", [P, H // 2, B * LC], BF16)
        part = sb("part", [P, 2, PARTS, L], BF16)
        rest = sb("rest", [P, 2, L])
        VS = sb("VS", [P, B * QT, H, 32])
        VX = sb("VX", [LC, B, H, 32])
        PT = sb("PT", [P, 2, HEADS, L])
        negm = sb("negm", [P, RING, QT, HEADS])
        mrest = sb("mrest", [P, RING, QT, HEADS])
        mpart = sb("mpart", [P, RING, QT, PARTS, HEADS], BF16)
        mT = sb("mT", [PARTS * HEADS, 2, L], BF16)
        U = sb("U", [P, 2, L])
        rden = sb("rden", [P, 2, QT, 8])
        O = sb("O", [P, QT, D])
        OT = sb("OT", [P, L])
        csa = sb("csa", [P, 2])
        kT1 = sb("kT1", [P, B * LC])
        kfold = sb("kfold", [P, B * LC])
        v1 = sb("v1", [LC, B, D])
        hbias = sb("hbias", [P, E * RC + 1, B])
        rbias = sb("rbias", [P, B, E])
        hT = VS[:, :, :, :].rearrange("p (b a) h c -> p b (a h c)", b=B).rearrange("p b (f t) -> p b f t", t=L)
        s1 = sb("s1", [P, B, QT, LC])
        mx1 = sb("mx1", [P, B, QT])
        sum1 = sb("sum1", [P, B, QT])
        rec1 = sb("rec1", [P, B, QT])
        p1T = sb("p1T", [LC, B, L])
        evT = sb("evT", [P, B, L])
        lg = sb("lg", [P, B, QT, E])
        rmx = sb("rmx", [P, B, QT])
        rsum = sb("rsum", [P, B, QT])
        rrec = sb("rrec", [P, B, QT])
        prT = sb("prT", [E, B, L])
        eh = sb("eh", [P, B, E * RC + 1, L])
        rtT = PT[:, 0, 0:2, :]
        gT = PT[:, 0, 2:4, :]
        dT = PT[:, 1, 0:2, :]

        S = psum("S", [P, 2, 512])
        ST = psum("ST", [P, 4, 512])
        UP = psum("UP", [P, 512])
        MB = psum("MB", [P, 512])
        MB16 = MB[:, :].bitcast(BF16)
        def bank(b, i):
            n = 4 * b + i
            if n < 4:
                return ST[:, n, :]
            return [S[:, 0, :], S[:, 1, :], UP[:, :], MB[:, :]][n - 4]

        scr_q = nc.dram_tensor("scr_q", [2 * B, PARTS, P, L], BF16, kind="Internal").ap()
        scr_k = nc.dram_tensor("scr_k", [B, PARTS, P, L], BF16, kind="Internal").ap()
        scr_kx = nc.dram_tensor("scr_kx", [PARTS, P, B * LC], BF16, kind="Internal").ap()

        def ve(name, i=0, n=1):
            at = EARLY_AT["vec"] + VEC_AT[name] + i
            return w_early[:, at:at + n]

        def we(name, i=0, n=D):
            at = EARLY_AT[name] + i * D
            return w_early[:, at:at + n]

        def wl(name, i=0, n=D):
            at = LATE_AT[name] + i * D
            return w_late[:, at:at + n]

        names = """ld_x ld_early ld_xT ld_late ld_small consts ones_set zeros_set
            aff_ready aff_out stats_out rstd_in rstd_out bn_out normed_out normT_ready xnT_out0 xnT_out1
            q_ready k_ready v_ready q1_out k1_out v_out rest_q rest_k q23_out k23_out
            strips_w strips_q0 strips_q1 strips_k0 strips_k1 strips_w2 strips_qx0 strips_qx1
            ctx_ready ctx_v_ready kx1_out kx_rest kx23_out kxw kxs vx_out kT1_out v1_out
            mod_step kfold_out small_ready small_out
            s_ready max_out negm_out mp1 mp2 mparts mrows_ready mT_out mrows_in0 mrows_in1
            st_ready exp_out u_ready u_out nat_ready rden_out o_out turn_ready oT_out
            proj_ready x_out qx_ready qx1_out rest_qx qx23_out
            n_ready n_stats n_aggr n_var n_rstd n_normed nT_ready nT_out0 nT_out1
            f_ready f_out f2_ready x3_out l_s_ready l_max l_sub l_exp l_sum l_rec l_p l_pT l_pT_out
            l_ev l_ev_out r_ready r_lg r_mx r_sub r_exp r_sum r_rec r_p r_pT r_pT_out
            e_ready e_out pb_ready e_scaled e2_ready rt_out g2_ready g_out d_ready d_out y_out
            stored""".split()
        s = {n: sem(n) for n in names}

        block = ctx.enter_context(nc.Block())

        @block.sync
        def _(sp):
            sp.dma_start(xn[:, :, :], x_nat).then_inc(s["ld_x"], 16)
            sp.dma_start(w_early[:, :], early).then_inc(s["ld_early"], 16)
            sp.dma_start(w_late[:, :], late).then_inc(s["ld_late"], 16)
            sp.dma_start(xT[:, :, :], x_T).then_inc(s["ld_xT"], 16)
            sp.dma_start(rb_row[:, :], router_b).then_inc(s["ld_small"], 16)
            sp.dma_start(b2_rows[:, :], e_b2).then_inc(s["ld_small"], 16)

            def strips(dst, src, counts_, lo, n, done):
                for p in range(2):
                    row = STRIP * p
                    for first, times, step in counts_:
                        v = src.rearrange("i (k q d) t -> q i d k t", q=2, d=DH)[p]
                        for j in range(times):
                            sp.dma_start(dst[row:row + DH, :, lo:lo + n],
                                         v[first + j * step]).then_inc(done, 16)
                            row += DH

            sp.wait_ge(s["ones_set"], 2)
            Q_STACK = [(0, 3, 0), (1, 2, 0), (2, 1, 0)]
            K_STACK = [(0, 3, 1), (0, 2, 1), (0, 1, 0)]
            for b in range(B):
                sp.wait_ge(s["q1_out"], b + 1)
                sp.wait_ge(s["q23_out"], 2 * b + 2)
                sp.dma_start(scr_q[b].rearrange("i p t -> p i t"), part[:, 0, :, :]).then_inc(s["strips_w"], 16)
                sp.wait_ge(s["k1_out"], b + 1)
                sp.wait_ge(s["k23_out"], 2 * b + 2)
                sp.dma_start(scr_k[b].rearrange("i p t -> p i t"), part[:, 1, :, :]).then_inc(s["strips_w"], 16)
                sp.wait_ge(s["strips_w"], 32 * (b + 1))
                strips(QS, scr_q[b], Q_STACK, b * L, L, s[f"strips_q{b}"])
                strips(KS, scr_k[b], K_STACK, b * L, L, s[f"strips_k{b}"])

            def cross_keys():
                sp.wait_ge(s["kx1_out"], 1)
                sp.wait_ge(s["kx23_out"], 2)
                sp.dma_start(scr_kx.rearrange("i p t -> p i t"), part[:, 1, :, 0:B * LC]).then_inc(s["kxw"], 16)
                sp.wait_ge(s["kxw"], 16)
                strips(KX, scr_kx, K_STACK, 0, B * LC, s["kxs"])

            for i, step in enumerate(steps):
                if step[0] == "mrows":
                    kind, b, g = step[1:]
                    n = nth[i]
                    sp.wait_ge(s["mT_out"], n + 1)
                    dst = QS if kind == SELF else QX
                    for p in range(2):
                        for jj in range(2):
                            sp.dma_start(dst[STRIP * p + STACK:STRIP * p + STACK + PARTS, 2 * g + jj, b * L:(b + 1) * L],
                                         mT[2 * jj + p:2 * jj + p + 2 * HEADS + 1:HEADS, n % 2, :]).then_inc(s[f"mrows_in{n % 2}"], 16)
                elif step[0] == "prepare_rest":
                    cross_keys()
                elif step[0] == "queries":
                    b = step[1]
                    sp.wait_ge(s["qx1_out"], b + 1)
                    sp.wait_ge(s["qx23_out"], 2 * b + 2)
                    sp.dma_start(scr_q[B + b].rearrange("i p t -> p i t"), part[:, 0, :, :]).then_inc(s["strips_w2"], 16)
                    sp.wait_ge(s["strips_w2"], 16 * (b + 1))
                    strips(QX, scr_q[B + b], Q_STACK, b * L, L, s[f"strips_qx{b}"])
            for b in range(B):
                sp.wait_ge(s["y_out"], b + 1)
                sp.dma_start(out_T[b], dT[:, b, :]).then_inc(s["stored"], 16)
            sp.wait_ge(s["stored"], 16 * B)

        STRIP_DMAS = 16 * 12

        @block.gpsimd
        def _(pool):
            g = nc.gpsimd
            g.memset(ident[:, :], 0.0).then_inc(s["zeros_set"], 1)
            g.memset(ident16[:, :], 0.0).then_inc(s["zeros_set"], 1)
            g.memset(pick[:, :, :], 0.0).then_inc(s["zeros_set"], 1)
            g.memset(half[:, :], -0.5).then_inc(s["zeros_set"], 1)
            g.memset(ones_row[:, :], 1.0).then_inc(s["consts"], 1)
            pool.wait_ge(s["zeros_set"], 4)
            for t in (ident, ident16):
                g.affine_select(out=t[:, :], in_=t[:, :], compare_op=ALU.not_equal, fill=1.0, base=0,
                                pattern=[[-1, P]], channel_multiplier=1).then_inc(s["consts"], 1)
            g.affine_select(out=pick[:, :, :], in_=pick[:, :, :], compare_op=ALU.not_equal, fill=1.0,
                            base=0, pattern=[[-1, E], [0, P]], channel_multiplier=1).then_inc(s["consts"], 1)
            for t in (KS, KX):
                g.memset(t[:, :, :].bitcast(F32), TWO_ONES).then_inc(s["ones_set"], 1)
            g.memset(VS[:, :, :, :], 0.0).then_inc(s["ones_set"], 1)
            g.memset(VX[:, :, :, :], 0.0).then_inc(s["ones_set"], 1)
            pool.wait_ge(s["ones_set"], 4)
            for t, lead in ((VS, B * QT), (VX, B)):
                v = t[:, :, :, :].rearrange("p a (r s j) c -> p (a r) s j c", s=2, j=HEADS)
                for sl in range(2):
                    g.memset(v[:, :, sl, :, 16 * sl + DH], 1.0).then_inc(s["ones_set"], 1)
            pool.wait_ge(s["rstd_in"], 1)
            g.tensor_tensor(rstd[:, :], rstd[:, :], half[:, :], ALU.pow).then_inc(s["rstd_out"], 1)

            def two_parts(slot, ready, done, n):
                pool.wait_ge(ready[0], ready[1])
                g.tensor_copy(part[:, slot, 1, 0:n], rest[:, slot, 0:n]).then_inc(done[0], 1)
                pool.wait_ge(done[0], done[1])
                g.tensor_tensor(part[:, slot, 2, 0:n], rest[:, slot, 0:n], part[:, slot, 1, 0:n],
                                ALU.subtract).then_inc(done[0], 1)

            for b in range(B):
                if b:
                    pool.wait_ge(s["strips_w"], 32 * b)
                two_parts(0, (s["rest_q"], b + 1), (s["q23_out"], 2 * b + 1), L)
                two_parts(1, (s["rest_k"], b + 1), (s["k23_out"], 2 * b + 1), L)
            pool.wait_ge(s["strips_w"], 32 * B)
            two_parts(1, (s["kx_rest"], 1), (s["kx23_out"], 1), B * LC)
            for i, step in enumerate(steps):
                if step[0] == "queries":
                    b = step[1]
                    if b:
                        pool.wait_ge(s["strips_w2"], 16 * b)
                    two_parts(0, (s["rest_qx"], b + 1), (s["qx23_out"], 2 * b + 1), L)
            for site in range(2):
                for b in range(B):
                    n = site * B + b
                    pool.wait_ge(s["n_var"], n + 1)
                    g.tensor_tensor(rstd[:, b * QT:(b + 1) * QT], rstd[:, b * QT:(b + 1) * QT],
                                    half[:, b * QT:(b + 1) * QT], ALU.pow).then_inc(s["n_rstd"], 1)

        @block.tensor
        def _(pe):
            mm = nc.tensor.matmul
            pe.wait_ge(s["consts"], 4)
            pe.wait_ge(s["ld_early"], 16)
            cond = ve("cond", 0, B)
            for i in range(2):
                last = mm(MB[:, B * i:B * i + B], we("aff1_w", i), cond, start=True, stop=True)
            last.then_inc(s["aff_ready"], 1)
            for b in range(B):
                for t in range(QT):
                    pe.wait_ge(s["normed_out"], b * QT + t + 1)
                    last = nc.tensor.transpose(ST[:, b, t * P:(t + 1) * P], normed[:, b * QT + t, :], ident[:, :])
                last.then_inc(s["normT_ready"], 1)
            for b in range(B):
                pe.wait_ge(s[f"xnT_out{b}"], 1)
                mm(ST[:, 2 * b, :] if b else S[:, 0, :], we("sa_qw"), xnT[:, b, :], start=True, stop=True).then_inc(s["q_ready"], 1)
                mm(ST[:, 3, :] if b else S[:, 1, :], we("sa_kw"), xnT[:, b, :], start=True, stop=True).then_inc(s["k_ready"], 1)
                if b:
                    pe.wait_ge(s["v_out"], 2)
                for t in range(QT):
                    last = mm(UP[:, t * P:(t + 1) * P], xnT[:, b, t * P:(t + 1) * P], we("sa_vw"), start=True, stop=True)
                last.then_inc(s["v_ready"], 1)
            pe.wait_ge(s["ld_late"], 16)
            ctxT = wl("ctxT", 0, B * LC)
            pe.wait_ge(s["aff_out"], 1)
            mm(MB[:, 0:B * LC], wl("ca_kw"), ctxT, start=True, stop=True)
            mm(MB[:, B * LC:2 * B * LC], wl("Wk"), ctxT, start=True, stop=True).then_inc(s["ctx_ready"], 1)
            for b in range(B):
                c = ctxT[:, b * LC:(b + 1) * LC]
                mm(ST[0:LC, 0, b * D:(b + 1) * D], c, wl("ca_vw"), start=True, stop=True)
                last = mm(ST[0:LC, 0, (B + b) * D:(B + b + 1) * D], c, wl("Wv"), start=True, stop=True)
            last.then_inc(s["ctx_v_ready"], 1)
            pe.wait_ge(s["kT1_out"], 1)
            mm(ST[:, 1, 0:B * LC], wl("WqT"), kT1[:, :], start=True, stop=True)
            at = B * LC
            for i in range(2):
                mm(ST[:, 1, at + B * i:at + B * i + B], wl("aff2_w", i), cond, start=True, stop=True)
            at += 2 * B
            mm(ST[:, 1, at:at + 1], wl("sa_ow"), ve("sa_vb"), start=True, stop=True)
            mm(ST[:, 1, at + 1:at + 2], wl("ca_ow"), ve("ca_vb"), start=True, stop=True)
            at += 2
            for c in range(E * RC + 1):
                w = e_w1(wl, c, 2)
                mm(ST[:, 1, at + B * c:at + B * c + B], w, cond, start=True, stop=True)
            at += B * (E * RC + 1)
            pe.wait_ge(s["ld_small"], 32)
            for b in range(B):
                o = ST[:, 1, at + E * b:at + E * b + E]
                mm(o, cond[:, b:b + 1].to_broadcast([P, P]), router_w(w_late, 2), start=True, stop=False)
                last = mm(o, ones_row[:, :], rb_row[:, :], start=False, stop=True)
            last.then_inc(s["small_ready"], 1)

            def maxima(c):
                kind, b, g, i = c
                n = event_at[c]
                if n == 0:
                    pe.wait_ge(s["rest_q"], 1)
                    pe.wait_ge(s["rest_k"], 1)
                    pe.wait_ge(s["ones_set"], 8)
                if kind == SELF:
                    pe.wait_ge(s[f"strips_q{b}"], STRIP_DMAS)
                    pe.wait_ge(s[f"strips_k{b}"], STRIP_DMAS)
                    for jj in range(2):
                        for p in range(2):
                            if n >= 2:
                                pe.wait_ge(s["max_out"], n - 1)
                            r = slice(STRIP * p, STRIP * p + STACK)
                            mm(S[:, n % 2, :], QS[r, 2 * g + jj, b * L + i * P:b * L + (i + 1) * P],
                               KS[r, 2 * g + jj, b * L:(b + 1) * L], start=True, stop=True).then_inc(s["s_ready"], 1)
                            n += 1
                else:
                    pe.wait_ge(s[f"strips_qx{b}"], STRIP_DMAS)
                    pe.wait_ge(s["kxs"], STRIP_DMAS)
                    for p in range(2):
                        pe.wait_ge(s["max_out"], n + p - 1)
                    for t in range(2):
                        for jj in range(2):
                            for p in range(2):
                                r = slice(STRIP * p, STRIP * p + STACK)
                                q0 = b * L + (2 * i + t) * P
                                last = mm(S[:, (n + p) % 2, (2 * t + jj) * LC:(2 * t + jj + 1) * LC],
                                          QX[r, 2 * g + jj, q0:q0 + P], KX[r, 2 * g + jj, b * LC:(b + 1) * LC],
                                          start=True, stop=True)
                                if t == 1 and jj == 1:
                                    last.then_inc(s["s_ready"], 1)

            def scores(unit, kt, n):
                kind, b, g = unit
                if n == 0:
                    pe.wait_ge(s["rest_q"], B)
                    pe.wait_ge(s["rest_k"], B)
                    pe.wait_ge(s["small_out"], 1)
                    pe.wait_ge(s["v1_out"], 1)
                m = mrows_nth[unit]
                pe.wait_ge(s[f"mrows_in{m % 2}"], 64 * (m // 2 + 1))
                for jj in range(2):
                    if n:
                        pe.wait_ge(s["exp_out"], 2 * (n - 1) + jj + 1)
                    for p in range(2):
                        r = slice(STRIP * p, STRIP * p + STACK + PARTS)
                        if kind == SELF:
                            last = mm(ST[:, 2 * jj + p, :], KS[r, 2 * g + jj, b * L + kt * P:b * L + (kt + 1) * P],
                                      QS[r, 2 * g + jj, b * L:(b + 1) * L], start=True, stop=True)
                        else:
                            last = mm(ST[0:LC, 2 * jj + p, :], KX[r, 2 * g + jj, b * LC:(b + 1) * LC],
                                      QX[r, 2 * g + jj, b * L:(b + 1) * L], start=True, stop=True)
                    last.then_inc(s["st_ready"], 1)

            def values(unit, kt, n):
                kind, b, g = unit
                nk = QT if kind == SELF else 1
                first = g % 2 == 0 and kt == 0
                final = g % 2 == 1 and kt == nk - 1
                w = (kind * B + b) * 2 + g // 2
                if first:
                    if w:
                        pe.wait_ge(s["u_out"], w)
                    else:
                        pe.wait_ge(s["v_out"], 2 * B)
                    if kind == CROSS:
                        pe.wait_ge(s["vx_out"], 2)
                pe.wait_ge(s["exp_out"], 2 * n + 2)
                for j in range(HEADS):
                    h = HEADS * g + j
                    if kind == SELF:
                        last = mm(UP[32 * j:32 * j + 32, :], VS[:, b * QT + kt, h, :], PT[:, n % 2, j, :],
                                  start=first, stop=final)
                    else:
                        last = mm(UP[32 * j:32 * j + 32, :], VX[:, b, h, :], PT[0:LC, n % 2, j, :],
                                  start=first, stop=final)
                last.then_inc(s["u_ready"], 1)

            for i, step in enumerate(steps):
                kind = step[0]
                if kind in TURNS and bank_reader[i]:
                    pe.wait_ge(s[bank_reader[i][0]], bank_reader[i][1])
                elif kind in TURNS:
                    pe.wait_ge(s["kT1_out"], 1)
                    pe.wait_ge(s["kx_rest"], 1)
                if kind == "maxima":
                    maxima(step[1])
                elif kind == "scores":
                    scores(*step[1:])
                elif kind == "values":
                    values(*step[1:])
                elif kind == "mrows":
                    n = split_nth[step[1:]]
                    pe.wait_ge(s["mparts"], n + 1)
                    for t in range(QT):
                        last = nc.tensor.transpose(MB16[0:PARTS * HEADS, t * P:(t + 1) * P],
                                                   mpart[:, n % RING, t, :, :].rearrange("p i j -> p (i j)"), ident16[:, :])
                    last.then_inc(s["mrows_ready"], 1)
                elif kind == "natural":
                    n = nth[i]
                    pe.wait_ge(s["u_out"], n + 1)
                    for t in range(QT):
                        last = nc.tensor.transpose(MB[:, t * P:(t + 1) * P], U[:, n % 2, t * P:(t + 1) * P], ident[:, :])
                    last.then_inc(s["nat_ready"], 1)
                elif kind == "turn":
                    pe.wait_ge(s["o_out"], 2 * nth[i] + 2)
                    for t in range(QT):
                        last = nc.tensor.transpose(MB[:, t * P:(t + 1) * P], O[:, t, :], ident[:, :])
                    last.then_inc(s["turn_ready"], 1)
                elif kind == "project":
                    pe.wait_ge(s["oT_out"], nth[i] + 1)
                    mm(MB[:, :], wl("sa_ow" if step[1] == SELF else "ca_ow"), OT[:, :], start=True, stop=True).then_inc(s["proj_ready"], 1)
                elif kind == "queries":
                    b = step[1]
                    pe.wait_ge(s["x_out"], b + 1)
                    mm(MB[:, :], wl("ca_qw"), xT[:, b, :], start=True, stop=True).then_inc(s["qx_ready"], 1)

            def norm(site, b):
                n = site * B + b
                if site == 0:
                    pe.wait_ge(s["x_out"], B + B)
                else:
                    pe.wait_ge(s["x3_out"], b + 1)
                for t in range(QT):
                    last = nc.tensor.transpose(bank(b, 0)[:, t * P:(t + 1) * P], xT[:, b, t * P:(t + 1) * P], ident[:, :])
                last.then_inc(s["n_ready"], 1)

            def norm_back(site, b):
                n = site * B + b
                pe.wait_ge(s["n_normed"], n + 1)
                for t in range(QT):
                    last = nc.tensor.transpose(bank(b, 1)[:, t * P:(t + 1) * P], normed[:, b * QT + t, :], ident[:, :])
                last.then_inc(s["nT_ready"], 1)

            for b in range(B):
                norm(0, b)
            for b in range(B):
                norm_back(0, b)
            for b in range(B):
                pe.wait_ge(s[f"nT_out{b}"], 1)
                for c in range(DFF // P):
                    mm(bank(b, c), wl("ffn_w1", c), xnT[:, b, :], start=True, stop=True).then_inc(s["f_ready"], 1)
            for b in range(B):
                pe.wait_ge(s["f_out"], (DFF // P) * (b + 1))
                for c in range(DFF // P):
                    last = mm(bank(b, 3), wl("ffn_w2", c), hT[:, b, c, :], start=(c == 0), stop=(c == DFF // P - 1))
                last.then_inc(s["f2_ready"], 1)
            for b in range(B):
                norm(1, b)
            for b in range(B):
                norm_back(1, b)
            for b in range(B):
                pe.wait_ge(s[f"nT_out{b}"], 2)
                for t in range(QT):
                    last = mm(bank(b, 2)[:, t * LC:(t + 1) * LC], xnT[:, b, t * P:(t + 1) * P],
                              kfold[:, b * LC:(b + 1) * LC], start=True, stop=True)
                last.then_inc(s["l_s_ready"], 1)
            for b in range(B):
                pe.wait_ge(s["l_p"], b + 1)
                for t in range(QT):
                    last = nc.tensor.transpose(bank(b, 3)[0:LC, t * P:(t + 1) * P], s1[:, b, t, :], ident[:, :])
                last.then_inc(s["l_pT"], 1)
            for b in range(B):
                pe.wait_ge(s["l_pT_out"], b + 1)
                mm(bank(b, 0), v1[:, b, :], p1T[:, b, :], start=True, stop=True).then_inc(s["l_ev"], 1)
            for b in range(B):
                pe.wait_ge(s["l_ev_out"], b + 1)
                for t in range(QT):
                    o = bank(b, 2)[:, t * E:(t + 1) * E]
                    mm(o, xnT[:, b, t * P:(t + 1) * P], router_w(w_late, 0), start=True, stop=False)
                    last = mm(o, evT[:, b, t * P:(t + 1) * P], router_w(w_late, 1), start=False, stop=True)
                last.then_inc(s["r_ready"], 1)
            for b in range(B):
                for c in range(E * RC + 1):
                    n = b * (E * RC + 1) + c
                    if c >= 3:
                        pe.wait_ge(s["e_out"], n - 2)
                    o = bank(b, (0, 1, 3)[c % 3])
                    mm(o, e_w1(wl, c, 0), xnT[:, b, :], start=True, stop=False)
                    mm(o, e_w1(wl, c, 1), evT[:, b, :], start=False, stop=True).then_inc(s["e_ready"], 1)
                pe.wait_ge(s["r_p"], b + 1)
                for t in range(QT):
                    last = nc.tensor.transpose(bank(b, 2)[0:E, t * P:(t + 1) * P], lg[:, b, t, :], ident[:, :])
                last.then_inc(s["r_pT"], 1)
            for b in range(B):
                pe.wait_ge(s["e_out"], (b + 1) * (E * RC + 1))
                pe.wait_ge(s["r_pT_out"], b + 1)
                for e in range(E):
                    mm(bank(b, e), pick[:, e, :], prT[:, b, :], start=True, stop=True).then_inc(s["pb_ready"], 1)
                mm(bank(b, 3), b2_rows[:, :], prT[:, b, :], start=True, stop=False)
                for c in range(E * RC):
                    pe.wait_ge(s["e_scaled"], b * E * RC + c + 1)
                    last = mm(bank(b, 3), wl("e_w2", c), eh[:, b, c, :], start=False, stop=(c == E * RC - 1))
                last.then_inc(s["e2_ready"], 1)
                mm(bank(b, 0), wl("gate_w2"), eh[:, b, E * RC, :], start=True, stop=True).then_inc(s["g2_ready"], 1)
                pe.wait_ge(s["rt_out"], b + 1)
                mm(bank(b, 1), wl("out_w"), rtT[:, b, :], start=True, stop=True).then_inc(s["d_ready"], 1)

        @block.scalar
        def _(act):
            a = nc.scalar.activation

            def first_part(ps, bias, slot, n, out_sem):
                a(part[:, slot, 0, 0:n], ps, ACT.Identity, bias=bias).then_inc(out_sem, 1)

            pb, kb = ve("sa_qb"), ve("sa_kb")
            act.wait_ge(s["ld_early"], 16)
            act.wait_ge(s["aff_out"], 1)
            act.wait_ge(s["normT_ready"], 2)
            a(xnT[:, 1, :], ST[:, 1, :], ACT.Identity, bias=lnB[:, 0, 1:2], scale=lnA[:, 0, 1:2]).then_inc(s["xnT_out1"], 1)
            for b in range(B):
                if b:
                    act.wait_ge(s["strips_w"], 32 * b)
                act.wait_ge(s["q_ready"], b + 1)
                first_part(ST[:, 2, :] if b else S[:, 0, :], pb, 0, L, s["q1_out"])
                act.wait_ge(s["k_ready"], b + 1)
                first_part(ST[:, 3, :] if b else S[:, 1, :], kb, 1, L, s["k1_out"])
                act.wait_ge(s["v_ready"], b + 1)
                act.wait_ge(s["ones_set"], 8)
                dst = VS[:, b * QT:(b + 1) * QT, :, :].rearrange("p a (r s j) c -> p (a r) s j c", s=2, j=HEADS)
                src = UP[:, :].rearrange("p (ar s j d) -> p ar s j d", s=2, j=HEADS, d=DH)
                for sl in range(2):
                    nc.scalar.copy(dst[:, :, sl, :, 16 * sl:16 * sl + DH], src[:, :, sl, :, :]).then_inc(s["v_out"], 1)
            act.wait_ge(s["strips_w"], 32 * B)
            act.wait_ge(s["ctx_ready"], 1)
            first_part(MB[:, 0:B * LC], ve("ca_kb"), 1, B * LC, s["kx1_out"])
            nc.scalar.copy(kT1[:, :], MB[:, B * LC:2 * B * LC]).then_inc(s["kT1_out"], 1)
            act.wait_ge(s["ctx_v_ready"], 1)
            dst = VX[:, :, :, :].rearrange("p a (r s j) c -> p (a r) s j c", s=2, j=HEADS)
            src = ST[0:LC, 0, 0:B * D].rearrange("p (ar s j d) -> p ar s j d", s=2, j=HEADS, d=DH)
            for sl in range(2):
                nc.scalar.copy(dst[:, :, sl, :, 16 * sl:16 * sl + DH], src[:, :, sl, :, :]).then_inc(s["vx_out"], 1)
            nc.scalar.copy(v1[:, :, :], ST[0:LC, 0, B * D:2 * B * D].rearrange("p (b d) -> p b d", b=B)).then_inc(s["v1_out"], 1)

            for i, step in enumerate(steps):
                kind = step[0]
                if kind == "exps":
                    unit, kt, n = step[1:]
                    rows = P if unit[0] == SELF else LC
                    if n >= 2:
                        act.wait_ge(s["u_ready"], n - 1)
                    for jj in range(2):
                        act.wait_ge(s["st_ready"], 2 * n + jj + 1)
                        a(PT[0:rows, n % 2, 2 * jj:2 * jj + 2, :], ST[0:rows, 2 * jj:2 * jj + 2, :], ACT.Exp,
                          scale=SCALE).then_inc(s["exp_out"], 1)
                elif kind == "mrows":
                    n = nth[i]
                    act.wait_ge(s["mrows_ready"], n + 1)
                    if n >= 2:
                        act.wait_ge(s[f"mrows_in{n % 2}"], 64 * (n // 2))
                    nc.scalar.copy(mT[:, n % 2, :], MB16[0:PARTS * HEADS, 0:L]).then_inc(s["mT_out"], 1)
                elif kind == "gather":
                    n = nth[i]
                    unit_n = last_round(steps, step)
                    act.wait_ge(s["u_ready"], unit_n + 1)
                    if n >= 2:
                        act.wait_ge(s["nat_ready"], n - 1)
                    nc.scalar.copy(U[:, n % 2, :], UP[:, :]).then_inc(s["u_out"], 1)
                elif kind == "turn":
                    act.wait_ge(s["turn_ready"], nth[i] + 1)
                    if nth[i]:
                        act.wait_ge(s["proj_ready"], nth[i])
                    nc.scalar.copy(OT[:, :], MB[:, :]).then_inc(s["oT_out"], 1)
                elif kind == "queries":
                    b = step[1]
                    act.wait_ge(s["qx_ready"], b + 1)
                    if b:
                        act.wait_ge(s["strips_w2"], 16 * b)
                    else:
                        act.wait_ge(s["strips_w"], 32 * B)
                    first_part(MB[:, :], ve("ca_qb"), 0, L, s["qx1_out"])

            NF = DFF // P
            act.wait_ge(s["nT_ready"], 2)
            a(xnT[:, 1, :], bank(1, 1), ACT.Identity, bias=lnB[:, 1, 1:2], scale=lnA[:, 1, 1:2]).then_inc(s["nT_out1"], 1)
            for b in range(B):
                for c in range(NF):
                    act.wait_ge(s["f_ready"], b * NF + c + 1)
                    a(hT[:, b, c, :], bank(b, c), ACT.Gelu, bias=ve("ffn_b1", c)).then_inc(s["f_out"], 1)
            act.wait_ge(s["nT_ready"], B + 2)
            a(xnT[:, 1, :], bank(1, 1), ACT.Identity, bias=ve("ln_beta"), scale=ve("ln_gamma")).then_inc(s["nT_out1"], 1)
            for b in range(B):
                act.wait_ge(s["l_sub"], b + 1)
                a(s1[:, b, :, :], s1[:, b, :, :], ACT.Exp, scale=SCALE1).then_inc(s["l_exp"], 1)
            for b in range(B):
                act.wait_ge(s["l_pT"], b + 1)
                nc.scalar.copy(p1T[:, b, :], bank(b, 3)[0:LC, :]).then_inc(s["l_pT_out"], 1)
            for b in range(B):
                act.wait_ge(s["l_ev"], b + 1)
                nc.scalar.copy(evT[:, b, :], bank(b, 0)).then_inc(s["l_ev_out"], 1)
            for b in range(B):
                act.wait_ge(s["r_sub"], b + 1)
                a(lg[:, b, :, :], lg[:, b, :, :], ACT.Exp).then_inc(s["r_exp"], 1)
            NE = E * RC + 1
            for b in range(B):
                for c in range(NE):
                    act.wait_ge(s["e_ready"], b * NE + c + 1)
                    a(eh[:, b, c, :], bank(b, (0, 1, 3)[c % 3]), ACT.Silu, bias=hbias[:, c, b:b + 1]).then_inc(s["e_out"], 1)
            for b in range(B):
                act.wait_ge(s["g2_ready"], b + 1)
                a(gT[:, b, :], bank(b, 0), ACT.Sigmoid, bias=ve("gate_b2")).then_inc(s["g_out"], 1)

        @block.vector
        def _(dve):
            v = nc.vector
            dve.wait_ge(s["ld_x"], 16)
            for t in range(B * QT):
                v.bn_stats(stats[:, t, :], xn[:, t, :]).then_inc(s["bn_out"], 1)
            for t in range(B * QT):
                dve.wait_ge(s["bn_out"], t + 1)
                last = v.bn_aggr(mv[:, t, :], stats[:, t, :])
            last.then_inc(s["stats_out"], 1)
            dve.wait_ge(s["stats_out"], 1)
            v.tensor_scalar(rstd[:, :], mv[:, :, 1], EPS, None, ALU.add).then_inc(s["rstd_in"], 1)
            dve.wait_ge(s["aff_ready"], 1)
            modulation(dve, v, s, aff, lnA, lnB, MB[:, 0:2 * B], ve, 0, "aff1_b", "ln1_g", "ln1_b", s["aff_out"])
            dve.wait_ge(s["rstd_out"], 1)
            for t in range(B * QT):
                v.tensor_scalar(normed[:, t, :], xn[:, t, :], mv[:, t, 0:1], rstd[:, t:t + 1],
                                ALU.subtract, ALU.mult).then_inc(s["normed_out"], 1)
            dve.wait_ge(s["normT_ready"], 1)
            dve.wait_ge(s["aff_out"], 1)
            v.tensor_scalar(xnT[:, 0, :], ST[:, 0, :], lnA[:, 0, 0:1], lnB[:, 0, 0:1], ALU.mult, ALU.add).then_inc(s["xnT_out0"], 1)

            def remainder(ps, bias, slot, n, first, out_sem):
                dve.wait_ge(*first)
                v.scalar_tensor_tensor(rest[:, slot, 0:n], ps, bias, part[:, slot, 0, 0:n], ALU.add,
                                       ALU.subtract).then_inc(out_sem, 1)

            for b in range(B):
                if b:
                    dve.wait_ge(s["q23_out"], 2 * b)
                remainder(ST[:, 2, :] if b else S[:, 0, :], ve("sa_qb"), 0, L, (s["q1_out"], b + 1), s["rest_q"])
                if b:
                    dve.wait_ge(s["k23_out"], 2 * b)
                remainder(ST[:, 3, :] if b else S[:, 1, :], ve("sa_kb"), 1, L, (s["k1_out"], b + 1), s["rest_k"])
            dve.wait_ge(s["k23_out"], 2 * B)
            dve.wait_ge(s["kT1_out"], 1)
            remainder(MB[:, 0:B * LC], ve("ca_kb"), 1, B * LC, (s["kx1_out"], 1), s["kx_rest"])
            dve.wait_ge(s["small_ready"], 1)
            v.tensor_copy(kfold[:, :], ST[:, 1, 0:B * LC]).then_inc(s["kfold_out"], 1)
            at = B * LC
            modulation(dve, v, s, aff, lnA, lnB, ST[:, 1, at:at + 2 * B], ve, 1, "aff2_b", "ln2_g", "ln2_b", s["aff_out"])
            at += 2 * B
            v.tensor_tensor(csa[:, 0:1], ST[:, 1, at:at + 1], ve("sa_ob"), ALU.add)
            v.tensor_tensor(csa[:, 1:2], ST[:, 1, at + 1:at + 2], ve("ca_ob"), ALU.add)
            at += 2
            NE = E * RC + 1
            for b in range(B):
                hp = ST[:, 1, at:at + B * NE].rearrange("p (c b) -> p c b", b=B)
                v.tensor_tensor(hbias[:, 0:NE - 1, b], hp[:, 0:NE - 1, b], ve("e_b1", 0, NE - 1), ALU.add)
                v.tensor_tensor(hbias[:, NE - 1:NE, b], hp[:, NE - 1:NE, b], ve("gate_b1"), ALU.add)
            at += B * NE
            v.tensor_copy(rbias[:, :, :], ST[:, 1, at:at + B * E].rearrange("p (b e) -> p b e", b=B)).then_inc(s["small_out"], 1)

            for i, step in enumerate(steps):
                kind = step[0]
                if kind == "maxima":
                    k, b, g, c = step[1]
                    n = event_at[step[1]]
                    slot = split_nth[(k, b, g)] % RING
                    if k == SELF:
                        for jj in range(2):
                            for p in range(2):
                                dve.wait_ge(s["s_ready"], n + 1)
                                v.tensor_reduce(negm[:, slot, c, 2 * jj + p:2 * jj + p + 1], S[:, n % 2, :], AX.X,
                                                ALU.max, negate=True).then_inc(s["max_out"], 1)
                                n += 1
                    else:
                        for p in range(2):
                            dve.wait_ge(s["s_ready"], n + 1)
                            v.tensor_reduce(negm[:, slot, 2 * c:2 * c + 2, :].rearrange("p t (jj q) -> p t jj q", q=2)[:, :, :, p],
                                            S[:, n % 2, 0:4 * LC].rearrange("p (t jj k) -> p t jj k", t=2, jj=2), AX.X,
                                            ALU.max, negate=True).then_inc(s["max_out"], 1)
                            n += 1
                elif kind == "split":
                    n = nth[i]
                    sl = n % RING
                    k, b, g = step[1:]
                    final = (k, b, g, QT - 1 if k == SELF else 1)
                    dve.wait_ge(s["max_out"], event_at[final] + (4 if k == SELF else 2))
                    if n >= RING:
                        dve.wait_ge(s["mrows_ready"], n - RING + 1)
                    v.tensor_copy(mpart[:, sl, :, 0, :], negm[:, sl, :, :]).then_inc(s["mp1"], 1)
                    dve.wait_ge(s["mp1"], 2 * n + 1)
                    v.tensor_tensor(mrest[:, sl, :, :], negm[:, sl, :, :], mpart[:, sl, :, 0, :], ALU.subtract).then_inc(s["mp1"], 1)
                    dve.wait_ge(s["mp1"], 2 * n + 2)
                    v.tensor_copy(mpart[:, sl, :, 1, :], mrest[:, sl, :, :]).then_inc(s["mp2"], 1)
                    dve.wait_ge(s["mp2"], n + 1)
                    v.tensor_tensor(mpart[:, sl, :, 2, :], mrest[:, sl, :, :], mpart[:, sl, :, 1, :], ALU.subtract).then_inc(s["mparts"], 1)
                elif kind == "natural":
                    n = nth[i]
                    k, b, r = step[1:]
                    dve.wait_ge(s["nat_ready"], n + 1)
                    t4 = MB[:, :].rearrange("p (t j s c) -> p t j s c", t=QT, j=HEADS, s=2)
                    v.reciprocal(rden[:, n % 2, :, :], MB[:, :].rearrange("p (t js c) -> p t js c", t=QT, c=16)[:, :, :, DH]).then_inc(s["rden_out"], 1)
                    dve.wait_ge(s["rden_out"], n + 1)
                    if r == 0 and n >= 2:
                        dve.wait_ge(s["turn_ready"], n // 2)
                    for sl in range(2):
                        o = O[:, :, :].rearrange("p t (r s j d) -> p t r s j d", r=2, s=2, j=HEADS)[:, :, r, sl, :, :]
                        rd = rden[:, n % 2, :, :].rearrange("p t (j s) -> p t j s", s=2)[:, :, :, sl]
                        last = v.tensor_tensor(o, t4[:, :, :, sl, 0:DH],
                                               rd.unsqueeze(3).to_broadcast([P, QT, HEADS, DH]), ALU.mult)
                    last.then_inc(s["o_out"], 1)
                elif kind == "project":
                    k, b = step[1:]
                    n = nth[i]
                    dve.wait_ge(s["proj_ready"], n + 1)
                    if n == 0:
                        dve.wait_ge(s["ld_xT"], 16)
                    v.scalar_tensor_tensor(xT[:, b, :], MB[:, :], csa[:, k:k + 1], xT[:, b, :], ALU.add, ALU.add).then_inc(s["x_out"], 1)
                elif kind == "queries":
                    b = step[1]
                    if b:
                        dve.wait_ge(s["qx23_out"], 2 * b)
                    else:
                        dve.wait_ge(s["q23_out"], 2 * B)
                    remainder(MB[:, :], ve("ca_qb"), 0, L, (s["qx1_out"], b + 1), s["rest_qx"])

            def norm_stats(site, b):
                n = site * B + b
                dve.wait_ge(s["n_ready"], n + 1)
                for t in range(QT):
                    last = v.bn_stats(stats[:, b * QT + t, :], bank(b, 0)[:, t * P:(t + 1) * P])
                last.then_inc(s["n_stats"], 1)
                dve.wait_ge(s["n_stats"], n + 1)
                for t in range(QT):
                    last = v.bn_aggr(mv[:, b * QT + t, :], stats[:, b * QT + t, :])
                last.then_inc(s["n_aggr"], 1)
                dve.wait_ge(s["n_aggr"], n + 1)
                v.tensor_scalar(rstd[:, b * QT:(b + 1) * QT], mv[:, b * QT:(b + 1) * QT, 1], EPS, None, ALU.add).then_inc(s["n_var"], 1)

            def norm_apply(site, b):
                n = site * B + b
                dve.wait_ge(s["n_rstd"], n + 1)
                for t in range(QT):
                    k = b * QT + t
                    last = v.tensor_scalar(normed[:, k, :], bank(b, 0)[:, t * P:(t + 1) * P], mv[:, k, 0:1],
                                           rstd[:, k:k + 1], ALU.subtract, ALU.mult)
                last.then_inc(s["n_normed"], 1)

            for b in range(B):
                norm_stats(0, b)
            for b in range(B):
                norm_apply(0, b)
            dve.wait_ge(s["nT_ready"], 1)
            v.tensor_scalar(xnT[:, 0, :], bank(0, 1), lnA[:, 1, 0:1], lnB[:, 1, 0:1], ALU.mult, ALU.add).then_inc(s["nT_out0"], 1)
            for b in range(B):
                dve.wait_ge(s["f2_ready"], b + 1)
                v.scalar_tensor_tensor(xT[:, b, :], bank(b, 3), ve("ffn_b2"), xT[:, b, :], ALU.add, ALU.add).then_inc(s["x3_out"], 1)
            for b in range(B):
                norm_stats(1, b)
            for b in range(B):
                norm_apply(1, b)
            dve.wait_ge(s["nT_ready"], B + 1)
            v.tensor_scalar(xnT[:, 0, :], bank(0, 1), ve("ln_gamma"), ve("ln_beta"), ALU.mult, ALU.add).then_inc(s["nT_out0"], 1)
            for b in range(B):
                sc = bank(b, 2)[:, 0:QT * LC].rearrange("p (t k) -> p t k", t=QT)
                dve.wait_ge(s["l_s_ready"], b + 1)
                v.tensor_reduce(mx1[:, b, :], sc, AX.X, ALU.max).then_inc(s["l_max"], 1)
                dve.wait_ge(s["l_max"], b + 1)
                v.tensor_tensor(s1[:, b, :, :], sc, mx1[:, b, :].unsqueeze(2).to_broadcast([P, QT, LC]), ALU.subtract).then_inc(s["l_sub"], 1)
            for b in range(B):
                dve.wait_ge(s["l_exp"], b + 1)
                v.tensor_reduce(sum1[:, b, :], s1[:, b, :, :], AX.X, ALU.add).then_inc(s["l_sum"], 1)
                dve.wait_ge(s["l_sum"], b + 1)
                v.reciprocal(rec1[:, b, :], sum1[:, b, :]).then_inc(s["l_rec"], 1)
                dve.wait_ge(s["l_rec"], b + 1)
                v.tensor_tensor(s1[:, b, :, :], s1[:, b, :, :], rec1[:, b, :].unsqueeze(2).to_broadcast([P, QT, LC]), ALU.mult).then_inc(s["l_p"], 1)
            for b in range(B):
                dve.wait_ge(s["r_ready"], b + 1)
                v.tensor_tensor(lg[:, b, :, :], bank(b, 2)[:, 0:QT * E].rearrange("p (t e) -> p t e", t=QT),
                                rbias[:, b, :].unsqueeze(1).to_broadcast([P, QT, E]), ALU.add).then_inc(s["r_lg"], 1)
                dve.wait_ge(s["r_lg"], b + 1)
                v.tensor_reduce(rmx[:, b, :], lg[:, b, :, :], AX.X, ALU.max).then_inc(s["r_mx"], 1)
                dve.wait_ge(s["r_mx"], b + 1)
                v.tensor_tensor(lg[:, b, :, :], lg[:, b, :, :], rmx[:, b, :].unsqueeze(2).to_broadcast([P, QT, E]), ALU.subtract).then_inc(s["r_sub"], 1)
            for b in range(B):
                dve.wait_ge(s["r_exp"], b + 1)
                v.tensor_reduce(rsum[:, b, :], lg[:, b, :, :], AX.X, ALU.add).then_inc(s["r_sum"], 1)
                dve.wait_ge(s["r_sum"], b + 1)
                v.reciprocal(rrec[:, b, :], rsum[:, b, :]).then_inc(s["r_rec"], 1)
                dve.wait_ge(s["r_rec"], b + 1)
                v.tensor_tensor(lg[:, b, :, :], lg[:, b, :, :], rrec[:, b, :].unsqueeze(2).to_broadcast([P, QT, E]), ALU.mult).then_inc(s["r_p"], 1)
            for b in range(B):
                dve.wait_ge(s["r_pT"], b + 1)
                v.tensor_copy(prT[:, b, :], bank(b, 2)[0:E, :]).then_inc(s["r_pT_out"], 1)
            for b in range(B):
                for e in range(E):
                    dve.wait_ge(s["pb_ready"], b * E + e + 1)
                    for c in range(RC):
                        k = e * RC + c
                        v.tensor_tensor(eh[:, b, k, :], eh[:, b, k, :], bank(b, e), ALU.mult).then_inc(s["e_scaled"], 1)
                dve.wait_ge(s["e2_ready"], b + 1)
                v.tensor_copy(rtT[:, b, :], bank(b, 3)).then_inc(s["rt_out"], 1)
                dve.wait_ge(s["d_ready"], b + 1)
                dve.wait_ge(s["g_out"], b + 1)
                v.scalar_tensor_tensor(dT[:, b, :], bank(b, 1), ve("out_b"), gT[:, b, :], ALU.add, ALU.mult).then_inc(s["d_out"], 1)
                dve.wait_ge(s["d_out"], b + 1)
                v.tensor_tensor(dT[:, b, :], dT[:, b, :], xT[:, b, :], ALU.add).then_inc(s["y_out"], 1)


def e_w1(wl, c, part):
    if c == E * RC:
        return wl("gate_w1", part)
    return wl("e_w1", (part * E + c // RC) * RC + c % RC)


def router_w(w_late, part):
    at = LATE_AT["router_W"] + part * E
    return w_late[:, at:at + E]


def last_round(steps, gather):
    _, kind, b, r = gather
    return max(s[3] for s in steps if s[0] == "values" and s[1] == (kind, b, 2 * r + 1))


def modulation(dve, v, s, aff, lnA, lnB, ps, ve, site, bias, g, bb, out_sem):
    for i in range(2):
        last = v.tensor_scalar(aff[:, site, i, :], ps[:, B * i:B * i + B], ve(bias, i), None, ALU.add)
    last.then_inc(s["mod_step"], 1)
    dve.wait_ge(s["mod_step"], 2 * site + 1)
    v.tensor_scalar(lnA[:, site, :], aff[:, site, 0, :], ve(g), None, ALU.mult)
    v.tensor_scalar(lnB[:, site, :], aff[:, site, 0, :], ve(bb), None, ALU.mult).then_inc(s["mod_step"], 1)
    dve.wait_ge(s["mod_step"], 2 * site + 2)
    v.tensor_tensor(lnB[:, site, :], lnB[:, site, :], aff[:, site, 1, :], ALU.add).then_inc(out_sem, 1)


def kernel(**inputs):
    import numpy as np
    import concourse.bacc as bacc
    from concourse.bass_utils import run_bass_kernel_spmd as run

    a = {k.replace("L0_xcond_", "").replace("L1_xcond_", ""): np.asarray(v) for k, v in inputs.items()}

    def wide(w):
        n = w.shape[0] // P
        return w.reshape(n, P, -1).transpose(1, 0, 2).reshape(P, -1)

    vec = np.concatenate([(a["cond_1024"] if n == "cond" else a[n]).reshape(k, P).T for n, k in VECTORS], axis=1)
    late = dict(a, ctxT=a["ctx_1024"].reshape(B * LC, D).T, WqT=a["Wq"].T, ffn_w2=wide(a["ffn_w2"]),
                router_W=wide(a["router_W"]), gate_w1=wide(a["gate_w1"]),
                e_w1=a["e_w1"].reshape(E, 3, P, RH).transpose(2, 1, 0, 3).reshape(P, -1),
                e_w2=wide(a["e_w2"].reshape(E * RH, D)))
    feeds = {
        "x_nat": a["x"].reshape(B * QT, P, D).transpose(1, 0, 2),
        "x_T": a["x"].transpose(2, 0, 1),
        "early": np.concatenate([vec if n == "vec" else a[n] for n, _ in EARLY], axis=1),
        "late": np.concatenate([late[n] for n, _ in LATE], axis=1),
        "router_b": a["router_b"].reshape(1, E),
        "e_b2": a["e_b2"],
    }
    feeds = {k: np.ascontiguousarray(v) for k, v in feeds.items()}
    nc = bacc.Bacc("TRN2", target_bir_lowering=False, num_devices=1)
    args = [nc.dram_tensor(k, v.shape, mybir.dt.from_np(v.dtype), kind="ExternalInput").ap() for k, v in feeds.items()]
    out = nc.dram_tensor("out_T", (B, D, L), F32, kind="ExternalOutput").ap()
    block_program(nc, *args, out)
    got = run(nc, [feeds], core_ids=[0]).results[0]["out_T"]
    return np.ascontiguousarray(got.transpose(0, 2, 1))
```

```python
from contextlib import ExitStack

import concourse.bass as bass
from concourse import mybir

F32 = mybir.dt.float32
BF16 = mybir.dt.bfloat16
ALU = mybir.AluOpType
ACT = mybir.ActivationFunctionType
AX = mybir.AxisListType

B, L, D = 2, 512, 128
H, DH = 16, 8
LC = 77
DFF = 512
P = 128
QT = L // P
E, RH = 3, 256
RC = RH // P
EPS = 1e-5
SCALE = 1.0 / (DH ** 0.5)
SCALE1 = D ** -0.5
HEADS = 4
GROUPS = H // HEADS
PARTS = 3
Q_RUNS = [(0, 3), (1, 2), (2, 1)]
K_RUNS = [(None, 3), (None, 2), (None, 1)]
STACK_DMAS = 16 * 3
STRIP_DMAS = 16 * 2
STACK = 6 * DH
STRIP = 64

VECTORS = [("ln1_g", 1), ("ln1_b", 1), ("aff1_b", 2), ("ln2_g", 1), ("ln2_b", 1), ("aff2_b", 2),
           ("sa_qb", 1), ("sa_kb", 1), ("sa_vb", 1), ("sa_ob", 1), ("ca_qb", 1), ("ca_kb", 1),
           ("ca_vb", 1), ("ca_ob", 1), ("ffn_b1", DFF // P), ("ffn_b2", 1), ("ln_gamma", 1),
           ("ln_beta", 1), ("e_b1", E * RC), ("gate_b1", 1), ("gate_b2", 1), ("out_b", 1),
           ("cond", B)]
EARLY = [("vec", sum(n for _, n in VECTORS)), ("aff1_w", 2 * D), ("sa_qw", D), ("sa_kw", D),
         ("sa_vw", D)]
LATE = [("ctxT", B * LC), ("ca_kw", D), ("ca_vw", D), ("Wk", D), ("WqT", D), ("Wv", D),
        ("sa_ow", D), ("ca_qw", D), ("ca_ow", D), ("aff2_w", 2 * D), ("ffn_w1", DFF),
        ("ffn_w2", DFF), ("router_W", 3 * E), ("e_w1", 3 * E * RH), ("e_w2", E * RC * D),
        ("gate_w1", 3 * D), ("gate_w2", D), ("out_w", D)]


def places(fields):
    at, out = 0, {}
    for name, n in fields:
        out[name] = at
        at += n
    return out, at


VEC_AT, _ = places(VECTORS)
EARLY_AT, EARLY_N = places(EARLY)
LATE_AT, LATE_N = places(LATE)

SELF, CROSS = 0, 1
TWO_ONES = 1 + 0x3F80 / 2 ** 23
EVENTS = (4 * QT, 4)
WARM = 8
ROUND = ("M", 0, "M", "V", "M", 1, "M")
RING = GROUPS


def plan():
    steps = []
    units = [(kind, b, g) for kind in (SELF, CROSS) for b in range(B) for g in range(GROUPS)]
    rounds = [(u, kt) for u in units for kt in range(QT if u[0] == SELF else 1)]
    todo = [(u, e) for u in units for e in range(EVENTS[u[0]])]
    due = {}
    reach = 2 * GROUPS

    def maxima(last_unit):
        if todo and units.index(todo[0][0]) < last_unit:
            u, e = todo.pop(0)
            steps.append(("maxima", u, e))
            if e == EVENTS[u[0]] - 1:
                steps.append(("split",) + u)

    def put(n, place, step):
        due.setdefault((n, place), []).append(step)

    for _ in range(EVENTS[SELF]):
        maxima(1)
    steps.append(("mrows",) + units[0])
    for _ in range(WARM):
        maxima(2)
        steps.append(("warm",))
    for n, (unit, kt) in enumerate(rounds):
        kind, b, g = unit
        at = units.index(unit)
        last = kt == (QT if kind == SELF else 1) - 1
        if kind == SELF and kt == 2 and units[at + 1][0] == SELF:
            put(n, 4, ("mrows",) + units[at + 1])
        if kind == CROSS:
            while todo and units.index(todo[0][0]) <= at:
                maxima(at + 1)
            steps.append(("mrows",) + unit)
        if last and g % 2 == 1:
            r = g // 2
            put(n + 1, 4, ("gather", kind, b, r))
            put(n + 2, 0, ("natural", kind, b, r))
            put(n + 2, 1, ("normalise", kind, b, r))
            if r == 1:
                put(n + 2, 5, ("turn", kind, b))
                put(n + 3, 2, ("project", kind, b))
                put(n + 3, 3, ("residual", kind, b))
                if kind == SELF:
                    put(n + 3, 6, ("queries", b))
                    put(n + 4, 1, ("rests", b))
                    put(n + 5, 6, ("reach", (3 + b) * GROUPS))
        for place, token in enumerate(ROUND):
            for step in due.pop((n, place), []):
                if step[0] == "reach":
                    reach = step[1]
                else:
                    steps.append(step)
            if token == "M":
                maxima(reach)
            elif token == "V" and n:
                steps.append(("values",) + rounds[n - 1] + (n - 1,))
            elif token == "V":
                steps.extend([("warm",)] * 2)
            else:
                steps.append(("scores", unit, kt, n, token))
                steps.append(("exps", unit, kt, n, token))
    steps.append(("values",) + rounds[-1] + (len(rounds) - 1,))
    for where in sorted(due):
        steps.extend(due[where])
    return steps


def counts(steps):
    seen, out = {}, []
    for s in steps:
        k = s[0]
        out.append(seen.get(k, 0))
        seen[k] = out[-1] + 1
    return out


def block_program(nc, x_nat, x_T, early, late, router_b, e_b2, out_T):
    steps = plan()
    nth = counts(steps)
    TURNS = {"mrows": "mT_out", "natural": "o_out", "turn": "oT_out", "project": "x_out",
             "queries": "rest_qx"}
    bank_reader, before = [], None
    for st, n in zip(steps, nth):
        bank_reader.append(before)
        if st[0] in TURNS:
            before = (TURNS[st[0]], n + 1)
    event_at, ev = {}, 0
    for s in steps:
        if s[0] == "maxima":
            event_at[s[1:]] = ev
            ev += 1
    split_nth = {s[1:]: nth[i] for i, s in enumerate(steps) if s[0] == "split"}
    mrows_nth = {s[1:]: nth[i] for i, s in enumerate(steps) if s[0] == "mrows"}
    queries_nth = {s[1]: nth[i] for i, s in enumerate(steps) if s[0] == "queries"}

    with ExitStack() as ctx:
        def sb(name, shape, dt=F32):
            return ctx.enter_context(nc.sbuf_tensor(name, shape, dt))

        def psum(name, shape, dt=F32):
            return ctx.enter_context(nc.psum_tensor(name, shape, dt))

        def sem(name):
            return ctx.enter_context(nc.semaphore(name))

        xn = sb("xn", [P, B * QT, D])
        xT = sb("xT", [P, B, L])
        w_early = sb("w_early", [P, EARLY_N])
        w_late = sb("w_late", [P, LATE_N])
        rb_row = sb("rb_row", [1, E])
        b2_rows = sb("b2_rows", [E, D])
        ident = sb("ident", [P, P])
        ident16 = sb("ident16", [P, P], BF16)
        ones_row = sb("ones_row", [1, P])
        pick = sb("pick", [E, E, P])
        half = sb("half", [P, B * QT])
        stats = sb("stats", [P, B * QT, 6])
        mv = sb("mv", [P, B * QT, 2])
        rstd = sb("rstd", [P, B * QT])
        aff = sb("aff", [P, 2, 2, B])
        lnA = sb("lnA", [P, 2, B])
        lnB = sb("lnB", [P, 2, B])
        normed = sb("normed", [P, B * QT, D])
        xnT = sb("xnT", [P, B, L])
        QS = sb("QS", [P, B, H // 2, L], BF16)
        KS = sb("KS", [P, B, H // 2, L], BF16)
        QX = sb("QX", [P, B, H // 2, L], BF16)
        KX = sb("KX", [P, H // 2, B * LC], BF16)
        part = sb("part", [P, 2, PARTS, L], BF16)
        rest = sb("rest", [P, 2, L])
        partx = sb("partx", [P, PARTS, B * LC], BF16)
        restx = sb("restx", [P, B * LC])
        VS = sb("VS", [P, B * QT, H, 32])
        VX = sb("VX", [LC, B, H, 32])
        PT = sb("PT", [P, 2, HEADS, L])
        negm = sb("negm", [P, RING, QT, 2, 2])
        mrest = sb("mrest", [P, RING, QT, 2, 2])
        mpart = sb("mpart", [P, RING, QT, 2, PARTS, 2], BF16)
        mT = sb("mT", [PARTS * HEADS, 2, L], BF16)
        U = sb("U", [P, 2, L])
        rden = sb("rden", [P, 2, QT, 8])
        O = sb("O", [P, QT, D])
        OT = sb("OT", [P, L])
        csa = sb("csa", [P, 2])
        kT1 = sb("kT1", [P, B * LC])
        kfold = sb("kfold", [P, B * LC])
        v1 = sb("v1", [LC, B, D])
        hbias = sb("hbias", [P, E * RC + 1, B])
        rbias = sb("rbias", [P, B, E])
        hT = VS[:, :, :, :].rearrange("p (b a) h c -> p b (a h c)", b=B).rearrange("p b (f t) -> p b f t", t=L)
        s1 = sb("s1", [P, B, QT, LC])
        mx1 = sb("mx1", [P, B, QT])
        sum1 = sb("sum1", [P, B, QT])
        rec1 = sb("rec1", [P, B, QT])
        p1T = sb("p1T", [LC, B, L])
        evT = sb("evT", [P, B, L])
        lg = sb("lg", [P, B, QT, E])
        rmx = sb("rmx", [P, B, QT])
        rsum = sb("rsum", [P, B, QT])
        rrec = sb("rrec", [P, B, QT])
        prT = sb("prT", [E, B, L])
        eh = sb("eh", [P, B, E * RC + 1, L])
        rtT = PT[:, 0, 0:2, :]
        gT = PT[:, 0, 2:4, :]
        dT = PT[:, 1, 0:2, :]

        S = psum("S", [P, 2, 512])
        ST = psum("ST", [P, 4, 512])
        UP = psum("UP", [P, 512])
        MB = psum("MB", [P, 512])
        MB16 = MB[:, :].bitcast(BF16)
        def bank(b, i):
            n = 4 * b + i
            if n < 4:
                return ST[:, n, :]
            return [S[:, 0, :], S[:, 1, :], UP[:, :], MB[:, :]][n - 4]

        scr_q = nc.dram_tensor("scr_q", [2 * B, 6, P, L], BF16, kind="Internal").ap()
        scr_k = nc.dram_tensor("scr_k", [B, 6, P, L], BF16, kind="Internal").ap()
        scr_kx = nc.dram_tensor("scr_kx", [6, P, B * LC], BF16, kind="Internal").ap()

        def ve(name, i=0, n=1):
            at = EARLY_AT["vec"] + VEC_AT[name] + i
            return w_early[:, at:at + n]

        def we(name, i=0, n=D):
            at = EARLY_AT[name] + i * D
            return w_early[:, at:at + n]

        def wl(name, i=0, n=D):
            at = LATE_AT[name] + i * D
            return w_late[:, at:at + n]

        names = """ld_x ld_early ld_xT ld_late ld_small consts ones_set zeros_set
            aff_ready aff_out stats_out rstd_in rstd_out bn_out normed_out normT_ready xnT_out0 xnT_out1
            q_ready k_ready v_ready q1_out k1_out v_out q2_out k2_out rest_q rest_k q3_out k3_out
            stack_q0 stack_q1 stack_k0 stack_k1 stack_qx0 stack_qx1 stack_kx strips_0 strips_1 strips_qx0 strips_qx1
            ctx_ready ctx_v_ready kx1_out kx_rest kx2_out kx3_out strips_kx vx_out kT1_out v1_out
            mod_step kfold_out small_ready small_out
            s_ready max_out negm_out mp1 mp2 mparts mrows_ready mT_out mrows_in0 mrows_in1
            st_ready exp_out u_ready u_out nat_ready rden_out o_out turn_ready oT_out
            proj_ready x_out qx_ready qx1_out rest_qx qx2_out qx3_out
            n_ready n_stats n_aggr n_var n_rstd n_normed nT_ready nT_out0 nT_out1
            f_ready f_out f2_ready x3_out l_s_ready l_max l_sub l_exp l_sum l_rec l_p l_pT l_pT_out
            l_ev l_ev_out r_ready r_lg r_mx r_sub r_exp r_sum r_rec r_p r_pT r_pT_out
            e_ready e_out pb_ready e_scaled e2_ready rt_out g2_ready g_out d_ready d_out y_out
            stored""".split()
        s = {n: sem(n) for n in names}

        block = ctx.enter_context(nc.Block())

        @block.sync
        def _(sp):
            sp.dma_start(xn[:, :, :], x_nat).then_inc(s["ld_x"], 16)
            sp.dma_start(w_early[:, :], early).then_inc(s["ld_early"], 16)
            sp.dma_start(w_late[:, :], late).then_inc(s["ld_late"], 16)
            sp.dma_start(xT[:, :, :], x_T).then_inc(s["ld_xT"], 16)
            sp.dma_start(rb_row[:, :], router_b).then_inc(s["ld_small"], 16)
            sp.dma_start(b2_rows[:, :], e_b2).then_inc(s["ld_small"], 16)

            def stack(scr, dense, runs, done):
                at = 0
                for first, times in runs:
                    if first is None:
                        src = dense[:, 0:times, :]
                    else:
                        src = dense[:, first:first + 1, :].to_broadcast([P, times, dense.shape[2]])
                    sp.dma_start(scr[at:at + times].rearrange("i p t -> p i t"), src).then_inc(done, 16)
                    at += times

            def strips(dst, scr, done):
                for q in range(2):
                    sp.dma_start(dst[STRIP * q:STRIP * q + STACK].rearrange("p k t -> p (k t)"),
                                 scr[:, 64 * q:64 * q + 64, :].rearrange("i (d k) t -> i d (k t)", d=DH)
                                 ).then_inc(done, 16)

            for b in range(B):
                sp.wait_ge(s["q3_out"], b + 1)
                stack(scr_q[b], part[:, 0, :, :], Q_RUNS, s[f"stack_q{b}"])
                sp.wait_ge(s["k3_out"], b + 1)
                stack(scr_k[b], part[:, 1, :, :], K_RUNS, s[f"stack_k{b}"])
                if b == 0:
                    sp.wait_ge(s["ones_set"], 2)
                sp.wait_ge(s[f"stack_q{b}"], STACK_DMAS)
                strips(QS[:, b, :, :], scr_q[b], s[f"strips_{b}"])
                sp.wait_ge(s[f"stack_k{b}"], STACK_DMAS)
                strips(KS[:, b, :, :], scr_k[b], s[f"strips_{b}"])
                if b == 0:
                    sp.wait_ge(s["kx3_out"], 1)
                    stack(scr_kx, partx[:, :, :], K_RUNS, s["stack_kx"])
            sp.wait_ge(s["stack_kx"], STACK_DMAS)
            strips(KX[:, :, :], scr_kx, s["strips_kx"])

            for i, step in enumerate(steps):
                if step[0] == "mrows":
                    kind, b, g = step[1:]
                    n = nth[i]
                    sp.wait_ge(s["mT_out"], n + 1)
                    dst = QS if kind == SELF else QX
                    for q in range(2):
                        row = STRIP * q + STACK
                        sp.dma_start(dst[row:row + PARTS, b, 2 * g:2 * g + 2, :],
                                     mT[2 * PARTS * q:2 * PARTS * (q + 1), n % 2, :]
                                     ).then_inc(s[f"mrows_in{n % 2}"], 16)
                elif step[0] == "queries":
                    b = step[1]
                    sp.wait_ge(s["qx3_out"], b + 1)
                    stack(scr_q[B + b], part[:, 0, :, :], Q_RUNS, s[f"stack_qx{b}"])
                    sp.wait_ge(s[f"stack_qx{b}"], STACK_DMAS)
                    strips(QX[:, b, :, :], scr_q[B + b], s[f"strips_qx{b}"])
            for b in range(B):
                sp.wait_ge(s["y_out"], b + 1)
                sp.dma_start(out_T[b], dT[:, b, :]).then_inc(s["stored"], 16)
            sp.wait_ge(s["stored"], 16 * B)

        

        @block.gpsimd
        def _(pool):
            g = nc.gpsimd
            g.memset(ident[:, :], 0.0).then_inc(s["zeros_set"], 1)
            g.memset(ident16[:, :], 0.0).then_inc(s["zeros_set"], 1)
            g.memset(pick[:, :, :], 0.0).then_inc(s["zeros_set"], 1)
            g.memset(half[:, :], -0.5).then_inc(s["zeros_set"], 1)
            g.memset(ones_row[:, :], 1.0).then_inc(s["consts"], 1)
            pool.wait_ge(s["zeros_set"], 4)
            for t in (ident, ident16):
                g.affine_select(out=t[:, :], in_=t[:, :], compare_op=ALU.not_equal, fill=1.0, base=0,
                                pattern=[[-1, P]], channel_multiplier=1).then_inc(s["consts"], 1)
            g.affine_select(out=pick[:, :, :], in_=pick[:, :, :], compare_op=ALU.not_equal, fill=1.0,
                            base=0, pattern=[[-1, E], [0, P]], channel_multiplier=1).then_inc(s["consts"], 1)
            for t in (KS[:, :, :, :], KX[:, :, :]):
                g.memset(t.bitcast(F32), TWO_ONES).then_inc(s["ones_set"], 1)
            pool.wait_ge(s["rstd_in"], 1)
            g.tensor_tensor(rstd[:, :], rstd[:, :], half[:, :], ALU.pow).then_inc(s["rstd_out"], 1)
            g.memset(VS[:, :, :, :], 0.0).then_inc(s["ones_set"], 1)
            g.memset(VX[:, :, :, :], 0.0).then_inc(s["ones_set"], 1)
            pool.wait_ge(s["ones_set"], 4)
            for t, lead in ((VS, B * QT), (VX, B)):
                v = t[:, :, :, :].rearrange("p a (r s j) c -> p (a r) s j c", s=2, j=HEADS)
                for sl in range(2):
                    g.memset(v[:, :, sl, :, 16 * sl + DH], 1.0).then_inc(s["ones_set"], 1)
            for i, step in enumerate(steps):
                if step[0] == "split":
                    n = nth[i]
                    sl = n % RING
                    k, b, grp = step[1:]
                    pool.wait_ge(s["max_out"], event_at[(k, b, grp), EVENTS[k] - 1] + 1)
                    if n >= RING:
                        pool.wait_ge(s["mrows_ready"], n - RING + 1)
                    g.tensor_copy(mpart[:, sl, :, :, 0, :], negm[:, sl, :, :, :]).then_inc(s["mp1"], 1)
                    pool.wait_ge(s["mp1"], 2 * n + 1)
                    g.tensor_tensor(mrest[:, sl, :, :, :], negm[:, sl, :, :, :], mpart[:, sl, :, :, 0, :], ALU.subtract).then_inc(s["mp1"], 1)
                    pool.wait_ge(s["mp1"], 2 * n + 2)
                    g.tensor_copy(mpart[:, sl, :, :, 1, :], mrest[:, sl, :, :, :]).then_inc(s["mp2"], 1)
                    pool.wait_ge(s["mp2"], n + 1)
                    g.tensor_tensor(mpart[:, sl, :, :, 2, :], mrest[:, sl, :, :, :], mpart[:, sl, :, :, 1, :], ALU.subtract).then_inc(s["mparts"], 1)
            for site in range(2):
                for b in range(B):
                    n = site * B + b
                    pool.wait_ge(s["n_var"], n + 1)
                    g.tensor_tensor(rstd[:, b * QT:(b + 1) * QT], rstd[:, b * QT:(b + 1) * QT],
                                    half[:, b * QT:(b + 1) * QT], ALU.pow).then_inc(s["n_rstd"], 1)

        @block.tensor
        def _(pe):
            mm = nc.tensor.matmul
            pe.wait_ge(s["consts"], 4)
            pe.wait_ge(s["ld_early"], 16)
            cond = ve("cond", 0, B)
            for i in range(2):
                last = mm(MB[:, B * i:B * i + B], we("aff1_w", i), cond, start=True, stop=True)
            last.then_inc(s["aff_ready"], 1)
            for b in range(B):
                for t in range(QT):
                    pe.wait_ge(s["normed_out"], b * QT + t + 1)
                    last = nc.tensor.transpose(ST[:, b, t * P:(t + 1) * P], normed[:, b * QT + t, :], ident[:, :])
                last.then_inc(s["normT_ready"], 1)
            for b in range(B):
                pe.wait_ge(s[f"xnT_out{b}"], 1)
                mm(ST[:, 2 * b, :] if b else S[:, 0, :], we("sa_qw"), xnT[:, b, :], start=True, stop=True).then_inc(s["q_ready"], 1)
                mm(ST[:, 3, :] if b else S[:, 1, :], we("sa_kw"), xnT[:, b, :], start=True, stop=True).then_inc(s["k_ready"], 1)
                if b:
                    pe.wait_ge(s["v_out"], 2)
                for t in range(QT):
                    last = mm(UP[:, t * P:(t + 1) * P], xnT[:, b, t * P:(t + 1) * P], we("sa_vw"), start=True, stop=True)
                last.then_inc(s["v_ready"], 1)
            pe.wait_ge(s["ld_late"], 16)
            ctxT = wl("ctxT", 0, B * LC)
            pe.wait_ge(s["aff_out"], 1)
            mm(MB[:, 0:B * LC], wl("ca_kw"), ctxT, start=True, stop=True)
            mm(MB[:, B * LC:2 * B * LC], wl("Wk"), ctxT, start=True, stop=True).then_inc(s["ctx_ready"], 1)
            for b in range(B):
                c = ctxT[:, b * LC:(b + 1) * LC]
                mm(ST[0:LC, 0, b * D:(b + 1) * D], c, wl("ca_vw"), start=True, stop=True)
                last = mm(ST[0:LC, 0, (B + b) * D:(B + b + 1) * D], c, wl("Wv"), start=True, stop=True)
            last.then_inc(s["ctx_v_ready"], 1)
            pe.wait_ge(s["kT1_out"], 1)
            mm(ST[:, 1, 0:B * LC], wl("WqT"), kT1[:, :], start=True, stop=True)
            at = B * LC
            for i in range(2):
                mm(ST[:, 1, at + B * i:at + B * i + B], wl("aff2_w", i), cond, start=True, stop=True)
            at += 2 * B
            mm(ST[:, 1, at:at + 1], wl("sa_ow"), ve("sa_vb"), start=True, stop=True)
            mm(ST[:, 1, at + 1:at + 2], wl("ca_ow"), ve("ca_vb"), start=True, stop=True)
            at += 2
            for c in range(E * RC + 1):
                w = e_w1(wl, c, 2)
                mm(ST[:, 1, at + B * c:at + B * c + B], w, cond, start=True, stop=True)
            at += B * (E * RC + 1)
            pe.wait_ge(s["ld_small"], 32)
            for b in range(B):
                o = ST[:, 1, at + E * b:at + E * b + E]
                mm(o, cond[:, b:b + 1].to_broadcast([P, P]), router_w(w_late, 2), start=True, stop=False)
                last = mm(o, ones_row[:, :], rb_row[:, :], start=False, stop=True)
            last.then_inc(s["small_ready"], 1)

            def maxima(unit, e):
                kind, b, g = unit
                n = event_at[unit, e]
                if n == 0:
                    pe.wait_ge(s["rest_q"], 1)
                    pe.wait_ge(s["rest_k"], 1)
                    pe.wait_ge(s["ones_set"], 8)
                if kind == SELF:
                    pe.wait_ge(s[f"strips_{b}"], 2 * STRIP_DMAS)
                else:
                    pe.wait_ge(s[f"strips_qx{b}"], STRIP_DMAS)
                    pe.wait_ge(s["strips_kx"], STRIP_DMAS)
                if n >= 2:
                    pe.wait_ge(s["max_out"], n - 1)
                p = e % 2
                r = slice(STRIP * p, STRIP * p + STACK)
                if kind == SELF:
                    i, jj = e // 4, e // 2 % 2
                    last = mm(S[:, n % 2, :], QS[r, b, 2 * g + jj, i * P:(i + 1) * P],
                              KS[r, b, 2 * g + jj, :], start=True, stop=True)
                else:
                    for t in range(2):
                        for jj in range(2):
                            q0 = (2 * (e // 2) + t) * P
                            last = mm(S[:, n % 2, (2 * t + jj) * LC:(2 * t + jj + 1) * LC],
                                      QX[r, b, 2 * g + jj, q0:q0 + P], KX[r, 2 * g + jj, b * LC:(b + 1) * LC],
                                      start=True, stop=True)
                last.then_inc(s["s_ready"], 1)

            def scores(unit, kt, n, jj):
                kind, b, g = unit
                if n == 0:
                    pe.wait_ge(s["rest_q"], B)
                    pe.wait_ge(s["rest_k"], B)
                    pe.wait_ge(s["small_out"], 1)
                    pe.wait_ge(s["v1_out"], 1)
                m = mrows_nth[unit]
                pe.wait_ge(s[f"mrows_in{m % 2}"], 32 * (m // 2 + 1))
                if n:
                    pe.wait_ge(s["exp_out"], 2 * (n - 1) + jj + 1)
                for p in range(2):
                    r = slice(STRIP * p, STRIP * p + STACK + PARTS)
                    if kind == SELF:
                        last = mm(ST[:, 2 * jj + p, :], KS[r, b, 2 * g + jj, kt * P:(kt + 1) * P],
                                  QS[r, b, 2 * g + jj, :], start=True, stop=True)
                    else:
                        last = mm(ST[0:LC, 2 * jj + p, :], KX[r, 2 * g + jj, b * LC:(b + 1) * LC],
                                  QX[r, b, 2 * g + jj, :], start=True, stop=True)
                last.then_inc(s["st_ready"], 1)

            def values(unit, kt, n):
                kind, b, g = unit
                nk = QT if kind == SELF else 1
                first = g % 2 == 0 and kt == 0
                final = g % 2 == 1 and kt == nk - 1
                w = (kind * B + b) * 2 + g // 2
                if first:
                    if w:
                        pe.wait_ge(s["u_out"], w)
                    else:
                        pe.wait_ge(s["v_out"], 2 * B)
                    if kind == CROSS:
                        pe.wait_ge(s["vx_out"], 2)
                pe.wait_ge(s["exp_out"], 2 * n + 2)
                for j in range(HEADS):
                    h = HEADS * g + j
                    if kind == SELF:
                        last = mm(UP[32 * j:32 * j + 32, :], VS[:, b * QT + kt, h, :], PT[:, n % 2, j, :],
                                  start=first, stop=final)
                    else:
                        last = mm(UP[32 * j:32 * j + 32, :], VX[:, b, h, :], PT[0:LC, n % 2, j, :],
                                  start=first, stop=final)
                last.then_inc(s["u_ready"], 1)

            for i, step in enumerate(steps):
                kind = step[0]
                if kind in TURNS and bank_reader[i]:
                    pe.wait_ge(s[bank_reader[i][0]], bank_reader[i][1])
                elif kind in TURNS:
                    pe.wait_ge(s["kT1_out"], 1)
                    pe.wait_ge(s["kx_rest"], 1)
                if kind == "maxima":
                    maxima(*step[1:])
                elif kind == "warm":
                    if nth[i] == 0:
                        pe.wait_ge(s["v_out"], 2 * B)
                        pe.wait_ge(s[f"strips_0"], 2 * STRIP_DMAS)
                    for _ in range(2):
                        mm(UP[:, :], KS[:, 0, 0, 0:P], KS[:, 0, 0, :], start=True, stop=True)
                elif kind == "scores":
                    scores(*step[1:])
                elif kind == "values":
                    values(*step[1:])
                elif kind == "mrows":
                    n = split_nth[step[1:]]
                    pe.wait_ge(s["mparts"], n + 1)
                    for t in range(QT):
                        last = nc.tensor.transpose(MB16[0:PARTS * HEADS, t * P:(t + 1) * P],
                                                   mpart[:, n % RING, t, :, :, :].rearrange("p q i j -> p (q i j)"), ident16[:, :])
                    last.then_inc(s["mrows_ready"], 1)
                elif kind == "natural":
                    n = nth[i]
                    pe.wait_ge(s["u_out"], n + 1)
                    for t in range(QT):
                        last = nc.tensor.transpose(MB[:, t * P:(t + 1) * P], U[:, n % 2, t * P:(t + 1) * P], ident[:, :])
                    last.then_inc(s["nat_ready"], 1)
                elif kind == "turn":
                    pe.wait_ge(s["o_out"], 2 * nth[i] + 2)
                    for t in range(QT):
                        last = nc.tensor.transpose(MB[:, t * P:(t + 1) * P], O[:, t, :], ident[:, :])
                    last.then_inc(s["turn_ready"], 1)
                elif kind == "project":
                    pe.wait_ge(s["oT_out"], nth[i] + 1)
                    mm(MB[:, :], wl("sa_ow" if step[1] == SELF else "ca_ow"), OT[:, :], start=True, stop=True).then_inc(s["proj_ready"], 1)
                elif kind == "queries":
                    b = step[1]
                    pe.wait_ge(s["x_out"], b + 1)
                    mm(MB[:, :], wl("ca_qw"), xT[:, b, :], start=True, stop=True).then_inc(s["qx_ready"], 1)

            def norm(site, b):
                n = site * B + b
                if site == 0:
                    pe.wait_ge(s["x_out"], B + B)
                else:
                    pe.wait_ge(s["x3_out"], b + 1)
                for t in range(QT):
                    last = nc.tensor.transpose(bank(b, 0)[:, t * P:(t + 1) * P], xT[:, b, t * P:(t + 1) * P], ident[:, :])
                last.then_inc(s["n_ready"], 1)

            def norm_back(site, b):
                n = site * B + b
                pe.wait_ge(s["n_normed"], n + 1)
                for t in range(QT):
                    last = nc.tensor.transpose(bank(b, 1)[:, t * P:(t + 1) * P], normed[:, b * QT + t, :], ident[:, :])
                last.then_inc(s["nT_ready"], 1)

            for b in range(B):
                norm(0, b)
            for b in range(B):
                norm_back(0, b)
            for b in range(B):
                pe.wait_ge(s[f"nT_out{b}"], 1)
                for c in range(DFF // P):
                    mm(bank(b, c), wl("ffn_w1", c), xnT[:, b, :], start=True, stop=True).then_inc(s["f_ready"], 1)
            for b in range(B):
                pe.wait_ge(s["f_out"], (DFF // P) * (b + 1))
                for c in range(DFF // P):
                    last = mm(bank(b, 3), wl("ffn_w2", c), hT[:, b, c, :], start=(c == 0), stop=(c == DFF // P - 1))
                last.then_inc(s["f2_ready"], 1)
            for b in range(B):
                norm(1, b)
            for b in range(B):
                norm_back(1, b)
            for b in range(B):
                pe.wait_ge(s[f"nT_out{b}"], 2)
                for t in range(QT):
                    last = mm(bank(b, 2)[:, t * LC:(t + 1) * LC], xnT[:, b, t * P:(t + 1) * P],
                              kfold[:, b * LC:(b + 1) * LC], start=True, stop=True)
                last.then_inc(s["l_s_ready"], 1)
            for b in range(B):
                pe.wait_ge(s["l_p"], b + 1)
                for t in range(QT):
                    last = nc.tensor.transpose(bank(b, 3)[0:LC, t * P:(t + 1) * P], s1[:, b, t, :], ident[:, :])
                last.then_inc(s["l_pT"], 1)
            for b in range(B):
                pe.wait_ge(s["l_pT_out"], b + 1)
                mm(bank(b, 0), v1[:, b, :], p1T[:, b, :], start=True, stop=True).then_inc(s["l_ev"], 1)
            for b in range(B):
                pe.wait_ge(s["l_ev_out"], b + 1)
                for t in range(QT):
                    o = bank(b, 2)[:, t * E:(t + 1) * E]
                    mm(o, xnT[:, b, t * P:(t + 1) * P], router_w(w_late, 0), start=True, stop=False)
                    last = mm(o, evT[:, b, t * P:(t + 1) * P], router_w(w_late, 1), start=False, stop=True)
                last.then_inc(s["r_ready"], 1)
            for b in range(B):
                for c in range(E * RC + 1):
                    n = b * (E * RC + 1) + c
                    if c >= 3:
                        pe.wait_ge(s["e_out"], n - 2)
                    o = bank(b, (0, 1, 3)[c % 3])
                    mm(o, e_w1(wl, c, 0), xnT[:, b, :], start=True, stop=False)
                    mm(o, e_w1(wl, c, 1), evT[:, b, :], start=False, stop=True).then_inc(s["e_ready"], 1)
                pe.wait_ge(s["r_p"], b + 1)
                for t in range(QT):
                    last = nc.tensor.transpose(bank(b, 2)[0:E, t * P:(t + 1) * P], lg[:, b, t, :], ident[:, :])
                last.then_inc(s["r_pT"], 1)
            for b in range(B):
                pe.wait_ge(s["e_out"], (b + 1) * (E * RC + 1))
                pe.wait_ge(s["r_pT_out"], b + 1)
                for e in range(E):
                    mm(bank(b, e), pick[:, e, :], prT[:, b, :], start=True, stop=True).then_inc(s["pb_ready"], 1)
                mm(bank(b, 3), b2_rows[:, :], prT[:, b, :], start=True, stop=False)
                for c in range(E * RC):
                    pe.wait_ge(s["e_scaled"], b * E * RC + c + 1)
                    last = mm(bank(b, 3), wl("e_w2", c), eh[:, b, c, :], start=False, stop=(c == E * RC - 1))
                last.then_inc(s["e2_ready"], 1)
                mm(bank(b, 0), wl("gate_w2"), eh[:, b, E * RC, :], start=True, stop=True).then_inc(s["g2_ready"], 1)
                pe.wait_ge(s["rt_out"], b + 1)
                mm(bank(b, 1), wl("out_w"), rtT[:, b, :], start=True, stop=True).then_inc(s["d_ready"], 1)

        @block.scalar
        def _(act):
            a = nc.scalar.activation

            def first_part(ps, bias, dense, out_sem):
                a(dense, ps, ACT.Identity, bias=bias).then_inc(out_sem, 1)

            act.wait_ge(s["ld_early"], 16)
            act.wait_ge(s["aff_out"], 1)
            act.wait_ge(s["normT_ready"], 2)
            a(xnT[:, 1, :], ST[:, 1, :], ACT.Identity, bias=lnB[:, 0, 1:2], scale=lnA[:, 0, 1:2]).then_inc(s["xnT_out1"], 1)
            def values_out(b):
                act.wait_ge(s["v_ready"], b + 1)
                act.wait_ge(s["ones_set"], 8)
                dst = VS[:, b * QT:(b + 1) * QT, :, :].rearrange("p a (r s j) c -> p (a r) s j c", s=2, j=HEADS)
                src = UP[:, :].rearrange("p (ar s j d) -> p ar s j d", s=2, j=HEADS, d=DH)
                for sl in range(2):
                    nc.scalar.copy(dst[:, :, sl, :, 16 * sl:16 * sl + DH], src[:, :, sl, :, :]).then_inc(s["v_out"], 1)

            act.wait_ge(s["q_ready"], 1)
            first_part(S[:, 0, :], ve("sa_qb"), part[:, 0, 0, :], s["q1_out"])
            act.wait_ge(s["k_ready"], 1)
            first_part(S[:, 1, :], ve("sa_kb"), part[:, 1, 0, :], s["k1_out"])
            values_out(0)
            values_out(1)
            act.wait_ge(s["ctx_ready"], 1)
            nc.scalar.copy(kT1[:, :], MB[:, B * LC:2 * B * LC]).then_inc(s["kT1_out"], 1)
            first_part(MB[:, 0:B * LC], ve("ca_kb"), partx[:, 0, :], s["kx1_out"])
            act.wait_ge(s["ctx_v_ready"], 1)
            dst = VX[:, :, :, :].rearrange("p a (r s j) c -> p (a r) s j c", s=2, j=HEADS)
            src = ST[0:LC, 0, 0:B * D].rearrange("p (ar s j d) -> p ar s j d", s=2, j=HEADS, d=DH)
            for sl in range(2):
                nc.scalar.copy(dst[:, :, sl, :, 16 * sl:16 * sl + DH], src[:, :, sl, :, :]).then_inc(s["vx_out"], 1)
            nc.scalar.copy(v1[:, :, :], ST[0:LC, 0, B * D:2 * B * D].rearrange("p (b d) -> p b d", b=B)).then_inc(s["v1_out"], 1)
            act.wait_ge(s["stack_q0"], STACK_DMAS)
            first_part(ST[:, 2, :], ve("sa_qb"), part[:, 0, 0, :], s["q1_out"])
            act.wait_ge(s["stack_k0"], STACK_DMAS)
            first_part(ST[:, 3, :], ve("sa_kb"), part[:, 1, 0, :], s["k1_out"])

            for i, step in enumerate(steps):
                kind = step[0]
                if kind == "exps":
                    unit, kt, n, jj = step[1:]
                    rows = P if unit[0] == SELF else LC
                    if n >= 2 and jj == 0:
                        act.wait_ge(s["u_ready"], n - 1)
                    act.wait_ge(s["st_ready"], 2 * n + jj + 1)
                    a(PT[0:rows, n % 2, 2 * jj:2 * jj + 2, :], ST[0:rows, 2 * jj:2 * jj + 2, :], ACT.Exp,
                      scale=SCALE).then_inc(s["exp_out"], 1)
                elif kind == "mrows":
                    n = nth[i]
                    act.wait_ge(s["mrows_ready"], n + 1)
                    if n >= 2:
                        act.wait_ge(s[f"mrows_in{n % 2}"], 32 * (n // 2))
                    nc.scalar.copy(mT[:, n % 2, :], MB16[0:PARTS * HEADS, 0:L]).then_inc(s["mT_out"], 1)
                elif kind == "gather":
                    n = nth[i]
                    unit_n = last_round(steps, step)
                    act.wait_ge(s["u_ready"], unit_n + 1)
                    if n >= 2:
                        act.wait_ge(s["nat_ready"], n - 1)
                    nc.scalar.copy(U[:, n % 2, :], UP[:, :]).then_inc(s["u_out"], 1)
                elif kind == "turn":
                    act.wait_ge(s["turn_ready"], nth[i] + 1)
                    if nth[i]:
                        act.wait_ge(s["proj_ready"], nth[i])
                    nc.scalar.copy(OT[:, :], MB[:, :]).then_inc(s["oT_out"], 1)
                elif kind == "queries":
                    b = step[1]
                    act.wait_ge(s["qx_ready"], b + 1)
                    act.wait_ge(s["stack_qx0"] if b else s["stack_q1"], STACK_DMAS)
                    first_part(MB[:, :], ve("ca_qb"), part[:, 0, 0, :], s["qx1_out"])

            NF = DFF // P
            act.wait_ge(s["nT_ready"], 2)
            a(xnT[:, 1, :], bank(1, 1), ACT.Identity, bias=lnB[:, 1, 1:2], scale=lnA[:, 1, 1:2]).then_inc(s["nT_out1"], 1)
            for b in range(B):
                for c in range(NF):
                    act.wait_ge(s["f_ready"], b * NF + c + 1)
                    a(hT[:, b, c, :], bank(b, c), ACT.Gelu, bias=ve("ffn_b1", c)).then_inc(s["f_out"], 1)
            act.wait_ge(s["nT_ready"], B + 2)
            a(xnT[:, 1, :], bank(1, 1), ACT.Identity, bias=ve("ln_beta"), scale=ve("ln_gamma")).then_inc(s["nT_out1"], 1)
            for b in range(B):
                act.wait_ge(s["l_sub"], b + 1)
                a(s1[:, b, :, :], s1[:, b, :, :], ACT.Exp, scale=SCALE1).then_inc(s["l_exp"], 1)
            for b in range(B):
                act.wait_ge(s["l_pT"], b + 1)
                nc.scalar.copy(p1T[:, b, :], bank(b, 3)[0:LC, :]).then_inc(s["l_pT_out"], 1)
            for b in range(B):
                act.wait_ge(s["l_ev"], b + 1)
                nc.scalar.copy(evT[:, b, :], bank(b, 0)).then_inc(s["l_ev_out"], 1)
            for b in range(B):
                act.wait_ge(s["r_sub"], b + 1)
                a(lg[:, b, :, :], lg[:, b, :, :], ACT.Exp).then_inc(s["r_exp"], 1)
            NE = E * RC + 1
            for b in range(B):
                for c in range(NE):
                    act.wait_ge(s["e_ready"], b * NE + c + 1)
                    a(eh[:, b, c, :], bank(b, (0, 1, 3)[c % 3]), ACT.Silu, bias=hbias[:, c, b:b + 1]).then_inc(s["e_out"], 1)
            for b in range(B):
                act.wait_ge(s["g2_ready"], b + 1)
                a(gT[:, b, :], bank(b, 0), ACT.Sigmoid, bias=ve("gate_b2")).then_inc(s["g_out"], 1)

        @block.vector
        def _(dve):
            v = nc.vector
            dve.wait_ge(s["ld_x"], 16)
            for t in range(B * QT):
                v.bn_stats(stats[:, t, :], xn[:, t, :]).then_inc(s["bn_out"], 1)
            for t in range(B * QT):
                dve.wait_ge(s["bn_out"], t + 1)
                last = v.bn_aggr(mv[:, t, :], stats[:, t, :])
            last.then_inc(s["stats_out"], 1)
            dve.wait_ge(s["stats_out"], 1)
            v.tensor_scalar(rstd[:, :], mv[:, :, 1], EPS, None, ALU.add).then_inc(s["rstd_in"], 1)
            dve.wait_ge(s["aff_ready"], 1)
            modulation(dve, v, s, aff, lnA, lnB, MB[:, 0:2 * B], ve, 0, "aff1_b", "ln1_g", "ln1_b", s["aff_out"])
            dve.wait_ge(s["rstd_out"], 1)
            for t in range(B * QT):
                v.tensor_scalar(normed[:, t, :], xn[:, t, :], mv[:, t, 0:1], rstd[:, t:t + 1],
                                ALU.subtract, ALU.mult).then_inc(s["normed_out"], 1)
            dve.wait_ge(s["normT_ready"], 1)
            dve.wait_ge(s["aff_out"], 1)
            v.tensor_scalar(xnT[:, 0, :], ST[:, 0, :], lnA[:, 0, 0:1], lnB[:, 0, 0:1], ALU.mult, ALU.add).then_inc(s["xnT_out0"], 1)

            def later_parts(ps, bias, dense, rem, n, outs):
                first, r, second, third = [s[x] for x in outs]
                dve.wait_ge(first, n)
                v.scalar_tensor_tensor(rem, ps, bias, dense[:, 0, :], ALU.add, ALU.subtract).then_inc(r, 1)
                dve.wait_ge(r, n)
                v.tensor_copy(dense[:, 1, :], rem).then_inc(second, 1)
                dve.wait_ge(second, n)
                v.tensor_tensor(dense[:, 2, :], rem, dense[:, 1, :], ALU.subtract).then_inc(third, 1)

            Q_OUTS = ("q1_out", "rest_q", "q2_out", "q3_out")
            K_OUTS = ("k1_out", "rest_k", "k2_out", "k3_out")
            later_parts(S[:, 0, :], ve("sa_qb"), part[:, 0, :, :], rest[:, 0, :], 1, Q_OUTS)
            later_parts(S[:, 1, :], ve("sa_kb"), part[:, 1, :, :], rest[:, 1, :], 1, K_OUTS)
            later_parts(MB[:, 0:B * LC], ve("ca_kb"), partx[:, :, :], restx[:, :], 1,
                        ("kx1_out", "kx_rest", "kx2_out", "kx3_out"))
            dve.wait_ge(s["small_ready"], 1)
            v.tensor_copy(kfold[:, :], ST[:, 1, 0:B * LC]).then_inc(s["kfold_out"], 1)
            at = B * LC
            modulation(dve, v, s, aff, lnA, lnB, ST[:, 1, at:at + 2 * B], ve, 1, "aff2_b", "ln2_g", "ln2_b", s["aff_out"])
            at += 2 * B
            v.tensor_tensor(csa[:, 0:1], ST[:, 1, at:at + 1], ve("sa_ob"), ALU.add)
            v.tensor_tensor(csa[:, 1:2], ST[:, 1, at + 1:at + 2], ve("ca_ob"), ALU.add)
            at += 2
            NE = E * RC + 1
            for b in range(B):
                hp = ST[:, 1, at:at + B * NE].rearrange("p (c b) -> p c b", b=B)
                v.tensor_tensor(hbias[:, 0:NE - 1, b], hp[:, 0:NE - 1, b], ve("e_b1", 0, NE - 1), ALU.add)
                v.tensor_tensor(hbias[:, NE - 1:NE, b], hp[:, NE - 1:NE, b], ve("gate_b1"), ALU.add)
            at += B * NE
            v.tensor_copy(rbias[:, :, :], ST[:, 1, at:at + B * E].rearrange("p (b e) -> p b e", b=B)).then_inc(s["small_out"], 1)

            later_parts(ST[:, 2, :], ve("sa_qb"), part[:, 0, :, :], rest[:, 0, :], 2, Q_OUTS)
            later_parts(ST[:, 3, :], ve("sa_kb"), part[:, 1, :, :], rest[:, 1, :], 2, K_OUTS)

            for i, step in enumerate(steps):
                kind = step[0]
                if kind == "maxima":
                    (k, b, g), e = step[1:]
                    n = event_at[step[1:]]
                    slot = split_nth[(k, b, g)] % RING
                    dve.wait_ge(s["s_ready"], n + 1)
                    if k == SELF:
                        v.tensor_reduce(negm[:, slot, e // 4, e % 2, e // 2 % 2:e // 2 % 2 + 1], S[:, n % 2, :], AX.X,
                                        ALU.max, negate=True).then_inc(s["max_out"], 1)
                    else:
                        c = 2 * (e // 2)
                        v.tensor_reduce(negm[:, slot, c:c + 2, e % 2, :],
                                        S[:, n % 2, 0:4 * LC].rearrange("p (t jj k) -> p t jj k", t=2, jj=2), AX.X,
                                        ALU.max, negate=True).then_inc(s["max_out"], 1)
                elif kind == "normalise":
                    n = nth[i]
                    k, b, r = step[1:]
                    dve.wait_ge(s["nat_ready"], n + 1)
                    t4 = MB[:, :].rearrange("p (t j s c) -> p t j s c", t=QT, j=HEADS, s=2)
                    v.reciprocal(rden[:, n % 2, :, :], MB[:, :].rearrange("p (t js c) -> p t js c", t=QT, c=16)[:, :, :, DH]).then_inc(s["rden_out"], 1)
                    dve.wait_ge(s["rden_out"], n + 1)
                    if r == 0 and n >= 2:
                        dve.wait_ge(s["turn_ready"], n // 2)
                    for sl in range(2):
                        o = O[:, :, :].rearrange("p t (r s j d) -> p t r s j d", r=2, s=2, j=HEADS)[:, :, r, sl, :, :]
                        rd = rden[:, n % 2, :, :].rearrange("p t (j s) -> p t j s", s=2)[:, :, :, sl]
                        last = v.tensor_tensor(o, t4[:, :, :, sl, 0:DH],
                                               rd.unsqueeze(3).to_broadcast([P, QT, HEADS, DH]), ALU.mult)
                    last.then_inc(s["o_out"], 1)
                elif kind == "residual":
                    k, b = step[1:]
                    n = nth[i]
                    dve.wait_ge(s["proj_ready"], n + 1)
                    if n == 0:
                        dve.wait_ge(s["ld_xT"], 16)
                    v.scalar_tensor_tensor(xT[:, b, :], MB[:, :], csa[:, k:k + 1], xT[:, b, :], ALU.add, ALU.add).then_inc(s["x_out"], 1)
                elif kind == "rests":
                    b = step[1]
                    later_parts(MB[:, :], ve("ca_qb"), part[:, 0, :, :], rest[:, 0, :], b + 1,
                                ("qx1_out", "rest_qx", "qx2_out", "qx3_out"))

            def norm_stats(site, b):
                n = site * B + b
                dve.wait_ge(s["n_ready"], n + 1)
                for t in range(QT):
                    last = v.bn_stats(stats[:, b * QT + t, :], bank(b, 0)[:, t * P:(t + 1) * P])
                last.then_inc(s["n_stats"], 1)
                dve.wait_ge(s["n_stats"], n + 1)
                for t in range(QT):
                    last = v.bn_aggr(mv[:, b * QT + t, :], stats[:, b * QT + t, :])
                last.then_inc(s["n_aggr"], 1)
                dve.wait_ge(s["n_aggr"], n + 1)
                v.tensor_scalar(rstd[:, b * QT:(b + 1) * QT], mv[:, b * QT:(b + 1) * QT, 1], EPS, None, ALU.add).then_inc(s["n_var"], 1)

            def norm_apply(site, b):
                n = site * B + b
                dve.wait_ge(s["n_rstd"], n + 1)
                for t in range(QT):
                    k = b * QT + t
                    last = v.tensor_scalar(normed[:, k, :], bank(b, 0)[:, t * P:(t + 1) * P], mv[:, k, 0:1],
                                           rstd[:, k:k + 1], ALU.subtract, ALU.mult)
                last.then_inc(s["n_normed"], 1)

            for b in range(B):
                norm_stats(0, b)
            for b in range(B):
                norm_apply(0, b)
            dve.wait_ge(s["nT_ready"], 1)
            v.tensor_scalar(xnT[:, 0, :], bank(0, 1), lnA[:, 1, 0:1], lnB[:, 1, 0:1], ALU.mult, ALU.add).then_inc(s["nT_out0"], 1)
            for b in range(B):
                dve.wait_ge(s["f2_ready"], b + 1)
                v.scalar_tensor_tensor(xT[:, b, :], bank(b, 3), ve("ffn_b2"), xT[:, b, :], ALU.add, ALU.add).then_inc(s["x3_out"], 1)
            for b in range(B):
                norm_stats(1, b)
            for b in range(B):
                norm_apply(1, b)
            dve.wait_ge(s["nT_ready"], B + 1)
            v.tensor_scalar(xnT[:, 0, :], bank(0, 1), ve("ln_gamma"), ve("ln_beta"), ALU.mult, ALU.add).then_inc(s["nT_out0"], 1)
            for b in range(B):
                sc = bank(b, 2)[:, 0:QT * LC].rearrange("p (t k) -> p t k", t=QT)
                dve.wait_ge(s["l_s_ready"], b + 1)
                v.tensor_reduce(mx1[:, b, :], sc, AX.X, ALU.max).then_inc(s["l_max"], 1)
                dve.wait_ge(s["l_max"], b + 1)
                v.tensor_tensor(s1[:, b, :, :], sc, mx1[:, b, :].unsqueeze(2).to_broadcast([P, QT, LC]), ALU.subtract).then_inc(s["l_sub"], 1)
            for b in range(B):
                dve.wait_ge(s["l_exp"], b + 1)
                v.tensor_reduce(sum1[:, b, :], s1[:, b, :, :], AX.X, ALU.add).then_inc(s["l_sum"], 1)
                dve.wait_ge(s["l_sum"], b + 1)
                v.reciprocal(rec1[:, b, :], sum1[:, b, :]).then_inc(s["l_rec"], 1)
                dve.wait_ge(s["l_rec"], b + 1)
                v.tensor_tensor(s1[:, b, :, :], s1[:, b, :, :], rec1[:, b, :].unsqueeze(2).to_broadcast([P, QT, LC]), ALU.mult).then_inc(s["l_p"], 1)
            for b in range(B):
                dve.wait_ge(s["r_ready"], b + 1)
                v.tensor_tensor(lg[:, b, :, :], bank(b, 2)[:, 0:QT * E].rearrange("p (t e) -> p t e", t=QT),
                                rbias[:, b, :].unsqueeze(1).to_broadcast([P, QT, E]), ALU.add).then_inc(s["r_lg"], 1)
                dve.wait_ge(s["r_lg"], b + 1)
                v.tensor_reduce(rmx[:, b, :], lg[:, b, :, :], AX.X, ALU.max).then_inc(s["r_mx"], 1)
                dve.wait_ge(s["r_mx"], b + 1)
                v.tensor_tensor(lg[:, b, :, :], lg[:, b, :, :], rmx[:, b, :].unsqueeze(2).to_broadcast([P, QT, E]), ALU.subtract).then_inc(s["r_sub"], 1)
            for b in range(B):
                dve.wait_ge(s["r_exp"], b + 1)
                v.tensor_reduce(rsum[:, b, :], lg[:, b, :, :], AX.X, ALU.add).then_inc(s["r_sum"], 1)
                dve.wait_ge(s["r_sum"], b + 1)
                v.reciprocal(rrec[:, b, :], rsum[:, b, :]).then_inc(s["r_rec"], 1)
                dve.wait_ge(s["r_rec"], b + 1)
                v.tensor_tensor(lg[:, b, :, :], lg[:, b, :, :], rrec[:, b, :].unsqueeze(2).to_broadcast([P, QT, E]), ALU.mult).then_inc(s["r_p"], 1)
            for b in range(B):
                dve.wait_ge(s["r_pT"], b + 1)
                v.tensor_copy(prT[:, b, :], bank(b, 2)[0:E, :]).then_inc(s["r_pT_out"], 1)
            for b in range(B):
                for e in range(E):
                    dve.wait_ge(s["pb_ready"], b * E + e + 1)
                    for c in range(RC):
                        k = e * RC + c
                        v.tensor_tensor(eh[:, b, k, :], eh[:, b, k, :], bank(b, e), ALU.mult).then_inc(s["e_scaled"], 1)
                dve.wait_ge(s["e2_ready"], b + 1)
                v.tensor_copy(rtT[:, b, :], bank(b, 3)).then_inc(s["rt_out"], 1)
                dve.wait_ge(s["d_ready"], b + 1)
                dve.wait_ge(s["g_out"], b + 1)
                v.scalar_tensor_tensor(dT[:, b, :], bank(b, 1), ve("out_b"), gT[:, b, :], ALU.add, ALU.mult).then_inc(s["d_out"], 1)
                dve.wait_ge(s["d_out"], b + 1)
                v.tensor_tensor(dT[:, b, :], dT[:, b, :], xT[:, b, :], ALU.add).then_inc(s["y_out"], 1)


def e_w1(wl, c, part):
    if c == E * RC:
        return wl("gate_w1", part)
    return wl("e_w1", (part * E + c // RC) * RC + c % RC)


def router_w(w_late, part):
    at = LATE_AT["router_W"] + part * E
    return w_late[:, at:at + E]


def last_round(steps, gather):
    _, kind, b, r = gather
    return max(s[3] for s in steps if s[0] == "values" and s[1] == (kind, b, 2 * r + 1))


def modulation(dve, v, s, aff, lnA, lnB, ps, ve, site, bias, g, bb, out_sem):
    for i in range(2):
        last = v.tensor_scalar(aff[:, site, i, :], ps[:, B * i:B * i + B], ve(bias, i), None, ALU.add)
    last.then_inc(s["mod_step"], 1)
    dve.wait_ge(s["mod_step"], 2 * site + 1)
    v.tensor_scalar(lnA[:, site, :], aff[:, site, 0, :], ve(g), None, ALU.mult)
    v.tensor_scalar(lnB[:, site, :], aff[:, site, 0, :], ve(bb), None, ALU.mult).then_inc(s["mod_step"], 1)
    dve.wait_ge(s["mod_step"], 2 * site + 2)
    v.tensor_tensor(lnB[:, site, :], lnB[:, site, :], aff[:, site, 1, :], ALU.add).then_inc(out_sem, 1)


def kernel(**inputs):
    import numpy as np
    import concourse.bacc as bacc
    from concourse.bass_utils import run_bass_kernel_spmd as run

    a = {k.replace("L0_xcond_", "").replace("L1_xcond_", ""): np.asarray(v) for k, v in inputs.items()}

    dense = np.arange(D).reshape(2, H // 2, DH).transpose(0, 2, 1).reshape(-1)
    for k in ("sa_q", "sa_k", "ca_q", "ca_k"):
        a[k + "w"], a[k + "b"] = a[k + "w"][:, dense], a[k + "b"][dense]
    order = np.array([8 * q + 2 * g + jj for g in range(GROUPS) for jj in range(2) for q in range(2)])
    order = (order[:, None] * DH + np.arange(DH)).reshape(-1)
    for k in ("sa", "ca"):
        a[k + "_vw"], a[k + "_vb"], a[k + "_ow"] = a[k + "_vw"][:, order], a[k + "_vb"][order], a[k + "_ow"][order]

    def wide(w):
        n = w.shape[0] // P
        return w.reshape(n, P, -1).transpose(1, 0, 2).reshape(P, -1)

    vec = np.concatenate([(a["cond_1024"] if n == "cond" else a[n]).reshape(k, P).T for n, k in VECTORS], axis=1)
    late = dict(a, ctxT=a["ctx_1024"].reshape(B * LC, D).T, WqT=a["Wq"].T, ffn_w2=wide(a["ffn_w2"]),
                router_W=wide(a["router_W"]), gate_w1=wide(a["gate_w1"]),
                e_w1=a["e_w1"].reshape(E, 3, P, RH).transpose(2, 1, 0, 3).reshape(P, -1),
                e_w2=wide(a["e_w2"].reshape(E * RH, D)))
    feeds = {
        "x_nat": a["x"].reshape(B * QT, P, D).transpose(1, 0, 2),
        "x_T": a["x"].transpose(2, 0, 1),
        "early": np.concatenate([vec if n == "vec" else a[n] for n, _ in EARLY], axis=1),
        "late": np.concatenate([late[n] for n, _ in LATE], axis=1),
        "router_b": a["router_b"].reshape(1, E),
        "e_b2": a["e_b2"],
    }
    feeds = {k: np.ascontiguousarray(v) for k, v in feeds.items()}
    nc = bacc.Bacc("TRN2", target_bir_lowering=False, num_devices=1)
    args = [nc.dram_tensor(k, v.shape, mybir.dt.from_np(v.dtype), kind="ExternalInput").ap() for k, v in feeds.items()]
    out = nc.dram_tensor("out_T", (B, D, L), F32, kind="ExternalOutput").ap()
    block_program(nc, *args, out)
    got = run(nc, [feeds], core_ids=[0]).results[0]["out_T"]
    return np.ascontiguousarray(got.transpose(0, 2, 1))
```

```python
from contextlib import ExitStack

import concourse.bass as bass
from concourse import mybir

F32 = mybir.dt.float32
BF16 = mybir.dt.bfloat16
ALU = mybir.AluOpType
ACT = mybir.ActivationFunctionType
AX = mybir.AxisListType

B, L, D = 2, 512, 128
H, DH = 16, 8
LC = 77
DFF = 512
P = 128
QT = L // P
E, RH = 3, 256
RC = RH // P
NE = E * RC + 1
NF = DFF // P
EPS = 1e-5
SCALE = 1.0 / (DH ** 0.5)
SCALE1 = D ** -0.5
HEADS = 4
GROUPS = H // HEADS
PARTS = 3
Q_RUNS = [(0, 0, 3), (3, 1, 2), (5, 2, 1)]
K_RUNS = [(5, None, 1), (3, None, 2), (0, None, 3)]
STACK_DMAS = 16 * 3
STRIP_DMAS = 16 * 2
STACK = 6 * DH
STRIP = 64

VECTORS = [("ln1_g", 1), ("ln1_b", 1), ("aff1_b", 2), ("ln2_g", 1), ("ln2_b", 1), ("aff2_b", 2),
           ("sa_qb", 1), ("sa_kb", 1), ("sa_vb", 1), ("sa_ob", 1), ("ca_qb", 1), ("ca_kb", 1),
           ("ca_vb", 1), ("ca_ob", 1), ("ffn_b1", DFF // P), ("ffn_b2", 1), ("ln_gamma", 1),
           ("ln_beta", 1), ("e_b1", E * RC), ("gate_b1", 1), ("gate_b2", 1), ("out_b", 1),
           ("cond", B)]
EARLY = [("vec", sum(n for _, n in VECTORS)), ("aff1_w", 2 * D), ("sa_qw", D), ("sa_kw", D),
         ("sa_vw", D)]
LATE = [("ctxT", B * LC), ("ca_kw", D), ("ca_vw", D), ("Wk", D), ("WqT", D), ("Wv", D),
        ("sa_ow", D), ("ca_qw", D), ("ca_ow", D), ("aff2_w", 2 * D), ("ffn_w1", DFF),
        ("ffn_w2", DFF), ("router_W", 3 * E), ("e_w1", 3 * E * RH), ("e_w2", E * RC * D),
        ("gate_w1", 3 * D), ("gate_w2", D), ("out_w", D)]


def places(fields):
    at, out = 0, {}
    for name, n in fields:
        out[name] = at
        at += n
    return out, at


VEC_AT, _ = places(VECTORS)
EARLY_AT, EARLY_N = places(EARLY)
LATE_AT, LATE_N = places(LATE)

SELF, CROSS = 0, 1
TWO_ONES = 1 + 0x3F80 / 2 ** 23
EVENTS = (4 * QT, 4)
OPENING = 6
WARM = 8
NORM_OPEN = 3
ROUND = ("M", 0, 1, "M", "V", "M", 2, "M", 3)
WITH_V = ROUND.index("V")
RING = GROUPS
HIDDEN_RING = (3, 6)


def plan():
    steps = []
    units = [(kind, b, g) for kind in (SELF, CROSS) for b in range(B) for g in range(GROUPS)]
    rounds = [(u, kt) for u in units for kt in range(QT if u[0] == SELF else 1)]
    todo = [(u, e) for u in units for e in range(EVENTS[u[0]])]
    due = {}
    reach = 2 * GROUPS

    def maxima(last_unit):
        if todo and units.index(todo[0][0]) < last_unit:
            u, e = todo.pop(0)
            steps.append(("maxima", u, e))
            if e == EVENTS[u[0]] - 1:
                steps.append(("split",) + u)

    def put(n, place, step):
        due.setdefault((n, place), []).append(step)

    def flush(warms):
        for where in sorted(due):
            for step in due[where]:
                if step[0] in ("natural", "turn", "project"):
                    steps.append(("open", warms))
                if step[0] != "reach":
                    steps.append(step)
        due.clear()
        steps.append(("open", warms))

    for _ in range(EVENTS[SELF]):
        maxima(1)
    steps.append(("mrows",) + units[0])
    for _ in range(WARM):
        maxima(2)
        steps.append(("warm",))
    for n, (unit, kt) in enumerate(rounds):
        kind, b, g = unit
        at = units.index(unit)
        last = kt == (QT if kind == SELF else 1) - 1
        if unit == (CROSS, 1, 0):
            steps.append(("values",) + rounds[n - 1] + (n - 1,))
            flush(NORM_OPEN)
            few = EVENTS[CROSS] // 2
            for step in (("norm", 0, 0), ("norm_back", 0, 0)):
                steps.append(step)
                for _ in range(2 * few):
                    maxima(len(units))
                    steps.append(("open", NORM_OPEN if step[0] == "norm" else 1))
            for k in range(2 * GROUPS - 4):
                for _ in range(few):
                    maxima(len(units))
                    steps.append(("open", 1))
                if k % 2 == 1:
                    steps.append(("mrows", CROSS, 1, k // 2))
                    steps.append(("open", NORM_OPEN))
            for c in range(NF):
                steps.append(("ffn1", 0, c))
                if c < 2:
                    steps.append(("mrows", CROSS, 1, GROUPS - 2 + c))
            for c in range(NF):
                put(n + c // 2, WITH_V - 1 + 2 * (c % 2), ("ffn2", 0, c))
            put(n + 2, 0, ("norm", 1, 0))
            put(n + 3, len(ROUND) - 1, ("norm_back", 1, 0))
        if kind == SELF and kt == 2 and units[at + 1][0] == SELF:
            put(n, WITH_V + 1, ("mrows",) + units[at + 1])
        if unit == (SELF, 1, GROUPS - 1):
            put(n, WITH_V + 1, ("mrows", CROSS, 0, kt))
        if last and g % 2 == 1:
            r = g // 2
            put(n + 1, WITH_V + 1, ("gather", kind, b, r))
            put(n + 2, 0, ("natural", kind, b, r))
            put(n + 2, 1, ("normalise", kind, b, r))
            if r == 1:
                put(n + 2, WITH_V + 2, ("turn", kind, b))
                put(n + 3, WITH_V - 1, ("project", kind, b))
                put(n + 3, WITH_V, ("residual", kind, b))
                if kind == SELF:
                    put(n + 3, len(ROUND) - 1, ("queries", b))
                    put(n + 4, 1, ("rests", b))
                    put(n + 5, len(ROUND) - 1, ("reach", (3 + b) * GROUPS))
        for place, token in enumerate(ROUND):
            for step in due.pop((n, place), []):
                if step[0] == "reach":
                    reach = step[1]
                else:
                    steps.append(step)
            if token == "M":
                maxima(reach)
            elif token == "V" and n and unit != (CROSS, 1, 0):
                steps.append(("values",) + rounds[n - 1] + (n - 1,))
            elif token == "V":
                if n == 0:
                    steps.extend([("warm",)] * 2)
            else:
                steps.append(("scores", unit, kt, n, token))
                steps.append(("exps", unit, kt, n, token))
    steps += [("values",) + rounds[-1] + (len(rounds) - 1,), ("gather", CROSS, 1, 1)]
    steps += [("context", 0), ("natural", CROSS, 1, 1), ("hidden_x", 0, 0), ("normalise", CROSS, 1, 1)]
    steps += [("turn", CROSS, 1), ("hidden_x", 0, 1), ("context_probs", 0), ("project", CROSS, 1), ("residual", CROSS, 1)]
    steps += [("context_value", 0), ("norm", 0, 1)]
    steps += [("hidden_ev", 0, 0), ("router", 0), ("hidden_ev", 0, 1)]
    steps += hidden(0, 2, 3)
    steps += [("norm_back", 0, 1), ("router_probs", 0)]
    steps += hidden(0, 3, NE)
    steps += [("ffn1", 1, c) for c in range(NF)] + [("spread", 0)]
    steps += [("ffn2", 1, c) for c in range(NF)] + [("combine", 0, 0), ("norm", 1, 1)]
    steps += [("combine", 0, c) for c in range(1, 5)] + [("norm_back", 1, 1)]
    steps += [("combine", 0, c) for c in range(5, E * RC)] + [("context", 1), ("routed", 0), ("out", 0)]
    steps += [("hidden_x", 1, c) for c in range(3)] + [("context_probs", 1)]
    steps += [("hidden_x", 1, 3), ("context_value", 1), ("hidden_x", 1, 4), ("hidden_x", 1, 5)]
    steps += [("hidden_ev", 1, 0), ("router", 1)] + [("hidden_ev", 1, c) for c in range(1, 4)]
    steps += [("router_probs", 1), ("hidden_ev", 1, 4), ("hidden_ev", 1, 5), ("hidden_x", 1, 6)]
    steps += [("spread", 1), ("hidden_ev", 1, 6)]
    steps += [("combine", 1, c) for c in range(E * RC)] + [("routed", 1), ("out", 1)]
    return steps


def hidden(b, first, end):
    return [(half, b, c) for c in range(first, end) for half in ("hidden_x", "hidden_ev")]


def counts(steps):
    seen, out = {}, []
    for s in steps:
        k = s[0]
        out.append(seen.get(k, 0))
        seen[k] = out[-1] + 1
    return out


def block_program(nc, x_nat, x_T, early, late, router_b, e_b2, out_T):
    steps = plan()
    nth = counts(steps)
    TURNS = {"mrows": "mT_out", "natural": "o_out", "turn": "oT_out", "project": "x_out",
             "queries": "rest_qx"}
    bank_reader, before = [], None
    for st, n in zip(steps, nth):
        bank_reader.append(before)
        if st[0] in TURNS:
            before = (TURNS[st[0]], n + 1)
    event_at, ev = {}, 0
    for s in steps:
        if s[0] == "maxima":
            event_at[s[1:]] = ev
            ev += 1
    norm_nth = {s[1:]: nth[i] for i, s in enumerate(steps) if s[0] == "norm"}
    residual_nth = {s[1:]: nth[i] for i, s in enumerate(steps) if s[0] == "residual"}
    ROUNDS = sum(s[0] == "scores" for s in steps) // HEADS
    CROSS_1 = ROUNDS - GROUPS
    split_nth = {s[1:]: nth[i] for i, s in enumerate(steps) if s[0] == "split"}
    mrows_nth = {s[1:]: nth[i] for i, s in enumerate(steps) if s[0] == "mrows"}
    queries_nth = {s[1]: nth[i] for i, s in enumerate(steps) if s[0] == "queries"}

    with ExitStack() as ctx:
        def sb(name, shape, dt=F32):
            return ctx.enter_context(nc.sbuf_tensor(name, shape, dt))

        def psum(name, shape, dt=F32):
            return ctx.enter_context(nc.psum_tensor(name, shape, dt))

        def sem(name):
            return ctx.enter_context(nc.semaphore(name))

        xn = sb("xn", [P, B * QT, D])
        xT = sb("xT", [P, B, L])
        w_early = sb("w_early", [P, EARLY_N])
        w_late = sb("w_late", [P, LATE_N])
        rb_row = sb("rb_row", [1, E])
        b2_rows = sb("b2_rows", [E, D])
        ident = sb("ident", [P, P])
        ident16 = sb("ident16", [P, P], BF16)
        ones_row = sb("ones_row", [1, P])
        pick = sb("pick", [E, E, P])
        half = sb("half", [P, B * QT])
        unread = sb("unread", [P, B * QT])
        stats = sb("stats", [P, B * QT, 6])
        mv = sb("mv", [P, B * QT, 2])
        rstd = sb("rstd", [P, B * QT])
        aff = sb("aff", [P, 2, 2, B])
        lnA = sb("lnA", [P, 2, B])
        lnB = sb("lnB", [P, 2, B])
        normed = sb("normed", [P, B * QT, D])
        xnT = sb("xnT", [P, B, L])
        QS = sb("QS", [P, B, H // 2, L], BF16)
        KS = sb("KS", [P, B, H // 2, L], BF16)
        QX = sb("QX", [P, B, H // 2, L], BF16)
        KX = sb("KX", [P, H // 2, B * LC], BF16)
        part = sb("part", [P, 2, PARTS, L], BF16)
        rest = sb("rest", [P, 2, L])
        partx = sb("partx", [P, PARTS, B * LC], BF16)
        restx = sb("restx", [P, B * LC])
        VS = sb("VS", [P, B * QT, H, 32])
        VX = sb("VX", [LC, B, H, 32])
        PT = sb("PT", [P, 2, HEADS, L])
        negm = sb("negm", [P, RING, QT, 2, 2])
        mrest = sb("mrest", [P, RING, QT, 2, 2])
        mpart = sb("mpart", [P, RING, QT, 2, PARTS, 2], BF16)
        mT = sb("mT", [PARTS * HEADS, 2, L], BF16)
        U = sb("U", [P, 2, L])
        rden = sb("rden", [P, 2, QT, 8])
        O = sb("O", [P, QT, D])
        OT = sb("OT", [P, L])
        csa = sb("csa", [P, 2])
        kT1 = sb("kT1", [P, B * LC])
        kfold = sb("kfold", [P, B * LC])
        v1 = sb("v1", [LC, B, D])
        hbias = sb("hbias", [P, E * RC + 1, B])
        rbias = sb("rbias", [P, B, E])
        hT = VS[:, :, :, :].rearrange("p (b a) h c -> p b (a h c)", b=B).rearrange("p b (f t) -> p b f t", t=L)
        s1 = sb("s1", [P, B, QT, LC])
        mx1 = sb("mx1", [P, B, QT])
        sum1 = sb("sum1", [P, B, QT])
        rec1 = sb("rec1", [P, B, QT])
        p1T = sb("p1T", [LC, B, L])
        evT = sb("evT", [P, B, L])
        lg = sb("lg", [P, B, QT, E])
        rmx = sb("rmx", [P, B, QT])
        rsum = sb("rsum", [P, B, QT])
        rrec = sb("rrec", [P, B, QT])
        prT = sb("prT", [E, B, L])
        eh = sb("eh", [P, B, E * RC + 1, L])
        rtT = PT[:, 0, 0:2, :]
        gT = PT[:, 0, 2:4, :]
        dT = PT[:, 1, 0:2, :]

        S = psum("S", [P, 3, 512])
        ST = psum("ST", [P, 3, 512])
        UP = psum("UP", [P, 512])
        MB = psum("MB", [P, 512])
        MB16 = MB[:, :].bitcast(BF16)
        def bank(b, i):
            n = 4 * b + i
            if n < 4:
                return ST[:, n, :] if n < 3 else S[:, 2, :]
            return [S[:, 0, :], S[:, 1, :], UP[:, :], MB[:, :]][n - 4]

        def mlp_bank(b, c):
            return S[:, c % 2, :] if b == 0 else bank(b, c)

        def mlp_out_bank(b):
            return S[:, 0, :] if b == 0 else bank(b, 3)

        def norm_bank(site, b, i):
            return S[:, i, :] if (site, b) == (1, 0) else bank(b, i)

        def hidden_bank(b, c):
            if b == 0:
                return bank(0, c % HIDDEN_RING[0])
            return [bank(1, 0), bank(1, 1), bank(0, 2), bank(0, 3), bank(0, 0), bank(0, 1)][c % HIDDEN_RING[1]]

        def spread_bank(b, e):
            return bank(0, e) if b == 0 else [bank(1, 2), bank(1, 1), bank(0, 2)][e]

        scr_q = nc.dram_tensor("scr_q", [2 * B, 6, P, L], BF16, kind="Internal").ap()
        scr_k = nc.dram_tensor("scr_k", [B, 6, P, L], BF16, kind="Internal").ap()
        scr_kx = nc.dram_tensor("scr_kx", [6, P, B * LC], BF16, kind="Internal").ap()

        def ve(name, i=0, n=1):
            at = EARLY_AT["vec"] + VEC_AT[name] + i
            return w_early[:, at:at + n]

        def we(name, i=0, n=D):
            at = EARLY_AT[name] + i * D
            return w_early[:, at:at + n]

        def wl(name, i=0, n=D):
            at = LATE_AT[name] + i * D
            return w_late[:, at:at + n]

        names = """ld_x ld_early ld_xT ld_late ld_small consts ones_set zeros_set
            aff_ready aff_out stats_out rstd_in rstd_out bn_out normed_out normT_ready xnT_out0 xnT_out1
            q_ready k_ready v_ready q1_out k1_out v_out q2_out k2_out rest_q rest_k q3_out k3_out
            stack_q0 stack_q1 stack_k0 stack_k1 stack_qx0 stack_qx1 stack_kx strips_0 strips_1 strips_qx0 strips_qx1
            ctx_ready ctx_v_ready kx1_out kx_rest kx2_out kx3_out strips_kx vx_out kT1_out v1_out
            mod_step kfold_out small_ready small_out
            s_ready max_out mp1 mp2 mparts mrows_ready mT_out mrows_in0 mrows_in1
            st_ready exp_out u_ready u_out nat_ready rden_out o_out turn_ready oT_out
            proj_ready x_out qx_ready qx1_out rest_qx qx2_out qx3_out
            n_ready n_stats n_aggr n_var n_rstd n_normed nT_ready nT_out0 nT_out1
            f_ready f_out f2_ready x3_out l_s_ready l_max l_sub l_exp l_sum l_rec l_p l_pT l_pT_out
            l_ev l_ev_out r_ready r_lg r_mx r_sub r_exp r_sum r_rec r_p r_pT r_pT_out
            e_ready e_out pb_ready e_scaled e2_ready rt_out g2_ready g_out d_ready d_out y_out
            stored""".split()
        s = {n: sem(n) for n in names}

        block = ctx.enter_context(nc.Block())

        @block.sync
        def _(sp):
            sp.dma_start(xn[:, :, :], x_nat).then_inc(s["ld_x"], 16)
            sp.dma_start(w_early[:, :], early).then_inc(s["ld_early"], 16)
            sp.dma_start(w_late[:, :], late).then_inc(s["ld_late"], 16)
            sp.dma_start(xT[:, :, :], x_T).then_inc(s["ld_xT"], 16)
            sp.dma_start(rb_row[:, :], router_b).then_inc(s["ld_small"], 16)
            sp.dma_start(b2_rows[:, :], e_b2).then_inc(s["ld_small"], 16)

            def stack(scr, dense, runs, done, parts, n):
                for at, first, times in runs:
                    if first is None:
                        sp.wait_ge(s[parts[times - 1]], n)
                        src = dense[:, 0:times, :]
                    else:
                        sp.wait_ge(s[parts[first]], n)
                        src = dense[:, first:first + 1, :].to_broadcast([P, times, dense.shape[2]])
                    sp.dma_start(scr[at:at + times].rearrange("i p t -> p i t"), src).then_inc(done, 16)

            def strips(dst, scr, done):
                for q in range(2):
                    sp.dma_start(dst[STRIP * q:STRIP * q + STACK].rearrange("p k t -> p (k t)"),
                                 scr[:, 64 * q:64 * q + 64, :].rearrange("i (d k) t -> i d (k t)", d=DH)
                                 ).then_inc(done, 16)

            for b in range(B):
                stack(scr_q[b], part[:, 0, :, :], Q_RUNS, s[f"stack_q{b}"], ("q1_out", "q2_out", "q3_out"), b + 1)
                stack(scr_k[b], part[:, 1, :, :], K_RUNS, s[f"stack_k{b}"], ("k1_out", "k2_out", "k3_out"), b + 1)
                if b == 0:
                    sp.wait_ge(s["ones_set"], 2)
                sp.wait_ge(s[f"stack_q{b}"], STACK_DMAS)
                strips(QS[:, b, :, :], scr_q[b], s[f"strips_{b}"])
                sp.wait_ge(s[f"stack_k{b}"], STACK_DMAS)
                strips(KS[:, b, :, :], scr_k[b], s[f"strips_{b}"])
                if b == 0:
                    stack(scr_kx, partx[:, :, :], K_RUNS, s["stack_kx"], ("kx1_out", "kx2_out", "kx3_out"), 1)
            sp.wait_ge(s["stack_kx"], STACK_DMAS)
            strips(KX[:, :, :], scr_kx, s["strips_kx"])

            for i, step in enumerate(steps):
                if step[0] == "mrows":
                    kind, b, g = step[1:]
                    n = nth[i]
                    sp.wait_ge(s["mT_out"], n + 1)
                    dst = QS if kind == SELF else QX
                    for q in range(2):
                        row = STRIP * q + STACK
                        sp.dma_start(dst[row:row + PARTS, b, 2 * g:2 * g + 2, :],
                                     mT[2 * PARTS * q:2 * PARTS * (q + 1), n % 2, :]
                                     ).then_inc(s[f"mrows_in{n % 2}"], 16)
                elif step[0] == "queries":
                    b = step[1]
                    stack(scr_q[B + b], part[:, 0, :, :], Q_RUNS, s[f"stack_qx{b}"], ("qx1_out", "qx2_out", "qx3_out"), b + 1)
                    sp.wait_ge(s[f"stack_qx{b}"], STACK_DMAS)
                    strips(QX[:, b, :, :], scr_q[B + b], s[f"strips_qx{b}"])
            for b in range(B):
                sp.wait_ge(s["y_out"], b + 1)
                sp.dma_start(out_T[b], dT[:, b, :]).then_inc(s["stored"], 16)
            sp.wait_ge(s["stored"], 16 * B)

        

        @block.gpsimd
        def _(pool):
            g = nc.gpsimd
            g.memset(ident[:, :], 0.0).then_inc(s["zeros_set"], 1)
            g.memset(ident16[:, :], 0.0).then_inc(s["zeros_set"], 1)
            g.memset(pick[:, :, :], 0.0).then_inc(s["zeros_set"], 1)
            g.memset(half[:, :], -0.5).then_inc(s["zeros_set"], 1)
            g.memset(ones_row[:, :], 1.0).then_inc(s["consts"], 1)
            pool.wait_ge(s["zeros_set"], 4)
            for t in (ident, ident16):
                g.affine_select(out=t[:, :], in_=t[:, :], compare_op=ALU.not_equal, fill=1.0, base=0,
                                pattern=[[-1, P]], channel_multiplier=1).then_inc(s["consts"], 1)
            g.affine_select(out=pick[:, :, :], in_=pick[:, :, :], compare_op=ALU.not_equal, fill=1.0,
                            base=0, pattern=[[-1, E], [0, P]], channel_multiplier=1).then_inc(s["consts"], 1)
            for t in (KS[:, :, :, :], KX[:, :, :]):
                g.memset(t.bitcast(F32), TWO_ONES).then_inc(s["ones_set"], 1)
            pool.wait_ge(s["rstd_in"], 1)
            g.tensor_tensor(rstd[:, :], rstd[:, :], half[:, :], ALU.pow).then_inc(s["rstd_out"], 1)
            g.memset(VS[:, :, :, :], 0.0).then_inc(s["ones_set"], 1)
            g.memset(VX[:, :, :, :], 0.0).then_inc(s["ones_set"], 1)
            pool.wait_ge(s["ones_set"], 4)
            for t, lead in ((VS, B * QT), (VX, B)):
                v = t[:, :, :, :].rearrange("p a (r s j) c -> p (a r) s j c", s=2, j=HEADS)
                for sl in range(2):
                    g.memset(v[:, :, sl, :, 16 * sl + DH], 1.0).then_inc(s["ones_set"], 1)
            for i, step in enumerate(steps):
                if step[0] == "split":
                    n = nth[i]
                    sl = n % RING
                    k, b, grp = step[1:]
                    pool.wait_ge(s["max_out"], event_at[(k, b, grp), EVENTS[k] - 1] + 1)
                    if n >= RING:
                        pool.wait_ge(s["mrows_ready"], n - RING + 1)
                    g.tensor_copy(mpart[:, sl, :, :, 0, :], negm[:, sl, :, :, :]).then_inc(s["mp1"], 1)
                    pool.wait_ge(s["mp1"], 2 * n + 1)
                    g.tensor_tensor(mrest[:, sl, :, :, :], negm[:, sl, :, :, :], mpart[:, sl, :, :, 0, :], ALU.subtract).then_inc(s["mp1"], 1)
                    pool.wait_ge(s["mp1"], 2 * n + 2)
                    g.tensor_copy(mpart[:, sl, :, :, 1, :], mrest[:, sl, :, :, :]).then_inc(s["mp2"], 1)
                    pool.wait_ge(s["mp2"], n + 1)
                    g.tensor_tensor(mpart[:, sl, :, :, 2, :], mrest[:, sl, :, :, :], mpart[:, sl, :, :, 1, :], ALU.subtract).then_inc(s["mparts"], 1)
                elif step[0] == "norm":
                    b = step[2]
                    pool.wait_ge(s["n_var"], nth[i] + 1)
                    g.tensor_tensor(rstd[:, b * QT:(b + 1) * QT], rstd[:, b * QT:(b + 1) * QT],
                                    half[:, b * QT:(b + 1) * QT], ALU.pow).then_inc(s["n_rstd"], 1)

        @block.tensor
        def _(pe):
            mm = nc.tensor.matmul
            pe.wait_ge(s["consts"], 4)
            pe.wait_ge(s["ld_early"], 16)
            cond = ve("cond", 0, B)
            for i in range(2):
                last = mm(MB[:, B * i:B * i + B], we("aff1_w", i), cond, start=True, stop=True)
            last.then_inc(s["aff_ready"], 1)
            wide = ident16[:, :].unsqueeze(1).to_broadcast([P, QT, P])
            for _ in range(OPENING):
                mm(UP[:, :], ident16[:, :], wide, start=True, stop=True)
            for b in range(B):
                for t in range(QT):
                    pe.wait_ge(s["normed_out"], b * QT + t + 1)
                    last = nc.tensor.transpose(ST[:, b, t * P:(t + 1) * P], normed[:, b * QT + t, :], ident[:, :])
                last.then_inc(s["normT_ready"], 1)
            for b in range(B):
                pe.wait_ge(s[f"xnT_out{b}"], 1)
                mm(ST[:, 2 * b, :] if b else S[:, 0, :], we("sa_qw"), xnT[:, b, :], start=True, stop=True).then_inc(s["q_ready"], 1)
                mm(S[:, 1 + b, :], we("sa_kw"), xnT[:, b, :], start=True, stop=True).then_inc(s["k_ready"], 1)
                if b:
                    pe.wait_ge(s["v_out"], 2)
                for t in range(QT):
                    last = mm(UP[:, t * P:(t + 1) * P], xnT[:, b, t * P:(t + 1) * P], we("sa_vw"), start=True, stop=True)
                last.then_inc(s["v_ready"], 1)
            pe.wait_ge(s["ld_late"], 16)
            ctxT = wl("ctxT", 0, B * LC)
            pe.wait_ge(s["aff_out"], 1)
            mm(MB[:, 0:B * LC], wl("ca_kw"), ctxT, start=True, stop=True)
            mm(MB[:, B * LC:2 * B * LC], wl("Wk"), ctxT, start=True, stop=True).then_inc(s["ctx_ready"], 1)
            for b in range(B):
                c = ctxT[:, b * LC:(b + 1) * LC]
                mm(ST[0:LC, 0, b * D:(b + 1) * D], c, wl("ca_vw"), start=True, stop=True)
                last = mm(ST[0:LC, 0, (B + b) * D:(B + b + 1) * D], c, wl("Wv"), start=True, stop=True)
            last.then_inc(s["ctx_v_ready"], 1)
            pe.wait_ge(s["kT1_out"], 1)
            mm(ST[:, 1, 0:B * LC], wl("WqT"), kT1[:, :], start=True, stop=True)
            at = B * LC
            for i in range(2):
                mm(ST[:, 1, at + B * i:at + B * i + B], wl("aff2_w", i), cond, start=True, stop=True)
            at += 2 * B
            mm(ST[:, 1, at:at + 1], wl("sa_ow"), ve("sa_vb"), start=True, stop=True)
            mm(ST[:, 1, at + 1:at + 2], wl("ca_ow"), ve("ca_vb"), start=True, stop=True)
            at += 2
            for c in range(E * RC + 1):
                w = e_w1(wl, c, 2)
                mm(ST[:, 1, at + B * c:at + B * c + B], w, cond, start=True, stop=True)
            at += B * (E * RC + 1)
            pe.wait_ge(s["ld_small"], 32)
            for b in range(B):
                o = ST[:, 1, at + E * b:at + E * b + E]
                mm(o, cond[:, b:b + 1].to_broadcast([P, P]), router_w(w_late, 2), start=True, stop=False)
                last = mm(o, ones_row[:, :], rb_row[:, :], start=False, stop=True)
            last.then_inc(s["small_ready"], 1)

            def maxima(unit, e):
                kind, b, g = unit
                n = event_at[unit, e]
                if n == 0:
                    pe.wait_ge(s["rest_q"], 1)
                    pe.wait_ge(s["rest_k"], 1)
                    pe.wait_ge(s["ones_set"], 8)
                if kind == SELF:
                    pe.wait_ge(s[f"strips_{b}"], 2 * STRIP_DMAS)
                else:
                    pe.wait_ge(s[f"strips_qx{b}"], STRIP_DMAS)
                    pe.wait_ge(s["strips_kx"], STRIP_DMAS)
                if n == 2:
                    pe.wait_ge(s["rest_k"], B)
                if n >= 3:
                    pe.wait_ge(s["max_out"], n - 2)
                p = e % 2
                r = slice(STRIP * p, STRIP * p + STACK)
                if kind == SELF:
                    i, jj = e // 4, e // 2 % 2
                    last = mm(S[:, n % 3, :], QS[r, b, 2 * g + jj, i * P:(i + 1) * P],
                              KS[r, b, 2 * g + jj, :], start=True, stop=True)
                else:
                    for t in range(2):
                        for jj in range(2):
                            q0 = (2 * (e // 2) + t) * P
                            last = mm(S[:, n % 3, (2 * t + jj) * LC:(2 * t + jj + 1) * LC],
                                      QX[r, b, 2 * g + jj, q0:q0 + P], KX[r, 2 * g + jj, b * LC:(b + 1) * LC],
                                      start=True, stop=True)
                last.then_inc(s["s_ready"], 1)

            def scores(unit, kt, n, j):
                kind, b, g = unit
                if n == 0:
                    pe.wait_ge(s["rest_q"], B)
                    pe.wait_ge(s["small_out"], 1)
                    pe.wait_ge(s["v1_out"], 1)
                m = mrows_nth[unit]
                pe.wait_ge(s[f"mrows_in{m % 2}"], 32 * (m // 2 + 1))
                k = HEADS * n + j
                if k >= 3:
                    pe.wait_ge(s["exp_out"], k - 2)
                r = slice(STRIP * (j % 2), STRIP * (j % 2) + STACK + PARTS)
                block = 2 * g + j // 2
                if kind == SELF:
                    mm(ST[:, k % 3, :], KS[r, b, block, kt * P:(kt + 1) * P], QS[r, b, block, :],
                       start=True, stop=True).then_inc(s["st_ready"], 1)
                else:
                    mm(ST[0:LC, k % 3, :], KX[r, block, b * LC:(b + 1) * LC], QX[r, b, block, :],
                       start=True, stop=True).then_inc(s["st_ready"], 1)

            def values(unit, kt, n):
                kind, b, g = unit
                nk = QT if kind == SELF else 1
                first = g % 2 == 0 and kt == 0
                final = g % 2 == 1 and kt == nk - 1
                w = (kind * B + b) * 2 + g // 2
                if first:
                    if w:
                        pe.wait_ge(s["u_out"], w)
                    else:
                        pe.wait_ge(s["v_out"], 2 * B)
                    if kind == CROSS:
                        pe.wait_ge(s["vx_out"], 2)
                pe.wait_ge(s["exp_out"], HEADS * (n + 1))
                for j in range(HEADS):
                    h = HEADS * g + j
                    if kind == SELF:
                        last = mm(UP[32 * j:32 * j + 32, :], VS[:, b * QT + kt, h, :], PT[:, n % 2, j, :],
                                  start=first, stop=final)
                    else:
                        last = mm(UP[32 * j:32 * j + 32, :], VX[:, b, h, :], PT[0:LC, n % 2, j, :],
                                  start=first, stop=final)
                last.then_inc(s["u_ready"], 1)

            for i, step in enumerate(steps):
                kind = step[0]
                if kind in TURNS and bank_reader[i]:
                    pe.wait_ge(s[bank_reader[i][0]], bank_reader[i][1])
                elif kind in TURNS:
                    pe.wait_ge(s["kT1_out"], 1)
                    pe.wait_ge(s["kx_rest"], 1)
                if kind == "maxima":
                    maxima(*step[1:])
                elif kind == "open":
                    for _ in range(step[1]):
                        mm(ST[:, 2, :], KS[:, 0, 0, 0:P], KS[:, 0, 0, :], start=True, stop=True)
                elif kind == "warm":
                    if nth[i] == 0:
                        pe.wait_ge(s["v_out"], 2 * B)
                        pe.wait_ge(s[f"strips_0"], 2 * STRIP_DMAS)
                    for _ in range(2):
                        mm(UP[:, :], KS[:, 0, 0, 0:P], KS[:, 0, 0, :], start=True, stop=True)
                elif kind == "scores":
                    scores(*step[1:])
                elif kind == "values":
                    values(*step[1:])
                elif kind == "mrows":
                    n = split_nth[step[1:]]
                    pe.wait_ge(s["mparts"], n + 1)
                    for t in range(QT):
                        last = nc.tensor.transpose(MB16[0:PARTS * HEADS, t * P:(t + 1) * P],
                                                   mpart[:, n % RING, t, :, :, :].rearrange("p q i j -> p (q i j)"), ident16[:, :])
                    last.then_inc(s["mrows_ready"], 1)
                elif kind == "natural":
                    n = nth[i]
                    pe.wait_ge(s["u_out"], n + 1)
                    for t in range(QT):
                        last = nc.tensor.transpose(MB[:, t * P:(t + 1) * P], U[:, n % 2, t * P:(t + 1) * P], ident[:, :])
                    last.then_inc(s["nat_ready"], 1)
                elif kind == "turn":
                    pe.wait_ge(s["o_out"], 2 * nth[i] + 2)
                    for t in range(QT):
                        last = nc.tensor.transpose(MB[:, t * P:(t + 1) * P], O[:, t, :], ident[:, :])
                    last.then_inc(s["turn_ready"], 1)
                elif kind == "project":
                    pe.wait_ge(s["oT_out"], nth[i] + 1)
                    mm(MB[:, :], wl("sa_ow" if step[1] == SELF else "ca_ow"), OT[:, :], start=True, stop=True).then_inc(s["proj_ready"], 1)
                elif kind == "queries":
                    b = step[1]
                    pe.wait_ge(s["x_out"], b + 1)
                    mm(MB[:, :], wl("ca_qw"), xT[:, b, :], start=True, stop=True).then_inc(s["qx_ready"], 1)

                elif kind == "norm":
                    site, b = step[1:]
                    if site == 0:
                        pe.wait_ge(s["x_out"], residual_nth[CROSS, b] + 1)
                        if b == 0:
                            pe.wait_ge(s["exp_out"], HEADS * CROSS_1)
                        else:
                            pe.wait_ge(s["nT_out0"], 2)
                    else:
                        pe.wait_ge(s["x3_out"], b + 1)
                    for t in range(QT):
                        last = nc.tensor.transpose(norm_bank(site, b, 0)[:, t * P:(t + 1) * P], xT[:, b, t * P:(t + 1) * P], ident[:, :])
                    last.then_inc(s["n_ready"], 1)
                elif kind == "norm_back":
                    site, b = step[1:]
                    pe.wait_ge(s["n_normed"], norm_nth[site, b] + 1)
                    for t in range(QT):
                        last = nc.tensor.transpose(norm_bank(site, b, 1)[:, t * P:(t + 1) * P], normed[:, b * QT + t, :], ident[:, :])
                    last.then_inc(s["nT_ready"], 1)
                elif kind == "ffn1":
                    b, c = step[1:]
                    if c == 0:
                        pe.wait_ge(s[f"nT_out{b}"], 1)
                        if b == 0:
                            pe.wait_ge(s["max_out"], len(event_at))
                    elif b == 0 and c >= 2:
                        pe.wait_ge(s["f_out"], c - 1)
                    mm(mlp_bank(b, c), wl("ffn_w1", c), xnT[:, b, :], start=True, stop=True).then_inc(s["f_ready"], 1)
                elif kind == "ffn2":
                    b, c = step[1:]
                    pe.wait_ge(s["f_out"], NF * (b + 1) if c == 0 else NF * b + c + 1)
                    last = mm(mlp_out_bank(b), wl("ffn_w2", c), hT[:, b, c, :], start=(c == 0), stop=(c == NF - 1))
                    if c == NF - 1:
                        last.then_inc(s["f2_ready"], 1)
                elif kind == "context":
                    b = step[1]
                    pe.wait_ge(s[f"nT_out{b}"], 2)
                    if b == 0:
                        pe.wait_ge(s["exp_out"], HEADS * ROUNDS)
                    for t in range(QT):
                        last = mm(bank(b, 2)[:, t * LC:(t + 1) * LC], xnT[:, b, t * P:(t + 1) * P],
                                  kfold[:, b * LC:(b + 1) * LC], start=True, stop=True)
                    last.then_inc(s["l_s_ready"], 1)
                elif kind == "context_probs":
                    b = step[1]
                    pe.wait_ge(s["l_p"], b + 1)
                    for t in range(QT):
                        last = nc.tensor.transpose(bank(b, 3)[0:LC, t * P:(t + 1) * P], s1[:, b, t, :], ident[:, :])
                    last.then_inc(s["l_pT"], 1)
                elif kind == "context_value":
                    b = step[1]
                    pe.wait_ge(s["l_pT_out"], b + 1)
                    mm(bank(b, 2), v1[:, b, :], p1T[:, b, :], start=True, stop=True).then_inc(s["l_ev"], 1)
                elif kind == "router":
                    b = step[1]
                    pe.wait_ge(s["l_ev_out"], b + 1)
                    for t in range(QT):
                        o = bank(b, 3)[:, t * E:(t + 1) * E]
                        mm(o, xnT[:, b, t * P:(t + 1) * P], router_w(w_late, 0), start=True, stop=False)
                        last = mm(o, evT[:, b, t * P:(t + 1) * P], router_w(w_late, 1), start=False, stop=True)
                    last.then_inc(s["r_ready"], 1)
                elif kind == "hidden_x":
                    b, c = step[1:]
                    if c >= HIDDEN_RING[b]:
                        pe.wait_ge(s["e_out"], b * NE + c - HIDDEN_RING[b] + 1)
                    elif b == 1 and c == 3:
                        pe.wait_ge(s["rt_out"], 1)
                    elif b == 1 and c == 4:
                        pe.wait_ge(s["g_out"], 1)
                    elif b == 1 and c == 5:
                        pe.wait_ge(s["d_out"], 1)
                    mm(hidden_bank(b, c), e_w1(wl, c, 0), xnT[:, b, :], start=True, stop=False)
                elif kind == "hidden_ev":
                    b, c = step[1:]
                    pe.wait_ge(s["l_ev_out"], b + 1)
                    mm(hidden_bank(b, c), e_w1(wl, c, 1), evT[:, b, :], start=False, stop=True).then_inc(s["e_ready"], 1)
                elif kind == "router_probs":
                    b = step[1]
                    pe.wait_ge(s["r_p"], b + 1)
                    for t in range(QT):
                        last = nc.tensor.transpose(bank(b, 3)[0:E, t * P:(t + 1) * P], lg[:, b, t, :], ident[:, :])
                    last.then_inc(s["r_pT"], 1)
                elif kind == "spread":
                    b = step[1]
                    pe.wait_ge(s["e_out"], NE if b == 0 else NE + E)
                    pe.wait_ge(s["r_pT_out"], b + 1)
                    for e in range(E):
                        mm(spread_bank(b, e), pick[:, e, :], prT[:, b, :], start=True, stop=True).then_inc(s["pb_ready"], 1)
                    mm(bank(b, 3), b2_rows[:, :], prT[:, b, :], start=True, stop=False)
                elif kind == "combine":
                    b, c = step[1:]
                    pe.wait_ge(s["e_scaled"], b * E * RC + c + 1)
                    last = mm(bank(b, 3), wl("e_w2", c), eh[:, b, c, :], start=False, stop=(c == E * RC - 1))
                    if c == E * RC - 1:
                        last.then_inc(s["e2_ready"], 1)
                elif kind == "out":
                    b = step[1]
                    pe.wait_ge(s["e_out"], (b + 1) * NE)
                    mm(bank(b, 0), wl("gate_w2"), eh[:, b, E * RC, :], start=True, stop=True).then_inc(s["g2_ready"], 1)
                    pe.wait_ge(s["rt_out"], b + 1)
                    mm(bank(b, 1), wl("out_w"), rtT[:, b, :], start=True, stop=True).then_inc(s["d_ready"], 1)

        @block.scalar
        def _(act):
            a = nc.scalar.activation

            def first_part(ps, bias, dense, out_sem):
                a(dense, ps, ACT.Identity, bias=bias).then_inc(out_sem, 1)

            act.wait_ge(s["consts"], 4)
            a(unread[:, :], half[:, :], ACT.Identity)
            act.wait_ge(s["ld_early"], 16)
            act.wait_ge(s["aff_out"], 1)
            act.wait_ge(s["normT_ready"], 1)
            a(xnT[:, 0, :], ST[:, 0, :], ACT.Identity, bias=lnB[:, 0, 0:1], scale=lnA[:, 0, 0:1]).then_inc(s["xnT_out0"], 1)
            def values_out(b):
                act.wait_ge(s["v_ready"], b + 1)
                act.wait_ge(s["ones_set"], 8)
                dst = VS[:, b * QT:(b + 1) * QT, :, :].rearrange("p a (r s j) c -> p (a r) s j c", s=2, j=HEADS)
                src = UP[:, :].rearrange("p (ar s j d) -> p ar s j d", s=2, j=HEADS, d=DH)
                for sl in range(2):
                    nc.scalar.copy(dst[:, :, sl, :, 16 * sl:16 * sl + DH], src[:, :, sl, :, :]).then_inc(s["v_out"], 1)

            act.wait_ge(s["q_ready"], 1)
            first_part(S[:, 0, :], ve("sa_qb"), part[:, 0, 0, :], s["q1_out"])
            act.wait_ge(s["k_ready"], 1)
            first_part(S[:, 1, :], ve("sa_kb"), part[:, 1, 0, :], s["k1_out"])
            values_out(0)
            values_out(1)
            act.wait_ge(s["ctx_ready"], 1)
            nc.scalar.copy(kT1[:, :], MB[:, B * LC:2 * B * LC]).then_inc(s["kT1_out"], 1)
            first_part(MB[:, 0:B * LC], ve("ca_kb"), partx[:, 0, :], s["kx1_out"])
            act.wait_ge(s["ctx_v_ready"], 1)
            dst = VX[:, :, :, :].rearrange("p a (r s j) c -> p (a r) s j c", s=2, j=HEADS)
            src = ST[0:LC, 0, 0:B * D].rearrange("p (ar s j d) -> p ar s j d", s=2, j=HEADS, d=DH)
            for sl in range(2):
                nc.scalar.copy(dst[:, :, sl, :, 16 * sl:16 * sl + DH], src[:, :, sl, :, :]).then_inc(s["vx_out"], 1)
            nc.scalar.copy(v1[:, :, :], ST[0:LC, 0, B * D:2 * B * D].rearrange("p (b d) -> p b d", b=B)).then_inc(s["v1_out"], 1)
            act.wait_ge(s["stack_q0"], STACK_DMAS)
            first_part(ST[:, 2, :], ve("sa_qb"), part[:, 0, 0, :], s["q1_out"])
            act.wait_ge(s["stack_k0"], STACK_DMAS)
            first_part(S[:, 2, :], ve("sa_kb"), part[:, 1, 0, :], s["k1_out"])

            for i, step in enumerate(steps):
                kind = step[0]
                if kind == "exps":
                    unit, kt, n, j = step[1:]
                    rows = P if unit[0] == SELF else LC
                    if n >= 2 and j == 0:
                        act.wait_ge(s["u_ready"], n - 1)
                    k = HEADS * n + j
                    act.wait_ge(s["st_ready"], k + 1)
                    a(PT[0:rows, n % 2, j, :], ST[0:rows, k % 3, :], ACT.Exp, scale=SCALE).then_inc(s["exp_out"], 1)
                elif kind == "mrows":
                    n = nth[i]
                    act.wait_ge(s["mrows_ready"], n + 1)
                    if n >= 2:
                        act.wait_ge(s[f"mrows_in{n % 2}"], 32 * (n // 2))
                    nc.scalar.copy(mT[:, n % 2, :], MB16[0:PARTS * HEADS, 0:L]).then_inc(s["mT_out"], 1)
                elif kind == "gather":
                    n = nth[i]
                    unit_n = last_round(steps, step)
                    act.wait_ge(s["u_ready"], unit_n + 1)
                    if n >= 2:
                        act.wait_ge(s["nat_ready"], n - 1)
                    nc.scalar.copy(U[:, n % 2, :], UP[:, :]).then_inc(s["u_out"], 1)
                elif kind == "turn":
                    act.wait_ge(s["turn_ready"], nth[i] + 1)
                    if nth[i]:
                        act.wait_ge(s["proj_ready"], nth[i])
                    nc.scalar.copy(OT[:, :], MB[:, :]).then_inc(s["oT_out"], 1)
                elif kind == "queries":
                    b = step[1]
                    act.wait_ge(s["qx_ready"], b + 1)
                    act.wait_ge(s["stack_qx0"] if b else s["stack_q1"], STACK_DMAS)
                    first_part(MB[:, :], ve("ca_qb"), part[:, 0, 0, :], s["qx1_out"])

                elif kind == "norm_back":
                    site, b = step[1:]
                    act.wait_ge(s["nT_ready"], norm_nth[site, b] + 1)
                    if site == 0:
                        scale, bias = lnA[:, 1, b:b + 1], lnB[:, 1, b:b + 1]
                    else:
                        scale, bias = ve("ln_gamma"), ve("ln_beta")
                    a(xnT[:, b, :], norm_bank(site, b, 1), ACT.Identity, bias=bias, scale=scale).then_inc(s[f"nT_out{b}"], 1)
                elif kind == "ffn1":
                    b, c = step[1:]
                    act.wait_ge(s["f_ready"], b * NF + c + 1)
                    a(hT[:, b, c, :], mlp_bank(b, c), ACT.Gelu, bias=ve("ffn_b1", c)).then_inc(s["f_out"], 1)
                elif kind == "context":
                    b = step[1]
                    act.wait_ge(s["l_sub"], b + 1)
                    a(s1[:, b, :, :], s1[:, b, :, :], ACT.Exp, scale=SCALE1).then_inc(s["l_exp"], 1)
                elif kind == "context_probs":
                    b = step[1]
                    act.wait_ge(s["l_pT"], b + 1)
                    nc.scalar.copy(p1T[:, b, :], bank(b, 3)[0:LC, :]).then_inc(s["l_pT_out"], 1)
                elif kind == "context_value":
                    b = step[1]
                    act.wait_ge(s["l_ev"], b + 1)
                    nc.scalar.copy(evT[:, b, :], bank(b, 2)).then_inc(s["l_ev_out"], 1)
                elif kind == "router":
                    b = step[1]
                    act.wait_ge(s["r_sub"], b + 1)
                    a(lg[:, b, :, :], lg[:, b, :, :], ACT.Exp).then_inc(s["r_exp"], 1)
                elif kind == "hidden_ev":
                    b, c = step[1:]
                    act.wait_ge(s["e_ready"], nth[i] + 1)
                    a(eh[:, b, c, :], hidden_bank(b, c), ACT.Silu, bias=hbias[:, c, b:b + 1]).then_inc(s["e_out"], 1)
                elif kind == "out":
                    b = step[1]
                    act.wait_ge(s["g2_ready"], b + 1)
                    a(gT[:, b, :], bank(b, 0), ACT.Sigmoid, bias=ve("gate_b2")).then_inc(s["g_out"], 1)

        @block.vector
        def _(dve):
            v = nc.vector
            dve.wait_ge(s["ld_x"], 16)
            for t in range(B * QT):
                v.bn_stats(stats[:, t, :], xn[:, t, :]).then_inc(s["bn_out"], 1)
            for t in range(B * QT):
                dve.wait_ge(s["bn_out"], t + 1)
                last = v.bn_aggr(mv[:, t, :], stats[:, t, :])
            last.then_inc(s["stats_out"], 1)
            dve.wait_ge(s["stats_out"], 1)
            v.tensor_scalar(rstd[:, :], mv[:, :, 1], EPS, None, ALU.add).then_inc(s["rstd_in"], 1)
            dve.wait_ge(s["aff_ready"], 1)
            modulation(dve, v, s, aff, lnA, lnB, MB[:, 0:2 * B], ve, 0, "aff1_b", "ln1_g", "ln1_b", s["aff_out"])
            dve.wait_ge(s["rstd_out"], 1)
            for t in range(B * QT):
                v.tensor_scalar(normed[:, t, :], xn[:, t, :], mv[:, t, 0:1], rstd[:, t:t + 1],
                                ALU.subtract, ALU.mult).then_inc(s["normed_out"], 1)
            dve.wait_ge(s["normT_ready"], 2)
            dve.wait_ge(s["aff_out"], 1)
            v.tensor_scalar(xnT[:, 1, :], ST[:, 1, :], lnA[:, 0, 1:2], lnB[:, 0, 1:2], ALU.mult, ALU.add).then_inc(s["xnT_out1"], 1)

            def later_parts(ps, bias, dense, rem, n, outs):
                first, r, second, third = [s[x] for x in outs]
                dve.wait_ge(first, n)
                v.scalar_tensor_tensor(rem, ps, bias, dense[:, 0, :], ALU.add, ALU.subtract).then_inc(r, 1)
                dve.wait_ge(r, n)
                v.tensor_copy(dense[:, 1, :], rem).then_inc(second, 1)
                dve.wait_ge(second, n)
                v.tensor_tensor(dense[:, 2, :], rem, dense[:, 1, :], ALU.subtract).then_inc(third, 1)

            Q_OUTS = ("q1_out", "rest_q", "q2_out", "q3_out")
            K_OUTS = ("k1_out", "rest_k", "k2_out", "k3_out")
            later_parts(S[:, 0, :], ve("sa_qb"), part[:, 0, :, :], rest[:, 0, :], 1, Q_OUTS)
            later_parts(S[:, 1, :], ve("sa_kb"), part[:, 1, :, :], rest[:, 1, :], 1, K_OUTS)
            later_parts(MB[:, 0:B * LC], ve("ca_kb"), partx[:, :, :], restx[:, :], 1,
                        ("kx1_out", "kx_rest", "kx2_out", "kx3_out"))
            later_parts(ST[:, 2, :], ve("sa_qb"), part[:, 0, :, :], rest[:, 0, :], 2, Q_OUTS)
            later_parts(S[:, 2, :], ve("sa_kb"), part[:, 1, :, :], rest[:, 1, :], 2, K_OUTS)
            dve.wait_ge(s["small_ready"], 1)
            v.tensor_copy(kfold[:, :], ST[:, 1, 0:B * LC]).then_inc(s["kfold_out"], 1)
            at = B * LC
            modulation(dve, v, s, aff, lnA, lnB, ST[:, 1, at:at + 2 * B], ve, 1, "aff2_b", "ln2_g", "ln2_b", s["aff_out"])
            at += 2 * B
            v.tensor_tensor(csa[:, 0:1], ST[:, 1, at:at + 1], ve("sa_ob"), ALU.add)
            v.tensor_tensor(csa[:, 1:2], ST[:, 1, at + 1:at + 2], ve("ca_ob"), ALU.add)
            at += 2
            for b in range(B):
                hp = ST[:, 1, at:at + B * NE].rearrange("p (c b) -> p c b", b=B)
                v.tensor_tensor(hbias[:, 0:NE - 1, b], hp[:, 0:NE - 1, b], ve("e_b1", 0, NE - 1), ALU.add)
                v.tensor_tensor(hbias[:, NE - 1:NE, b], hp[:, NE - 1:NE, b], ve("gate_b1"), ALU.add)
            at += B * NE
            v.tensor_copy(rbias[:, :, :], ST[:, 1, at:at + B * E].rearrange("p (b e) -> p b e", b=B)).then_inc(s["small_out"], 1)

            for i, step in enumerate(steps):
                kind = step[0]
                if kind == "maxima":
                    (k, b, g), e = step[1:]
                    n = event_at[step[1:]]
                    slot = split_nth[(k, b, g)] % RING
                    dve.wait_ge(s["s_ready"], n + 1)
                    if k == SELF:
                        v.tensor_reduce(negm[:, slot, e // 4, e % 2, e // 2 % 2:e // 2 % 2 + 1], S[:, n % 3, :], AX.X,
                                        ALU.max, negate=True).then_inc(s["max_out"], 1)
                    else:
                        c = 2 * (e // 2)
                        v.tensor_reduce(negm[:, slot, c:c + 2, e % 2, :],
                                        S[:, n % 3, 0:4 * LC].rearrange("p (t jj k) -> p t jj k", t=2, jj=2), AX.X,
                                        ALU.max, negate=True).then_inc(s["max_out"], 1)
                elif kind == "normalise":
                    n = nth[i]
                    k, b, r = step[1:]
                    dve.wait_ge(s["nat_ready"], n + 1)
                    t4 = MB[:, :].rearrange("p (t j s c) -> p t j s c", t=QT, j=HEADS, s=2)
                    v.reciprocal(rden[:, n % 2, :, :], MB[:, :].rearrange("p (t js c) -> p t js c", t=QT, c=16)[:, :, :, DH]).then_inc(s["rden_out"], 1)
                    dve.wait_ge(s["rden_out"], n + 1)
                    if r == 0 and n >= 2:
                        dve.wait_ge(s["turn_ready"], n // 2)
                    for sl in range(2):
                        o = O[:, :, :].rearrange("p t (r s j d) -> p t r s j d", r=2, s=2, j=HEADS)[:, :, r, sl, :, :]
                        rd = rden[:, n % 2, :, :].rearrange("p t (j s) -> p t j s", s=2)[:, :, :, sl]
                        last = v.tensor_tensor(o, t4[:, :, :, sl, 0:DH],
                                               rd.unsqueeze(3).to_broadcast([P, QT, HEADS, DH]), ALU.mult)
                    last.then_inc(s["o_out"], 1)
                elif kind == "residual":
                    k, b = step[1:]
                    n = nth[i]
                    dve.wait_ge(s["proj_ready"], n + 1)
                    if n == 0:
                        dve.wait_ge(s["ld_xT"], 16)
                    v.scalar_tensor_tensor(xT[:, b, :], MB[:, :], csa[:, k:k + 1], xT[:, b, :], ALU.add, ALU.add).then_inc(s["x_out"], 1)
                elif kind == "rests":
                    b = step[1]
                    later_parts(MB[:, :], ve("ca_qb"), part[:, 0, :, :], rest[:, 0, :], b + 1,
                                ("qx1_out", "rest_qx", "qx2_out", "qx3_out"))

                elif kind == "norm":
                    site, b = step[1:]
                    n = nth[i]
                    dve.wait_ge(s["n_ready"], n + 1)
                    for t in range(QT):
                        last = v.bn_stats(stats[:, b * QT + t, :], norm_bank(site, b, 0)[:, t * P:(t + 1) * P])
                    last.then_inc(s["n_stats"], 1)
                    dve.wait_ge(s["n_stats"], n + 1)
                    for t in range(QT):
                        last = v.bn_aggr(mv[:, b * QT + t, :], stats[:, b * QT + t, :])
                    last.then_inc(s["n_aggr"], 1)
                    dve.wait_ge(s["n_aggr"], n + 1)
                    v.tensor_scalar(rstd[:, b * QT:(b + 1) * QT], mv[:, b * QT:(b + 1) * QT, 1], EPS, None, ALU.add).then_inc(s["n_var"], 1)
                elif kind == "norm_back":
                    site, b = step[1:]
                    dve.wait_ge(s["n_rstd"], norm_nth[site, b] + 1)
                    for t in range(QT):
                        k = b * QT + t
                        last = v.tensor_scalar(normed[:, k, :], norm_bank(site, b, 0)[:, t * P:(t + 1) * P], mv[:, k, 0:1],
                                               rstd[:, k:k + 1], ALU.subtract, ALU.mult)
                    last.then_inc(s["n_normed"], 1)
                elif kind == "ffn2" and step[2] == NF - 1:
                    b = step[1]
                    dve.wait_ge(s["f2_ready"], b + 1)
                    v.scalar_tensor_tensor(xT[:, b, :], mlp_out_bank(b), ve("ffn_b2"), xT[:, b, :], ALU.add, ALU.add).then_inc(s["x3_out"], 1)
                elif kind == "context":
                    b = step[1]
                    sc = bank(b, 2)[:, 0:QT * LC].rearrange("p (t k) -> p t k", t=QT)
                    dve.wait_ge(s["l_s_ready"], b + 1)
                    v.tensor_reduce(mx1[:, b, :], sc, AX.X, ALU.max).then_inc(s["l_max"], 1)
                    dve.wait_ge(s["l_max"], b + 1)
                    v.tensor_tensor(s1[:, b, :, :], sc, mx1[:, b, :].unsqueeze(2).to_broadcast([P, QT, LC]), ALU.subtract).then_inc(s["l_sub"], 1)
                elif kind == "context_probs":
                    b = step[1]
                    dve.wait_ge(s["l_exp"], b + 1)
                    v.tensor_reduce(sum1[:, b, :], s1[:, b, :, :], AX.X, ALU.add).then_inc(s["l_sum"], 1)
                    dve.wait_ge(s["l_sum"], b + 1)
                    v.reciprocal(rec1[:, b, :], sum1[:, b, :]).then_inc(s["l_rec"], 1)
                    dve.wait_ge(s["l_rec"], b + 1)
                    v.tensor_tensor(s1[:, b, :, :], s1[:, b, :, :], rec1[:, b, :].unsqueeze(2).to_broadcast([P, QT, LC]), ALU.mult).then_inc(s["l_p"], 1)
                elif kind == "router":
                    b = step[1]
                    dve.wait_ge(s["r_ready"], b + 1)
                    v.tensor_tensor(lg[:, b, :, :], bank(b, 3)[:, 0:QT * E].rearrange("p (t e) -> p t e", t=QT),
                                    rbias[:, b, :].unsqueeze(1).to_broadcast([P, QT, E]), ALU.add).then_inc(s["r_lg"], 1)
                    dve.wait_ge(s["r_lg"], b + 1)
                    v.tensor_reduce(rmx[:, b, :], lg[:, b, :, :], AX.X, ALU.max).then_inc(s["r_mx"], 1)
                    dve.wait_ge(s["r_mx"], b + 1)
                    v.tensor_tensor(lg[:, b, :, :], lg[:, b, :, :], rmx[:, b, :].unsqueeze(2).to_broadcast([P, QT, E]), ALU.subtract).then_inc(s["r_sub"], 1)
                elif kind == "router_probs":
                    b = step[1]
                    dve.wait_ge(s["r_exp"], b + 1)
                    v.tensor_reduce(rsum[:, b, :], lg[:, b, :, :], AX.X, ALU.add).then_inc(s["r_sum"], 1)
                    dve.wait_ge(s["r_sum"], b + 1)
                    v.reciprocal(rrec[:, b, :], rsum[:, b, :]).then_inc(s["r_rec"], 1)
                    dve.wait_ge(s["r_rec"], b + 1)
                    v.tensor_tensor(lg[:, b, :, :], lg[:, b, :, :], rrec[:, b, :].unsqueeze(2).to_broadcast([P, QT, E]), ALU.mult).then_inc(s["r_p"], 1)
                    dve.wait_ge(s["r_pT"], b + 1)
                    v.tensor_copy(prT[:, b, :], bank(b, 3)[0:E, :]).then_inc(s["r_pT_out"], 1)
                elif kind == "spread":
                    b = step[1]
                    for e in range(E):
                        dve.wait_ge(s["pb_ready"], b * E + e + 1)
                        for c in range(RC):
                            k = e * RC + c
                            dve.wait_ge(s["e_out"], b * NE + k + 1)
                            v.tensor_tensor(eh[:, b, k, :], eh[:, b, k, :], spread_bank(b, e), ALU.mult).then_inc(s["e_scaled"], 1)
                elif kind == "routed":
                    b = step[1]
                    dve.wait_ge(s["e2_ready"], b + 1)
                    v.tensor_copy(rtT[:, b, :], bank(b, 3)).then_inc(s["rt_out"], 1)
                elif kind == "out":
                    b = step[1]
                    dve.wait_ge(s["d_ready"], b + 1)
                    dve.wait_ge(s["g_out"], b + 1)
                    v.scalar_tensor_tensor(dT[:, b, :], bank(b, 1), ve("out_b"), gT[:, b, :], ALU.add, ALU.mult).then_inc(s["d_out"], 1)
                    dve.wait_ge(s["d_out"], b + 1)
                    v.tensor_tensor(dT[:, b, :], dT[:, b, :], xT[:, b, :], ALU.add).then_inc(s["y_out"], 1)


def e_w1(wl, c, part):
    if c == E * RC:
        return wl("gate_w1", part)
    return wl("e_w1", (part * E + c // RC) * RC + c % RC)


def router_w(w_late, part):
    at = LATE_AT["router_W"] + part * E
    return w_late[:, at:at + E]


def last_round(steps, gather):
    _, kind, b, r = gather
    return max(s[3] for s in steps if s[0] == "values" and s[1] == (kind, b, 2 * r + 1))


def modulation(dve, v, s, aff, lnA, lnB, ps, ve, site, bias, g, bb, out_sem):
    for i in range(2):
        last = v.tensor_scalar(aff[:, site, i, :], ps[:, B * i:B * i + B], ve(bias, i), None, ALU.add)
    last.then_inc(s["mod_step"], 1)
    dve.wait_ge(s["mod_step"], 2 * site + 1)
    v.tensor_scalar(lnA[:, site, :], aff[:, site, 0, :], ve(g), None, ALU.mult)
    v.tensor_scalar(lnB[:, site, :], aff[:, site, 0, :], ve(bb), None, ALU.mult).then_inc(s["mod_step"], 1)
    dve.wait_ge(s["mod_step"], 2 * site + 2)
    v.tensor_tensor(lnB[:, site, :], lnB[:, site, :], aff[:, site, 1, :], ALU.add).then_inc(out_sem, 1)


def kernel(**inputs):
    import numpy as np
    import concourse.bacc as bacc
    from concourse.bass_utils import run_bass_kernel_spmd as run

    a = {k.replace("L0_xcond_", "").replace("L1_xcond_", ""): np.asarray(v) for k, v in inputs.items()}

    dense = np.arange(D).reshape(2, H // 2, DH).transpose(0, 2, 1).reshape(-1)
    for k in ("sa_q", "sa_k", "ca_q", "ca_k"):
        a[k + "w"], a[k + "b"] = a[k + "w"][:, dense], a[k + "b"][dense]
    order = np.array([8 * q + 2 * g + jj for g in range(GROUPS) for jj in range(2) for q in range(2)])
    order = (order[:, None] * DH + np.arange(DH)).reshape(-1)
    for k in ("sa", "ca"):
        a[k + "_vw"], a[k + "_vb"], a[k + "_ow"] = a[k + "_vw"][:, order], a[k + "_vb"][order], a[k + "_ow"][order]

    def wide(w):
        n = w.shape[0] // P
        return w.reshape(n, P, -1).transpose(1, 0, 2).reshape(P, -1)

    vec = np.concatenate([(a["cond_1024"] if n == "cond" else a[n]).reshape(k, P).T for n, k in VECTORS], axis=1)
    late = dict(a, ctxT=a["ctx_1024"].reshape(B * LC, D).T, WqT=a["Wq"].T, ffn_w2=wide(a["ffn_w2"]),
                router_W=wide(a["router_W"]), gate_w1=wide(a["gate_w1"]),
                e_w1=a["e_w1"].reshape(E, 3, P, RH).transpose(2, 1, 0, 3).reshape(P, -1),
                e_w2=wide(a["e_w2"].reshape(E * RH, D)))
    feeds = {
        "x_nat": a["x"].reshape(B * QT, P, D).transpose(1, 0, 2),
        "x_T": a["x"].transpose(2, 0, 1),
        "early": np.concatenate([vec if n == "vec" else a[n] for n, _ in EARLY], axis=1),
        "late": np.concatenate([late[n] for n, _ in LATE], axis=1),
        "router_b": a["router_b"].reshape(1, E),
        "e_b2": a["e_b2"],
    }
    feeds = {k: np.ascontiguousarray(v) for k, v in feeds.items()}
    nc = bacc.Bacc("TRN2", target_bir_lowering=False, num_devices=1)
    args = [nc.dram_tensor(k, v.shape, mybir.dt.from_np(v.dtype), kind="ExternalInput").ap() for k, v in feeds.items()]
    out = nc.dram_tensor("out_T", (B, D, L), F32, kind="ExternalOutput").ap()
    block_program(nc, *args, out)
    got = run(nc, [feeds], core_ids=[0]).results[0]["out_T"]
    return np.ascontiguousarray(got.transpose(0, 2, 1))
```
